# Optimizing a Trainium2 kernel written in Bass

```python
import numpy as np
import jax
import jax.numpy as jnp

def _softmax(x, axis=-1):
    return jax.nn.softmax(x, axis=axis)

def _gelu(x):
    return jax.nn.gelu(x, approximate=True)

def _silu(x):
    return jax.nn.silu(x)

def _sigmoid(x):
    return jax.nn.sigmoid(x)

def _layernorm(x, axis=-1, eps=1e-05):
    m = jnp.mean(x, axis=axis, keepdims=True)
    v = jnp.var(x, axis=axis, keepdims=True)
    return (x - m) / jnp.sqrt(v + eps)

def _scatter_add(tgt, idx, src, axis=0):
    return tgt.at[idx].add(src)

def _segment_sum(src, seg, n):
    return jax.ops.segment_sum(src, seg, n)
kernel_name = 'mk_lm_tower_d4_tok_ids1024_r4_bbac9d'

def setup_inputs(seed: int=0):
    np.random.seed(seed)
    _w = jnp.asarray

    def _rec_inputs():
        import jax
        import jax.numpy as jnp
        _rk = jax.random.key(seed)
        x = jax.random.randint(jax.random.fold_in(_rk, 1), (8, 256), 0, 12564, jnp.int32)
        return x
    x = _rec_inputs()

    def _L0_tok_setup():
        import jax, jax.numpy as jnp
        import numpy as np
        VOCAB = 50257
        DIM = 256
        BLOCK_SIZE = 32
        QMAX = 31.0

        def fake_quantize(x, block_size=BLOCK_SIZE):
            shape = x.shape
            xb = x.reshape(shape[:-1] + (shape[-1] // block_size, block_size))
            amax = jnp.max(jnp.abs(xb), axis=-1, keepdims=True)
            scale = amax / QMAX
            safe_scale = jnp.where(scale > 0, scale, 1.0)
            q = jnp.clip(jnp.round(xb / safe_scale), -QMAX, QMAX)
            deq = jnp.where(scale > 0, q * scale, 0.0)
            return deq.reshape(shape)
        key = jax.random.key(seed)
        k1, k2 = jax.random.split(key)
        input_ids = jax.random.randint(k1, (16, 1024), 0, VOCAB, dtype=jnp.int64)
        weight = jax.random.normal(k2, (VOCAB, DIM), dtype=jnp.float32)
        return {'input': input_ids, 'weight': weight}
    _L0_tok_all = _L0_tok_setup()
    _L0_tok_in = {k: v for k, v in _L0_tok_all.items() if k in ('weight',)}
    del _L0_tok_all

    def _L0_attn_setup():
        import jax, jax.numpy as jnp
        import numpy as np
        LN_EPS = 1e-05
        WKV_EPS = 1e-08

        def _layernorm(x, g, b):
            mu = jnp.mean(x, axis=-1, keepdims=True)
            var = jnp.mean((x - mu) ** 2, axis=-1, keepdims=True)
            return (x - mu) * jax.lax.rsqrt(var + LN_EPS) * g + b

        def _time_mix(xn, Wr, Ww, Wk, Wv, Wo, time_decay):
            r = jax.nn.sigmoid(jnp.einsum('bsd,ed->bse', xn, Wr))
            w = -jnp.exp(jnp.einsum('bsd,ed->bse', xn, Ww))
            k = jnp.einsum('bsd,ed->bse', xn, Wk)
            v = jnp.einsum('bsd,ed->bse', xn, Wv)
            ewk = jnp.exp(w + k)
            decay = jnp.exp(time_decay)

            def step(carry, inp):
                num, den = carry
                e, vt = inp
                num = decay * num + e * vt
                den = decay * den + e
                wkv = num / (den + WKV_EPS)
                return ((num, den), wkv)
            B, S, D = xn.shape
            init = (jnp.zeros((B, D), xn.dtype), jnp.zeros((B, D), xn.dtype))
            (num_f, den_f), wkv = jax.lax.scan(step, init, (jnp.swapaxes(ewk, 0, 1), jnp.swapaxes(v, 0, 1)))
            wkv = jnp.swapaxes(wkv, 0, 1)
            out = jnp.einsum('bsd,ed->bse', r * wkv, Wo)
            final_state = jnp.stack([num_f, den_f], axis=1)
            return (out, final_state)

        def _channel_mix(xn, Wkey, Wval, Wrec):
            k = jnp.einsum('bsd,fd->bsf', xn, Wkey)
            k = jnp.square(jax.nn.relu(k))
            v = jnp.einsum('bsf,df->bsd', k, Wval)
            r = jax.nn.sigmoid(jnp.einsum('bsd,ed->bse', xn, Wrec))
            return r * v

        def _reference_tuple_inner(x, ln1_g, ln1_b, ln2_g, ln2_b, Wr, Ww, Wk, Wv, Wo, time_decay, time_first, Wkey, Wval, Wrec):
            tm, new_state = _time_mix(_layernorm(x, ln1_g, ln1_b), Wr, Ww, Wk, Wv, Wo, time_decay)
            x = x + tm
            x = x + _channel_mix(_layernorm(x, ln2_g, ln2_b), Wkey, Wval, Wrec)
            return (x, new_state)
        key = jax.random.key(seed)
        ks = jax.random.split(key, 16)
        B, S, D, F = (4, 512, 256, 1024)
        xavier_d = float(np.sqrt(6.0 / (D + D)))
        xavier_df = float(np.sqrt(6.0 / (D + F)))
        u = lambda k, sh, s: jax.random.uniform(k, sh, jnp.float32, -s, s)
        return {'x': jax.random.normal(ks[0], (B, S, D), jnp.float32), 'ln1_g': jnp.ones((D,), jnp.float32), 'ln1_b': jnp.zeros((D,), jnp.float32), 'ln2_g': jnp.ones((D,), jnp.float32), 'ln2_b': jnp.zeros((D,), jnp.float32), 'Wr': u(ks[1], (D, D), xavier_d), 'Ww': u(ks[2], (D, D), xavier_d), 'Wk': u(ks[3], (D, D), xavier_d), 'Wv': u(ks[4], (D, D), xavier_d), 'Wo': u(ks[5], (D, D), xavier_d), 'time_decay': jax.random.uniform(ks[6], (D,), jnp.float32, -1.0, 0.0), 'time_first': jax.random.uniform(ks[7], (D,), jnp.float32, -1.0, 1.0), 'Wkey': u(ks[8], (F, D), xavier_df), 'Wval': u(ks[9], (D, F), xavier_df), 'Wrec': u(ks[10], (D, D), xavier_d)}
    _L0_attn_all = _L0_attn_setup()
    _L0_attn_in = {k: v for k, v in _L0_attn_all.items() if k in ('ln1_g', 'ln1_b', 'ln2_g', 'ln2_b', 'Wr', 'Ww', 'Wk', 'Wv', 'Wo', 'time_decay', 'time_first', 'Wkey', 'Wval', 'Wrec')}
    del _L0_attn_all

    def _L0_ffn_setup():
        import jax, jax.numpy as jnp
        import numpy as np
        NUM_EXPERTS = 8
        TOP_K = 2
        ROUTE_SCALE = 1.0
        DIM = 256
        HID = 256
        B, S = (2, 1024)
        key = jax.random.key(seed)
        ks = jax.random.split(key, 9)
        sc = 0.05
        return {'x': jax.random.normal(ks[0], (B, S, DIM), dtype=jnp.float32), 'gate_w': jax.random.normal(ks[1], (NUM_EXPERTS, DIM), dtype=jnp.float32) * sc, 'w1': jax.random.normal(ks[2], (NUM_EXPERTS, HID, DIM), dtype=jnp.float32) * sc, 'w2': jax.random.normal(ks[3], (NUM_EXPERTS, DIM, HID), dtype=jnp.float32) * sc, 'w3': jax.random.normal(ks[4], (NUM_EXPERTS, HID, DIM), dtype=jnp.float32) * sc, 'sw1': jax.random.normal(ks[5], (HID, DIM), dtype=jnp.float32) * sc, 'sw2': jax.random.normal(ks[6], (DIM, HID), dtype=jnp.float32) * sc, 'sw3': jax.random.normal(ks[7], (HID, DIM), dtype=jnp.float32) * sc, 'expert_bias': jnp.zeros((NUM_EXPERTS,), dtype=jnp.float32)}
    _L0_ffn_all = _L0_ffn_setup()
    _L0_ffn_in = {k: v for k, v in _L0_ffn_all.items() if k in ('gate_w', 'w1', 'w2', 'w3', 'sw1', 'sw2', 'sw3', 'expert_bias')}
    del _L0_ffn_all

    def _L1_attn_setup():
        import jax, jax.numpy as jnp
        import numpy as np
        N_HEAD = 16
        LATENT = 32

        def _rotate_half(x):
            xe = x[..., ::2]
            xo = x[..., 1::2]
            return jnp.stack((-xo, xe), axis=-1).reshape(x.shape)

        def _rope_tables(T, latent_dim, dtype):
            inv_freq = 1.0 / 10000.0 ** (jnp.arange(0, latent_dim, 2, dtype=jnp.float32) / latent_dim)
            t = jnp.arange(T, dtype=jnp.float32)
            freqs = jnp.outer(t, inv_freq)
            cos = jnp.repeat(jnp.cos(freqs), 2, axis=-1)[:, :latent_dim]
            sin = jnp.repeat(jnp.sin(freqs), 2, axis=-1)[:, :latent_dim]
            return (cos.astype(dtype), sin.astype(dtype))
        key = jax.random.key(seed)
        ks = jax.random.split(key, 14)
        C = 256
        hd = C // N_HEAD
        L = LATENT
        s = 0.02
        return {'x': jax.random.normal(ks[0], (4, 512, C), jnp.float32), 'c_attn_w': jax.random.normal(ks[1], (3 * C, C), jnp.float32) * s, 'c_attn_b': jnp.zeros((3 * C,), jnp.float32), 'q2l_w': jax.random.normal(ks[2], (L, hd), jnp.float32) * s, 'q2l_b': jnp.zeros((L,), jnp.float32), 'kv2l_w': jax.random.normal(ks[3], (L, hd), jnp.float32) * s, 'kv2l_b': jnp.zeros((L,), jnp.float32), 'l2o_w': jax.random.normal(ks[4], (hd, L), jnp.float32) * s, 'l2o_b': jnp.zeros((hd,), jnp.float32), 'wqk_w': jax.random.normal(ks[5], (L, L), jnp.float32) * s, 'wqk_b': jnp.zeros((L,), jnp.float32), 'cproj_w': jax.random.normal(ks[6], (C, C), jnp.float32) * s, 'cproj_b': jnp.zeros((C,), jnp.float32)}
    _L1_attn_all = _L1_attn_setup()
    _L1_attn_in = {k: v for k, v in _L1_attn_all.items() if k in ('c_attn_w', 'c_attn_b', 'q2l_w', 'q2l_b', 'kv2l_w', 'kv2l_b', 'l2o_w', 'l2o_b', 'wqk_w', 'wqk_b', 'cproj_w', 'cproj_b')}
    del _L1_attn_all

    def _L1_ffn_setup():
        import jax, jax.numpy as jnp
        import numpy as np
        D, H, E, K = (256, 256, 8, 2)

        def _moe(x, router_w, w_in, b_in, w_out, b_out):
            B, S, Dm = x.shape
            T = B * S
            x2 = x.reshape(T, Dm)
            logits = x2 @ router_w
            probs = jax.nn.softmax(logits, axis=-1)
            top_p, top_e = jax.lax.top_k(probs, K)
            flat_e = top_e.reshape(-1)
            flat_p = top_p.reshape(-1)
            tok = jnp.repeat(jnp.arange(T), K)
            order = jnp.argsort(flat_e)
            se, sp, st = (flat_e[order], flat_p[order], tok[order])
            xd = x2[st]
            N = xd.shape[0]
            h = jnp.zeros((N, H), x.dtype)
            for e in range(E):
                m = (se == e)[:, None]
                h = h + jnp.where(m, jax.nn.gelu(xd @ w_in[e] + b_in[e]), 0.0)
            y = jnp.zeros((N, Dm), x.dtype)
            for e in range(E):
                m = (se == e)[:, None]
                y = y + jnp.where(m, h @ w_out[e] + b_out[e], 0.0)
            y = y * sp[:, None]
            out = jnp.zeros((T, Dm), x.dtype).at[st].add(y)
            return out.reshape(B, S, Dm)
        key = jax.random.key(seed)
        ks = jax.random.split(key, 5)
        s = lambda k, shape, scale: jax.random.normal(k, shape, dtype=jnp.float32) * scale
        return {'input_batch': s(ks[0], (2, 128, D), 1.0), 'router_w': s(ks[1], (D, E), D ** (-0.5)), 'w_in': s(ks[2], (E, D, H), D ** (-0.5)), 'b_in': jnp.zeros((E, H), jnp.float32), 'w_out': s(ks[3], (E, H, D), H ** (-0.5)), 'b_out': jnp.zeros((E, D), jnp.float32)}
    _L1_ffn_all = _L1_ffn_setup()
    _L1_ffn_in = {k: v for k, v in _L1_ffn_all.items() if k in ('router_w', 'w_in', 'b_in', 'w_out', 'b_out')}
    del _L1_ffn_all

    def _L2_attn_setup():
        import math
        import jax, jax.numpy as jnp
        import numpy as np
        D_MODEL = 256
        NHEAD = 16
        DK = D_MODEL // NHEAD
        FACTOR = 5
        B, L = (4, 2048)
        U = max(1, min(FACTOR * math.ceil(math.log(L + 1)), L))
        key = jax.random.key(seed)
        ks = jax.random.split(key, 10)
        s = 1.0 / math.sqrt(D_MODEL)
        inp = {'x': jax.random.normal(ks[0], (B, L, D_MODEL), dtype=jnp.float32), 'Wq': jax.random.normal(ks[1], (D_MODEL, D_MODEL), dtype=jnp.float32) * s, 'bq': jnp.zeros((D_MODEL,), dtype=jnp.float32), 'Wk': jax.random.normal(ks[2], (D_MODEL, D_MODEL), dtype=jnp.float32) * s, 'bk': jnp.zeros((D_MODEL,), dtype=jnp.float32), 'Wv': jax.random.normal(ks[3], (D_MODEL, D_MODEL), dtype=jnp.float32) * s, 'bv': jnp.zeros((D_MODEL,), dtype=jnp.float32), 'Wo': jax.random.normal(ks[4], (D_MODEL, D_MODEL), dtype=jnp.float32) * s, 'bo': jnp.zeros((D_MODEL,), dtype=jnp.float32), 'idx_k': jax.random.permutation(ks[5], L)[:U].astype(jnp.int32)}
        return inp
    _L2_attn_all = _L2_attn_setup()
    _L2_attn_in = {k: v for k, v in _L2_attn_all.items() if k in ('Wq', 'bq', 'Wk', 'bk', 'Wv', 'bv', 'Wo', 'bo', 'idx_k')}
    del _L2_attn_all

    def _L2_ffn_setup():
        import jax, jax.numpy as jnp
        import numpy as np
        TOP_K = 2
        CAP_FACTOR = 1.25
        MIN_CAPACITY = 4
        key = jax.random.key(seed)
        k1, k2, k3, k4 = jax.random.split(key, 4)
        B, T, C, E = (8, 512, 256, 8)
        x = jax.random.normal(k1, (B, T, C), dtype=jnp.float32)
        w_g = jax.random.normal(k2, (E, C), dtype=jnp.float32) * 0.02
        c_fc = jax.random.normal(k3, (E, C, 4 * C), dtype=jnp.float32) * 0.02
        c_proj = jax.random.normal(k4, (E, 4 * C, C), dtype=jnp.float32) * 0.02
        return {'x': x, 'w_g': w_g, 'c_fc': c_fc, 'c_proj': c_proj}
    _L2_ffn_all = _L2_ffn_setup()
    _L2_ffn_in = {k: v for k, v in _L2_ffn_all.items() if k in ('w_g', 'c_fc', 'c_proj')}
    del _L2_ffn_all

    def _L3_attn_setup():
        import jax, jax.numpy as jnp
        import numpy as np
        EMBED_DIM = 256
        NUM_HEADS = 16
        HEAD_DIM = EMBED_DIM // NUM_HEADS
        NUM_DECAYS = 2
        BATCH = 2
        SEQ = 512
        W_SCALE = 0.02
        key = jax.random.key(seed)
        ks = jax.random.split(key, 12)
        d = EMBED_DIM
        inp = {'x': jax.random.normal(ks[0], (BATCH, SEQ, d), dtype=jnp.float32), 'Wq': jax.random.normal(ks[1], (d, d), dtype=jnp.float32) * W_SCALE, 'bq': jnp.zeros((d,), dtype=jnp.float32), 'Wk': jax.random.normal(ks[2], (d, d), dtype=jnp.float32) * W_SCALE, 'bk': jnp.zeros((d,), dtype=jnp.float32), 'Wv': jax.random.normal(ks[3], (d, d), dtype=jnp.float32) * W_SCALE, 'bv': jnp.zeros((d,), dtype=jnp.float32), 'Wo': jax.random.normal(ks[4], (d, d), dtype=jnp.float32) * W_SCALE, 'bo': jnp.zeros((d,), dtype=jnp.float32), 'decay_params': jax.random.uniform(ks[5], (NUM_HEADS, NUM_DECAYS), dtype=jnp.float32), 'mix_weights': jax.random.normal(ks[6], (NUM_HEADS, NUM_DECAYS), dtype=jnp.float32)}
        return inp
    _L3_attn_all = _L3_attn_setup()
    _L3_attn_in = {k: v for k, v in _L3_attn_all.items() if k in ('Wq', 'bq', 'Wk', 'bk', 'Wv', 'bv', 'Wo', 'bo', 'decay_params', 'mix_weights')}
    del _L3_attn_all

    def _L3_ffn_setup():
        import jax, jax.numpy as jnp
        import numpy as np
        HIDDEN = 256
        INNER = 1024

        def _weight_quant(w):
            scale = 1.0 / jnp.clip(jnp.mean(jnp.abs(w)), 1e-05)
            wq = jnp.clip(jnp.round(w * scale), -1.0, 1.0) / scale
            return w + jax.lax.stop_gradient(wq - w)

        def _act_quant(x):
            scale = 127.0 / jnp.clip(jnp.max(jnp.abs(x), axis=-1, keepdims=True), 1e-05)
            xq = jnp.clip(jnp.round(x * scale), -128.0, 127.0) / scale
            return x + jax.lax.stop_gradient(xq - x)

        def _bitlinear(x, w):
            return jnp.einsum('bsi,oi->bso', _act_quant(x), _weight_quant(w))
        key = jax.random.key(seed)
        k0, k1, k2, k3 = jax.random.split(key, 4)
        x = jax.random.normal(k0, (4, 512, HIDDEN), dtype=jnp.float32)
        w_gate = jax.random.normal(k1, (INNER, HIDDEN), dtype=jnp.float32) / np.sqrt(HIDDEN)
        w_up = jax.random.normal(k2, (INNER, HIDDEN), dtype=jnp.float32) / np.sqrt(HIDDEN)
        w_down = jax.random.normal(k3, (HIDDEN, INNER), dtype=jnp.float32) / np.sqrt(INNER)
        return {'x': x, 'w_gate': w_gate, 'w_up': w_up, 'w_down': w_down}
    _L3_ffn_all = _L3_ffn_setup()
    _L3_ffn_in = {k: v for k, v in _L3_ffn_all.items() if k in ('w_gate', 'w_up', 'w_down')}
    del _L3_ffn_all
    return {'x': x, 'L0_tok_weight': _L0_tok_in['weight'], 'L0_attn_ln1_g': _L0_attn_in['ln1_g'], 'L0_attn_ln1_b': _L0_attn_in['ln1_b'], 'L0_attn_ln2_g': _L0_attn_in['ln2_g'], 'L0_attn_ln2_b': _L0_attn_in['ln2_b'], 'L0_attn_Wr': _L0_attn_in['Wr'], 'L0_attn_Ww': _L0_attn_in['Ww'], 'L0_attn_Wk': _L0_attn_in['Wk'], 'L0_attn_Wv': _L0_attn_in['Wv'], 'L0_attn_Wo': _L0_attn_in['Wo'], 'L0_attn_time_decay': _L0_attn_in['time_decay'], 'L0_attn_time_first': _L0_attn_in['time_first'], 'L0_attn_Wkey': _L0_attn_in['Wkey'], 'L0_attn_Wval': _L0_attn_in['Wval'], 'L0_attn_Wrec': _L0_attn_in['Wrec'], 'L0_ffn_gate_w': _L0_ffn_in['gate_w'], 'L0_ffn_w1': _L0_ffn_in['w1'], 'L0_ffn_w2': _L0_ffn_in['w2'], 'L0_ffn_w3': _L0_ffn_in['w3'], 'L0_ffn_sw1': _L0_ffn_in['sw1'], 'L0_ffn_sw2': _L0_ffn_in['sw2'], 'L0_ffn_sw3': _L0_ffn_in['sw3'], 'L0_ffn_expert_bias': _L0_ffn_in['expert_bias'], 'L1_attn_c_attn_w': _L1_attn_in['c_attn_w'], 'L1_attn_c_attn_b': _L1_attn_in['c_attn_b'], 'L1_attn_q2l_w': _L1_attn_in['q2l_w'], 'L1_attn_q2l_b': _L1_attn_in['q2l_b'], 'L1_attn_kv2l_w': _L1_attn_in['kv2l_w'], 'L1_attn_kv2l_b': _L1_attn_in['kv2l_b'], 'L1_attn_l2o_w': _L1_attn_in['l2o_w'], 'L1_attn_l2o_b': _L1_attn_in['l2o_b'], 'L1_attn_wqk_w': _L1_attn_in['wqk_w'], 'L1_attn_wqk_b': _L1_attn_in['wqk_b'], 'L1_attn_cproj_w': _L1_attn_in['cproj_w'], 'L1_attn_cproj_b': _L1_attn_in['cproj_b'], 'L1_ffn_router_w': _L1_ffn_in['router_w'], 'L1_ffn_w_in': _L1_ffn_in['w_in'], 'L1_ffn_b_in': _L1_ffn_in['b_in'], 'L1_ffn_w_out': _L1_ffn_in['w_out'], 'L1_ffn_b_out': _L1_ffn_in['b_out'], 'L2_attn_Wq': _L2_attn_in['Wq'], 'L2_attn_bq': _L2_attn_in['bq'], 'L2_attn_Wk': _L2_attn_in['Wk'], 'L2_attn_bk': _L2_attn_in['bk'], 'L2_attn_Wv': _L2_attn_in['Wv'], 'L2_attn_bv': _L2_attn_in['bv'], 'L2_attn_Wo': _L2_attn_in['Wo'], 'L2_attn_bo': _L2_attn_in['bo'], 'L2_attn_idx_k': _L2_attn_in['idx_k'], 'L2_ffn_w_g': _L2_ffn_in['w_g'], 'L2_ffn_c_fc': _L2_ffn_in['c_fc'], 'L2_ffn_c_proj': _L2_ffn_in['c_proj'], 'L3_attn_Wq': _L3_attn_in['Wq'], 'L3_attn_bq': _L3_attn_in['bq'], 'L3_attn_Wk': _L3_attn_in['Wk'], 'L3_attn_bk': _L3_attn_in['bk'], 'L3_attn_Wv': _L3_attn_in['Wv'], 'L3_attn_bv': _L3_attn_in['bv'], 'L3_attn_Wo': _L3_attn_in['Wo'], 'L3_attn_bo': _L3_attn_in['bo'], 'L3_attn_decay_params': _L3_attn_in['decay_params'], 'L3_attn_mix_weights': _L3_attn_in['mix_weights'], 'L3_ffn_w_gate': _L3_ffn_in['w_gate'], 'L3_ffn_w_up': _L3_ffn_in['w_up'], 'L3_ffn_w_down': _L3_ffn_in['w_down']}

def reference(x, L0_tok_weight, L0_attn_ln1_g, L0_attn_ln1_b, L0_attn_ln2_g, L0_attn_ln2_b, L0_attn_Wr, L0_attn_Ww, L0_attn_Wk, L0_attn_Wv, L0_attn_Wo, L0_attn_time_decay, L0_attn_time_first, L0_attn_Wkey, L0_attn_Wval, L0_attn_Wrec, L0_ffn_gate_w, L0_ffn_w1, L0_ffn_w2, L0_ffn_w3, L0_ffn_sw1, L0_ffn_sw2, L0_ffn_sw3, L0_ffn_expert_bias, L1_attn_c_attn_w, L1_attn_c_attn_b, L1_attn_q2l_w, L1_attn_q2l_b, L1_attn_kv2l_w, L1_attn_kv2l_b, L1_attn_l2o_w, L1_attn_l2o_b, L1_attn_wqk_w, L1_attn_wqk_b, L1_attn_cproj_w, L1_attn_cproj_b, L1_ffn_router_w, L1_ffn_w_in, L1_ffn_b_in, L1_ffn_w_out, L1_ffn_b_out, L2_attn_Wq, L2_attn_bq, L2_attn_Wk, L2_attn_bk, L2_attn_Wv, L2_attn_bv, L2_attn_Wo, L2_attn_bo, L2_attn_idx_k, L2_ffn_w_g, L2_ffn_c_fc, L2_ffn_c_proj, L3_attn_Wq, L3_attn_bq, L3_attn_Wk, L3_attn_bk, L3_attn_Wv, L3_attn_bv, L3_attn_Wo, L3_attn_bo, L3_attn_decay_params, L3_attn_mix_weights, L3_ffn_w_gate, L3_ffn_w_up, L3_ffn_w_down):
    import jax
    import jax.numpy as jnp

    def _L0_tok_ref(input, weight):
        import jax, jax.numpy as jnp
        import numpy as np
        VOCAB = 50257
        DIM = 256
        BLOCK_SIZE = 32
        QMAX = 31.0

        def fake_quantize(x, block_size=BLOCK_SIZE):
            shape = x.shape
            xb = x.reshape(shape[:-1] + (shape[-1] // block_size, block_size))
            amax = jnp.max(jnp.abs(xb), axis=-1, keepdims=True)
            scale = amax / QMAX
            safe_scale = jnp.where(scale > 0, scale, 1.0)
            q = jnp.clip(jnp.round(xb / safe_scale), -QMAX, QMAX)
            deq = jnp.where(scale > 0, q * scale, 0.0)
            return deq.reshape(shape)
        raw = weight[input]
        return fake_quantize(raw, BLOCK_SIZE)

    def _L0_attn_ref(x, ln1_g, ln1_b, ln2_g, ln2_b, Wr, Ww, Wk, Wv, Wo, time_decay, time_first, Wkey, Wval, Wrec):
        import jax, jax.numpy as jnp
        import numpy as np
        LN_EPS = 1e-05
        WKV_EPS = 1e-08

        def _layernorm(x, g, b):
            mu = jnp.mean(x, axis=-1, keepdims=True)
            var = jnp.mean((x - mu) ** 2, axis=-1, keepdims=True)
            return (x - mu) * jax.lax.rsqrt(var + LN_EPS) * g + b

        def _time_mix(xn, Wr, Ww, Wk, Wv, Wo, time_decay):
            r = jax.nn.sigmoid(jnp.einsum('bsd,ed->bse', xn, Wr))
            w = -jnp.exp(jnp.einsum('bsd,ed->bse', xn, Ww))
            k = jnp.einsum('bsd,ed->bse', xn, Wk)
            v = jnp.einsum('bsd,ed->bse', xn, Wv)
            ewk = jnp.exp(w + k)
            decay = jnp.exp(time_decay)

            def step(carry, inp):
                num, den = carry
                e, vt = inp
                num = decay * num + e * vt
                den = decay * den + e
                wkv = num / (den + WKV_EPS)
                return ((num, den), wkv)
            B, S, D = xn.shape
            init = (jnp.zeros((B, D), xn.dtype), jnp.zeros((B, D), xn.dtype))
            (num_f, den_f), wkv = jax.lax.scan(step, init, (jnp.swapaxes(ewk, 0, 1), jnp.swapaxes(v, 0, 1)))
            wkv = jnp.swapaxes(wkv, 0, 1)
            out = jnp.einsum('bsd,ed->bse', r * wkv, Wo)
            final_state = jnp.stack([num_f, den_f], axis=1)
            return (out, final_state)

        def _channel_mix(xn, Wkey, Wval, Wrec):
            k = jnp.einsum('bsd,fd->bsf', xn, Wkey)
            k = jnp.square(jax.nn.relu(k))
            v = jnp.einsum('bsf,df->bsd', k, Wval)
            r = jax.nn.sigmoid(jnp.einsum('bsd,ed->bse', xn, Wrec))
            return r * v

        def _reference_tuple_inner(x, ln1_g, ln1_b, ln2_g, ln2_b, Wr, Ww, Wk, Wv, Wo, time_decay, time_first, Wkey, Wval, Wrec):
            tm, new_state = _time_mix(_layernorm(x, ln1_g, ln1_b), Wr, Ww, Wk, Wv, Wo, time_decay)
            x = x + tm
            x = x + _channel_mix(_layernorm(x, ln2_g, ln2_b), Wkey, Wval, Wrec)
            return (x, new_state)
        return _reference_tuple_inner(x, ln1_g, ln1_b, ln2_g, ln2_b, Wr, Ww, Wk, Wv, Wo, time_decay, time_first, Wkey, Wval, Wrec)[0]

    def _L0_ffn_ref(x, gate_w, w1, w2, w3, sw1, sw2, sw3, expert_bias):
        import jax, jax.numpy as jnp
        import numpy as np
        NUM_EXPERTS = 8
        TOP_K = 2
        ROUTE_SCALE = 1.0
        DIM = 256
        HID = 256
        B, S = (2, 1024)
        bs, slen, dim = x.shape
        xf = x.reshape(-1, dim)
        scores = jax.nn.sigmoid((xf @ gate_w.T).astype(jnp.float32))
        _, sel = jax.lax.top_k(scores + expert_bias[None, :], TOP_K)
        top_scores = jnp.take_along_axis(scores, sel, axis=1) * ROUTE_SCALE
        flat_sel = sel.reshape(-1)
        order = jnp.argsort(flat_sel, stable=True)
        scores_sorted = top_scores.reshape(-1)[order]
        tok_idx = order // TOP_K
        expert_ids = flat_sel[order]
        routed = xf[tok_idx]
        routed = (routed.astype(jnp.float32) * scores_sorted[:, None]).astype(x.dtype)
        out_r = jnp.zeros_like(routed)
        for e in range(NUM_EXPERTS):
            m = (expert_ids == e)[:, None]
            h = jax.nn.silu(routed @ w1[e].T) * (routed @ w3[e].T)
            out_r = out_r + jnp.where(m, h @ w2[e].T, jnp.zeros((), routed.dtype))
        shared = jax.nn.silu(xf @ sw1.T) * (xf @ sw3.T) @ sw2.T
        out_r = (out_r.astype(jnp.float32) * scores_sorted[:, None]).astype(x.dtype)
        out = shared.at[tok_idx].add(out_r)
        return out.reshape(bs, slen, dim)

    def _L1_attn_ref(x, c_attn_w, c_attn_b, q2l_w, q2l_b, kv2l_w, kv2l_b, l2o_w, l2o_b, wqk_w, wqk_b, cproj_w, cproj_b):
        import jax, jax.numpy as jnp
        import numpy as np
        N_HEAD = 16
        LATENT = 32

        def _rotate_half(x):
            xe = x[..., ::2]
            xo = x[..., 1::2]
            return jnp.stack((-xo, xe), axis=-1).reshape(x.shape)

        def _rope_tables(T, latent_dim, dtype):
            inv_freq = 1.0 / 10000.0 ** (jnp.arange(0, latent_dim, 2, dtype=jnp.float32) / latent_dim)
            t = jnp.arange(T, dtype=jnp.float32)
            freqs = jnp.outer(t, inv_freq)
            cos = jnp.repeat(jnp.cos(freqs), 2, axis=-1)[:, :latent_dim]
            sin = jnp.repeat(jnp.sin(freqs), 2, axis=-1)[:, :latent_dim]
            return (cos.astype(dtype), sin.astype(dtype))
        B, T, C = x.shape
        H = N_HEAD
        hd = C // H
        L = q2l_w.shape[0]
        qkv = x @ c_attn_w.T + c_attn_b
        q, k, v = jnp.split(qkv, 3, axis=2)

        def heads(t):
            return t.reshape(B, T, H, hd).transpose(0, 2, 1, 3)
        q, k, v = (heads(q), heads(k), heads(v))
        q_lat = q @ q2l_w.T + q2l_b
        k_lat = k @ kv2l_w.T + kv2l_b
        v_lat = v @ kv2l_w.T + kv2l_b
        cos, sin = _rope_tables(T, L, x.dtype)
        cos = cos[None, None]
        sin = sin[None, None]
        q_lat = q_lat * cos + _rotate_half(q_lat) * sin
        k_lat = k_lat * cos + _rotate_half(k_lat) * sin
        q_for_k = q_lat @ wqk_w.T + wqk_b
        att = jnp.einsum('bhql,bhkl->bhqk', q_for_k, k_lat) * L ** (-0.5)
        causal = jnp.tril(jnp.ones((T, T), dtype=bool))
        att = jnp.where(causal[None, None], att, -jnp.inf)
        att = jax.nn.softmax(att, axis=-1)
        y_lat = jnp.einsum('bhqk,bhkl->bhql', att, v_lat)
        y = y_lat @ l2o_w.T + l2o_b
        y = y.transpose(0, 2, 1, 3).reshape(B, T, C)
        return y @ cproj_w.T + cproj_b

    def _L1_ffn_ref(input_batch, router_w, w_in, b_in, w_out, b_out):
        import jax, jax.numpy as jnp
        import numpy as np
        D, H, E, K = (256, 256, 8, 2)

        def _moe(x, router_w, w_in, b_in, w_out, b_out):
            B, S, Dm = x.shape
            T = B * S
            x2 = x.reshape(T, Dm)
            logits = x2 @ router_w
            probs = jax.nn.softmax(logits, axis=-1)
            top_p, top_e = jax.lax.top_k(probs, K)
            flat_e = top_e.reshape(-1)
            flat_p = top_p.reshape(-1)
            tok = jnp.repeat(jnp.arange(T), K)
            order = jnp.argsort(flat_e)
            se, sp, st = (flat_e[order], flat_p[order], tok[order])
            xd = x2[st]
            N = xd.shape[0]
            h = jnp.zeros((N, H), x.dtype)
            for e in range(E):
                m = (se == e)[:, None]
                h = h + jnp.where(m, jax.nn.gelu(xd @ w_in[e] + b_in[e]), 0.0)
            y = jnp.zeros((N, Dm), x.dtype)
            for e in range(E):
                m = (se == e)[:, None]
                y = y + jnp.where(m, h @ w_out[e] + b_out[e], 0.0)
            y = y * sp[:, None]
            out = jnp.zeros((T, Dm), x.dtype).at[st].add(y)
            return out.reshape(B, S, Dm)
        return _moe(input_batch, router_w, w_in, b_in, w_out, b_out)

    def _L2_attn_ref(x, Wq, bq, Wk, bk, Wv, bv, Wo, bo, idx_k):
        import math
        import jax, jax.numpy as jnp
        import numpy as np
        D_MODEL = 256
        NHEAD = 16
        DK = D_MODEL // NHEAD
        FACTOR = 5
        B, L = (4, 2048)
        U = max(1, min(FACTOR * math.ceil(math.log(L + 1)), L))
        Bv, Lv, _ = x.shape
        H, dk = (NHEAD, DK)
        u = idx_k.shape[0]
        scale = 1.0 / math.sqrt(dk)
        Q = (x @ Wq.T + bq).reshape(Bv, Lv, H, dk).transpose(0, 2, 1, 3)
        K = (x @ Wk.T + bk).reshape(Bv, Lv, H, dk).transpose(0, 2, 1, 3)
        V = (x @ Wv.T + bv).reshape(Bv, Lv, H, dk).transpose(0, 2, 1, 3)
        K_samp = K[:, :, idx_k, :]
        scores = jnp.einsum('bhld,bhud->bhlu', Q, K_samp) * scale
        M = scores.max(-1) - scores.mean(-1)
        _, top_idx = jax.lax.top_k(M, u)
        Q_top = jnp.take_along_axis(Q, top_idx[..., None], axis=2)
        attn = jax.nn.softmax(jnp.einsum('bhud,bhld->bhul', Q_top, K) * scale, axis=-1)
        ctx_top = jnp.einsum('bhul,bhld->bhud', attn, V)
        ctx = jnp.broadcast_to(V.mean(axis=2, keepdims=True), (Bv, H, Lv, dk))
        bidx = jnp.arange(Bv)[:, None, None]
        hidx = jnp.arange(H)[None, :, None]
        ctx = ctx.at[bidx, hidx, top_idx].set(ctx_top)
        ctx = ctx.transpose(0, 2, 1, 3).reshape(Bv, Lv, H * dk)
        return ctx @ Wo.T + bo

    def _L2_ffn_ref(x, w_g, c_fc, c_proj):
        import jax, jax.numpy as jnp
        import numpy as np
        TOP_K = 2
        CAP_FACTOR = 1.25
        MIN_CAPACITY = 4
        B, T, C = x.shape
        E = w_g.shape[0]
        N = B * T
        capacity = max(MIN_CAPACITY, int(CAP_FACTOR * N * TOP_K / E))
        xf = x.reshape(N, C)
        logits = xf @ w_g.T
        top_logits, top_idx = jax.lax.top_k(logits, TOP_K)
        router_probs = jax.nn.softmax(top_logits, axis=-1)
        oh = jax.nn.one_hot(top_idx, E, dtype=jnp.int32)
        oh_t = oh.transpose(1, 0, 2).reshape(TOP_K * N, E)
        pos = jnp.cumsum(oh_t, axis=0).reshape(TOP_K, N, E).transpose(1, 0, 2)
        rank = jnp.sum((pos - 1) * oh, axis=-1)
        valid = rank < capacity
        probs_masked = router_probs * valid.astype(router_probs.dtype)
        rank_c = jnp.clip(rank, 0, capacity - 1)
        contrib = xf[:, None, :] * valid[..., None].astype(xf.dtype)
        buf = jnp.zeros((E, capacity, C), dtype=xf.dtype).at[top_idx, rank_c].add(contrib)
        h = jnp.einsum('ecd,edf->ecf', buf, c_fc)
        h = jnp.square(jax.nn.relu(h))
        expert_out = jnp.einsum('ecf,efd->ecd', h, c_proj)
        gathered = expert_out[top_idx, rank_c]
        out = jnp.sum(gathered * probs_masked[..., None], axis=1)
        return out.reshape(B, T, C)

    def _L3_attn_ref(x, Wq, bq, Wk, bk, Wv, bv, Wo, bo, decay_params, mix_weights):
        import jax, jax.numpy as jnp
        import numpy as np
        EMBED_DIM = 256
        NUM_HEADS = 16
        HEAD_DIM = EMBED_DIM // NUM_HEADS
        NUM_DECAYS = 2
        BATCH = 2
        SEQ = 512
        W_SCALE = 0.02
        B, S, _ = x.shape
        H, D = (NUM_HEADS, HEAD_DIM)

        def proj(W, b):
            return (jnp.einsum('bse,fe->bsf', x, W) + b).reshape(B, S, H, D).transpose(0, 2, 1, 3)
        q = proj(Wq, bq)
        k = proj(Wk, bk)
        v = proj(Wv, bv)
        attn_scores = jnp.einsum('bhqd,bhkd->bhqk', q, k) / jnp.sqrt(jnp.float32(D))
        t = jnp.arange(S, dtype=jnp.float32)
        time_diffs = jnp.abs(t[:, None] - t[None, :])
        dp = jnp.clip(decay_params, 0.01, 0.9999)
        decay_masks = dp[:, :, None, None] ** time_diffs[None, None, :, :]
        mix = jax.nn.softmax(mix_weights, axis=-1)
        decay_mask = jnp.einsum('hnqk,hn->hqk', decay_masks, mix)
        attn_scores = attn_scores * decay_mask[None]
        attn_probs = jax.nn.softmax(attn_scores, axis=-1)
        out = jnp.einsum('bhqk,bhkd->bhqd', attn_probs, v)
        out = out.transpose(0, 2, 1, 3).reshape(B, S, H * D)
        return jnp.einsum('bse,fe->bsf', out, Wo) + bo

    def _L3_ffn_ref(x, w_gate, w_up, w_down):
        import jax, jax.numpy as jnp
        import numpy as np
        HIDDEN = 256
        INNER = 1024

        def _weight_quant(w):
            scale = 1.0 / jnp.clip(jnp.mean(jnp.abs(w)), 1e-05)
            wq = jnp.clip(jnp.round(w * scale), -1.0, 1.0) / scale
            return w + jax.lax.stop_gradient(wq - w)

        def _act_quant(x):
            scale = 127.0 / jnp.clip(jnp.max(jnp.abs(x), axis=-1, keepdims=True), 1e-05)
            xq = jnp.clip(jnp.round(x * scale), -128.0, 127.0) / scale
            return x + jax.lax.stop_gradient(xq - x)

        def _bitlinear(x, w):
            return jnp.einsum('bsi,oi->bso', _act_quant(x), _weight_quant(w))
        gate = jax.nn.silu(_bitlinear(x, w_gate))
        up = _bitlinear(x, w_up)
        return _bitlinear(gate * up, w_down)
    h = _L0_tok_ref(x, L0_tok_weight)
    h = h + _L0_attn_ref(_layernorm(h, axis=-1), L0_attn_ln1_g, L0_attn_ln1_b, L0_attn_ln2_g, L0_attn_ln2_b, L0_attn_Wr, L0_attn_Ww, L0_attn_Wk, L0_attn_Wv, L0_attn_Wo, L0_attn_time_decay, L0_attn_time_first, L0_attn_Wkey, L0_attn_Wval, L0_attn_Wrec)
    h = h + _L0_ffn_ref(_layernorm(h, axis=-1), L0_ffn_gate_w, L0_ffn_w1, L0_ffn_w2, L0_ffn_w3, L0_ffn_sw1, L0_ffn_sw2, L0_ffn_sw3, L0_ffn_expert_bias)
    h = h + _L1_attn_ref(_layernorm(h, axis=-1), L1_attn_c_attn_w, L1_attn_c_attn_b, L1_attn_q2l_w, L1_attn_q2l_b, L1_attn_kv2l_w, L1_attn_kv2l_b, L1_attn_l2o_w, L1_attn_l2o_b, L1_attn_wqk_w, L1_attn_wqk_b, L1_attn_cproj_w, L1_attn_cproj_b)
    h = h + _L1_ffn_ref(_layernorm(h, axis=-1), L1_ffn_router_w, L1_ffn_w_in, L1_ffn_b_in, L1_ffn_w_out, L1_ffn_b_out)
    h = h + _L2_attn_ref(_layernorm(h, axis=-1), L2_attn_Wq, L2_attn_bq, L2_attn_Wk, L2_attn_bk, L2_attn_Wv, L2_attn_bv, L2_attn_Wo, L2_attn_bo, L2_attn_idx_k)
    h = h + _L2_ffn_ref(_layernorm(h, axis=-1), L2_ffn_w_g, L2_ffn_c_fc, L2_ffn_c_proj)
    h = h + _L3_attn_ref(_layernorm(h, axis=-1), L3_attn_Wq, L3_attn_bq, L3_attn_Wk, L3_attn_bk, L3_attn_Wv, L3_attn_bv, L3_attn_Wo, L3_attn_bo, L3_attn_decay_params, L3_attn_mix_weights)
    h = h + _L3_ffn_ref(_layernorm(h, axis=-1), L3_ffn_w_gate, L3_ffn_w_up, L3_ffn_w_down)
    return h

_drawn_inputs = setup_inputs


def setup_inputs(seed=0):
    import zlib

    import numpy as np

    out = dict(_drawn_inputs(seed))
    spreads = {'L0_attn_ln1_g': (1.0, 0.2),
     'L0_attn_ln1_b': (0.0, 0.1),
     'L0_attn_ln2_g': (1.0, 0.2),
     'L0_attn_ln2_b': (0.0, 0.297),
     'L0_ffn_expert_bias': (0.0, 0.1),
     'L1_attn_c_attn_b': (0.0, 0.8),
     'L1_attn_q2l_b': (0.0, 0.8),
     'L1_attn_kv2l_b': (0.0, 0.8),
     'L1_attn_l2o_b': (0.0, 0.354),
     'L1_attn_wqk_b': (0.0, 0.8),
     'L1_attn_cproj_b': (0.0, 0.1),
     'L1_ffn_b_in': (0.0, 0.522),
     'L1_ffn_b_out': (0.0, 0.355),
     'L2_attn_bq': (0.0, 0.8),
     'L2_attn_bk': (0.0, 0.8),
     'L2_attn_bv': (0.0, 0.1),
     'L2_attn_bo': (0.0, 0.1),
     'L3_attn_bq': (0.0, 0.8),
     'L3_attn_bk': (0.0, 0.8),
     'L3_attn_bv': (0.0, 0.576),
     'L3_attn_bo': (0.0, 0.1)}
    factors = {'L1_attn_c_attn_w': 8.0,
     'L1_attn_q2l_w': 8.0,
     'L1_attn_kv2l_w': 8.0,
     'L1_attn_l2o_w': 8.0,
     'L1_attn_wqk_w': 8.0,
     'L3_attn_Wq': 8.0,
     'L3_attn_Wk': 8.0,
     'L3_attn_Wv': 7.671,
     'L3_attn_Wo': 3.613,
     'L3_attn_decay_params': 8.0,
     'L3_attn_mix_weights': 8.0}
    for name, (base, spread) in spreads.items():
        noise = np.random.default_rng([zlib.crc32(name.encode()), seed]).standard_normal(out[name].shape)
        drawn = base * np.exp(spread * noise) if base else spread * noise
        out[name] = jnp.asarray(drawn.astype(out[name].dtype))
    for name, factor in factors.items():
        out[name] = (out[name] * factor).astype(out[name].dtype)
    return out
```

```python
from contextlib import ExitStack

import numpy as np

import concourse.bass as bass
from concourse import mybir

F32 = mybir.dt.float32
BF16 = mybir.dt.bfloat16
I32 = mybir.dt.int32
U32 = mybir.dt.uint32
ALU = mybir.AluOpType
ACT = mybir.ActivationFunctionType
AXX = mybir.AxisListType.X
ds = bass.ds

P = 128
D = 256
DC = D // P
B = 8
S = 256
ST = S // P
T = B * S
NT = T // P
LN_EPS = 1e-5
ROUND = 1.5 * 2.0 ** 23


class Shared:
    pass


class Signals:

    def __init__(self, nc):
        self.nc, self.held = nc, []

    def __call__(self, name):
        self.held.append(self.nc.alloc_semaphore(name))
        return self.held[-1]

    def __enter__(self):
        return self

    def __exit__(self, *failed):
        if not failed[0]:
            self.nc.clear_and_free_semaphores(self.held)
            self.nc.all_engine_barrier()
        return False


def bc(ap, shape):
    return ap.unsqueeze(1).broadcast_to(shape)


def row_ap(vec, parts=P):
    return vec.partition_broadcast(parts)


def col_ap(vec):
    return vec.rearrange("(c p) -> p c", p=P)


def kxn(w):
    return w.rearrange("(c p) n -> p c n", p=P)


def normed(v, src, out, stats, mv, rstd, var_sem, rstd_sem, count):
    for t in range(ST):
        v.bn_stats(stats[:, t, :], src(t))
    v.drain()
    for t in range(ST):
        v.bn_aggr(mv[:, t, :], stats[:, t, :])
    v.drain()
    v.tensor_scalar(mv[:, :, 1:2], mv[:, :, 1:2], LN_EPS, None, ALU.add).then_inc(var_sem, 1)
    v.wait_ge(rstd_sem, count)
    for t in range(ST):
        v.tensor_scalar(out[:, t, :], src(t), mv[:, t, 0:1], rstd[:, t, 0:1], ALU.subtract, ALU.mult)
    v.drain()


def rstd_of(g, sh, mv, rstd, var_sem, rstd_sem, count):
    g.wait_ge(var_sem, count)
    g.tensor_tensor(rstd[:], mv[:, :, 1:2], sh.minus_half[:], ALU.pow).then_inc(rstd_sem, 1)


def turn(pe, out, src, ident):
    for c in range(DC):
        for t in range(ST):
            last = pe.transpose(out[:, c, t * P:(t + 1) * P], src[:, t, c * P:(c + 1) * P], ident)
    return last


def project(pe, out, w, xT, m0, m=P):
    chunks = xT.shape[1]
    for c in range(chunks):
        last = pe.matmul(out, w[:, c, m0:m0 + m], xT[:, c, :], start=(c == 0), stop=(c == chunks - 1))
    return last


def project_rows(pe, out, xT, w, t):
    chunks = xT.shape[1]
    for c in range(chunks):
        last = pe.matmul(out, xT[:, c, t * P:(t + 1) * P], w[:, c, :], start=(c == 0), stop=(c == chunks - 1))
    return last


def setup_constants(nc, ctx, sh):
    sb = lambda name, shape, dt=F32: ctx.enter_context(nc.sbuf_tensor(name, shape, dt))
    sh.h = sb("h", [P, NT, D])
    sh.ident = sb("ident", [P, P])
    sh.identb = sb("identb", [P, P], BF16)
    sh.ones = sb("ones", [P, P])
    sh.above = sb("above", [P, P])
    sh.minus_half = sb("minus_half", [P, ST, 1])
    filled = nc.alloc_semaphore("filled")
    with nc.Block() as block:
        @block.gpsimd
        def _(g):
            g.memset(sh.ident[:], 0.0)
            g.memset(sh.identb[:], 0.0)
            g.memset(sh.ones[:], 1.0)
            g.memset(sh.above[:], 1.0)
            g.memset(sh.minus_half[:], -0.5)
            g.drain().then_inc(filled, 1)
            g.wait_ge(filled, 1)
            for m in (sh.ident, sh.identb):
                g.affine_select(out=m[:], in_=m[:], compare_op=ALU.not_equal, fill=1.0, base=0,
                                pattern=[[-1, P]], channel_multiplier=1)
            g.affine_select(out=sh.above[:], in_=sh.above[:], compare_op=ALU.is_gt, fill=0.0, base=0,
                            pattern=[[1, P]], channel_multiplier=-1)

        @block.scalar
        def _(a):
            a.preload_act_table(ACT.Exp)


def embedding(nc, sh, x, table):
    BLK, QMAX, PART = 32, 31.0, 4
    NB = PART * D // BLK
    with ExitStack() as ctx, Signals(nc) as signals:
        sb = lambda name, shape, dt=F32: ctx.enter_context(nc.sbuf_tensor(name, shape, dt))
        ids = sb("e_ids", [P, NT], I32)
        raw = sb("e_raw", [P, NT, D])
        amax = sb("e_amax", [P, NB])
        scale = sb("e_scale", [P, NB])
        safe = sb("e_safe", [P, NB])
        inv = sb("e_inv", [P, NB])
        q = sb("e_q", [P, NB, BLK])
        ids_in = signals("e_ids_in")
        rows_in = [signals(f"e_rows_in{k}") for k in range(NT // PART)]
        with nc.Block() as block:
            @block.sync
            def _(sp):
                sp.dma_start(ids[:], x.rearrange("b (t p) -> p (b t)", p=P),
                             allow_slow_non_contiguous=True).then_inc(ids_in, 16)

            @block.gpsimd
            def _(g):
                g.wait_ge(ids_in, 16)
                for t in range(NT):
                    g.indirect_dma_start(out=raw[:, t, :], out_offset=None, in_=table,
                                         in_offset=bass.IndirectOffsetOnAxis(ap=ids[:, t:t + 1].bitcast(U32), axis=0)
                                         ).then_inc(rows_in[t // PART], 16)

            @block.vector
            def _(v):
                for k in range(NT // PART):
                    rows = raw[:, k * PART:(k + 1) * PART, :].rearrange("p t (n j) -> p (t n) j", j=BLK)
                    out = sh.h[:, k * PART:(k + 1) * PART, :].rearrange("p t (n j) -> p (t n) j", j=BLK)
                    v.wait_ge(rows_in[k], 16 * PART)
                    v.tensor_reduce(amax[:], rows, AXX, ALU.max, apply_absolute_value=True)
                    v.drain()
                    v.tensor_scalar(scale[:], amax[:], 1.0 / QMAX, None, ALU.mult)
                    v.drain()
                    v.scalar_tensor_tensor(safe[:], scale[:], 0.0, scale[:], ALU.is_equal, ALU.add)
                    v.drain()
                    v.reciprocal(inv[:], safe[:])
                    v.drain()
                    v.tensor_tensor(q[:], rows, inv[:].unsqueeze(2).broadcast_to([P, NB, BLK]), ALU.mult)
                    v.drain()
                    v.tensor_scalar(q[:], q[:], ROUND, ROUND, ALU.add, ALU.subtract)
                    v.drain()
                    v.tensor_scalar(q[:], q[:], QMAX, -QMAX, ALU.min, ALU.max)
                    v.drain()
                    v.tensor_tensor(out, q[:], scale[:].unsqueeze(2).broadcast_to([P, NB, BLK]), ALU.mult)
                    v.drain()


def time_and_channel_mix(nc, sh, w):
    F = w["Wkey"].shape[1]
    FC = F // P
    with ExitStack() as ctx, Signals(nc) as signals:
        sb = lambda name, shape, dt=F32: ctx.enter_context(nc.sbuf_tensor("a0_" + name, shape, dt))
        ps = lambda name, shape, dt=F32: ctx.enter_context(nc.psum_tensor("a0_" + name, shape, dt))
        sem = lambda name: signals("a0_" + name)
        W = {n: sb(n, [P, DC, D]) for n in ("Wr", "Ww", "Wk", "Wv", "Wo", "Wrec")}
        Wkey = sb("Wkey", [P, DC, F])
        Wval = sb("Wval", [P, FC, D])
        rows = {n: sb(n, [P, D]) for n in ("ln1_g", "ln1_b", "ln2_g", "ln2_b")}
        tdecay = sb("tdecay", [P, DC])
        decay = sb("decay", [P, DC])
        decays = sb("decays", [P, DC, S])
        stats, mv, rstd = sb("stats", [P, ST, 6]), sb("mv", [P, ST, 2]), sb("rstd", [P, ST, 1])
        x0 = sb("x0", [P, ST, D])
        xn = sb("xn", [P, ST, D])
        xT = sb("xT", [P, DC, S])
        er, ew, e, ev = (sb(n, [P, DC, S]) for n in ("er", "ew", "e", "ev"))
        num, den = sb("num", [P, DC, S]), sb("den", [P, DC, S])
        rw = sb("rw", [P, DC, S])
        kr = sb("kr", [P, FC, S])
        ksq = sb("ksq", [P, FC, S])
        erec = sb("erec", [P, ST, D])
        cm = sb("cm", [P, ST, D])
        turned = ps("turned", [P, DC, S])
        proj = [ps(n, [P, DC, S]) for n in ("p_r", "p_w", "p_k", "p_v")]
        p_o, p_val, p_rec = (ps(n, [P, ST, D]) for n in ("p_o", "p_val", "p_rec"))
        w_in, decay_in, var, rst = sem("w_in"), sem("decay_in"), sem("var"), sem("rst")
        decay_ready = sem("decay_ready")
        xn_ready, turned_ready, xT_ready = sem("xn_ready"), sem("turned_ready"), sem("xT_ready")
        proj_ready, ew_ready, kw_ready, e_ready, rw_ready = (
            sem(n) for n in ("proj_ready", "ew_ready", "kw_ready", "e_ready", "rw_ready"))
        o_ready, key_ready, relu_ready, ksq_ready, rec_ready, erec_ready, val_ready = (
            sem(n) for n in ("o_ready", "key_ready", "relu_ready", "ksq_ready", "rec_ready", "erec_ready", "val_ready"))
        NW = 12
        PAIRS = FC // 2
        with nc.Block() as block:
            @block.sync
            def _(sp):
                sp.dma_start(tdecay[:], col_ap(w["time_decay"]), allow_slow_non_contiguous=True).then_inc(decay_in, 16)
                for n in ("Wr", "Ww", "Wk", "Wv", "Wo", "Wrec"):
                    sp.dma_start(W[n][:], kxn(w[n])).then_inc(w_in, 16)
                sp.dma_start(Wkey[:], kxn(w["Wkey"])).then_inc(w_in, 16)
                sp.dma_start(Wval[:], kxn(w["Wval"])).then_inc(w_in, 16)
                for n in ("ln1_g", "ln1_b", "ln2_g", "ln2_b"):
                    sp.dma_start(rows[n][:], row_ap(w[n])).then_inc(w_in, 16)

            @block.gpsimd
            def _(g):
                with g.Fori(0, B) as b:
                    for k in range(3):
                        rstd_of(g, sh, mv, rstd, var, rst, b * 3 + k + 1)

            @block.tensor
            def _(pe):
                pe.wait_ge(w_in, 16 * NW)
                with pe.Fori(0, B) as b:
                    pe.wait_ge(xn_ready, b * 2 + 1)
                    turn(pe, turned, xn, sh.ident[:]).then_inc(turned_ready, 1)
                    pe.wait_ge(xT_ready, b * 2 + 1)
                    for n, bank in zip(("Ww", "Wk", "Wr", "Wv"), (1, 2, 0, 3)):
                        for c in range(DC):
                            last = project(pe, proj[bank][:, c, :], W[n], xT, c * P)
                        last.then_inc(proj_ready, 1)
                    pe.wait_ge(rw_ready, b + 1)
                    for t in range(ST):
                        last = project_rows(pe, p_o[:, t, :], rw, W["Wo"], t)
                    last.then_inc(o_ready, 1)
                    pe.wait_ge(xn_ready, b * 2 + 2)
                    turn(pe, turned, xn, sh.ident[:]).then_inc(turned_ready, 1)
                    pe.wait_ge(xT_ready, b * 2 + 2)
                    for j in range(PAIRS):
                        for c in range(2):
                            last = project(pe, proj[j][:, c, :], Wkey, xT, (2 * j + c) * P)
                        last.then_inc(key_ready, 1)
                    for t in range(ST):
                        last = project_rows(pe, p_rec[:, t, :], xT, W["Wrec"], t)
                    last.then_inc(rec_ready, 1)
                    pe.wait_ge(ksq_ready, b * PAIRS + PAIRS)
                    for t in range(ST):
                        last = project_rows(pe, p_val[:, t, :], ksq, Wval, t)
                    last.then_inc(val_ready, 1)

            @block.scalar
            def _(a):
                a.wait_ge(decay_in, 16)
                a.activation(decay[:], tdecay[:], ACT.Exp).then_inc(decay_ready, 1)
                with a.Fori(0, B) as b:
                    a.wait_ge(turned_ready, b * 2 + 1)
                    a.copy(xT[:], turned[:]).then_inc(xT_ready, 1)
                    a.wait_ge(proj_ready, b * 4 + 1)
                    a.activation(ew[:], proj[1][:], ACT.Exp).then_inc(ew_ready, 1)
                    a.wait_ge(proj_ready, b * 4 + 3)
                    a.activation(er[:], proj[0][:], ACT.Exp, scale=-1.0)
                    a.wait_ge(kw_ready, b + 1)
                    a.activation(e[:], num[:], ACT.Exp).then_inc(e_ready, 1)
                    a.wait_ge(turned_ready, b * 2 + 2)
                    a.copy(xT[:], turned[:]).then_inc(xT_ready, 1)
                    for j in range(PAIRS):
                        a.wait_ge(key_ready, b * PAIRS + j + 1)
                        a.activation(kr[:, 2 * j:2 * j + 2, :], proj[j][:], ACT.Relu).then_inc(relu_ready, 1)
                    a.wait_ge(rec_ready, b + 1)
                    a.activation(erec[:], p_rec[:], ACT.Exp, scale=-1.0).then_inc(erec_ready, 1)

            @block.vector
            def _(v):
                v.wait_ge(decay_ready, 1)
                for c in range(DC):
                    v.tensor_copy(decays[:, c, :], decay[:, c:c + 1].broadcast_to([P, S]))
                v.wait_ge(w_in, 16 * NW)
                with v.Fori(0, B) as b:
                    normed(v, lambda t: sh.h[:, ds(b * ST + t, 1), :], x0, stats, mv, rstd, var, rst, b * 3 + 1)
                    normed(v, lambda t: x0[:, t, :], xn, stats, mv, rstd, var, rst, b * 3 + 2)
                    v.tensor_tensor(xn[:], xn[:], bc(rows["ln1_g"][:], [P, ST, D]), ALU.mult)
                    v.drain()
                    v.tensor_tensor(xn[:], xn[:], bc(rows["ln1_b"][:], [P, ST, D]), ALU.add).then_inc(xn_ready, 1)
                    v.wait_ge(ew_ready, b + 1)
                    v.wait_ge(proj_ready, b * 4 + 2)
                    v.tensor_tensor(num[:], proj[2][:], ew[:], ALU.subtract).then_inc(kw_ready, 1)
                    v.wait_ge(e_ready, b + 1)
                    v.wait_ge(proj_ready, b * 4 + 4)
                    v.tensor_tensor(ev[:], proj[3][:], e[:], ALU.mult)
                    for c in range(DC):
                        v.tensor_tensor_scan(den[:, c, :], decays[:, c, :], e[:, c, :], 0.0, ALU.mult, ALU.add)
                    v.drain()
                    for c in range(DC):
                        v.tensor_tensor_scan(num[:, c, :], decays[:, c, :], ev[:, c, :], 0.0, ALU.mult, ALU.add)
                    v.tensor_scalar(er[:], er[:], 1.0, None, ALU.add)
                    v.drain()
                    v.scalar_tensor_tensor(den[:], den[:], 1e-8, er[:], ALU.add, ALU.mult)
                    v.drain()
                    v.reciprocal(den[:], den[:])
                    v.drain()
                    v.tensor_tensor(rw[:], num[:], den[:], ALU.mult).then_inc(rw_ready, 1)
                    v.wait_ge(o_ready, b + 1)
                    v.tensor_tensor(x0[:], x0[:], p_o[:], ALU.add)
                    v.drain()
                    normed(v, lambda t: x0[:, t, :], xn, stats, mv, rstd, var, rst, b * 3 + 3)
                    v.tensor_tensor(xn[:], xn[:], bc(rows["ln2_g"][:], [P, ST, D]), ALU.mult)
                    v.drain()
                    v.tensor_tensor(xn[:], xn[:], bc(rows["ln2_b"][:], [P, ST, D]), ALU.add).then_inc(xn_ready, 1)
                    for j in range(PAIRS):
                        v.wait_ge(relu_ready, b * PAIRS + j + 1)
                        r = kr[:, 2 * j:2 * j + 2, :]
                        v.tensor_tensor(ksq[:, 2 * j:2 * j + 2, :], r, r, ALU.mult).then_inc(ksq_ready, 1)
                    v.tensor_tensor(x0[:], x0[:], sh.h[:, ds(b * ST, ST), :], ALU.add)
                    v.wait_ge(erec_ready, b + 1)
                    v.tensor_scalar(erec[:], erec[:], 1.0, None, ALU.add)
                    v.drain()
                    v.reciprocal(erec[:], erec[:])
                    v.drain()
                    v.wait_ge(val_ready, b + 1)
                    v.tensor_tensor(cm[:], p_val[:], erec[:], ALU.mult)
                    v.drain()
                    v.tensor_tensor(sh.h[:, ds(b * ST, ST), :], x0[:], cm[:], ALU.add)
                    v.drain()


def store_out(nc, sh, out):
    with ExitStack() as ctx, Signals(nc) as signals:
        stored = signals("stored")
        with nc.Block() as block:
            @block.sync
            def _(sp):
                for k in range(2):
                    half = slice(k * NT // 2, (k + 1) * NT // 2)
                    sp.dma_start(out.rearrange("b (t p) d -> p (b t) d", p=P)[:, half, :], sh.h[:, half, :]).then_inc(stored, 16)
                sp.wait_ge(stored, 32)


E = 8
K = 2
TILE = 256
TB = TILE // P
KT = K * NT
SHARED_TILES = T // TILE
ROUTED_TILES = K * T // TILE + E
CAP = 640
SLOTS = (SHARED_TILES + ROUTED_TILES) * TILE
TRASH = SLOTS


def routing_state(nc, ctx, sh, name):
    sb = lambda n, shape, dt=F32: ctx.enter_context(nc.sbuf_tensor(f"{name}_{n}", shape, dt))
    sh.xn_all = sb("xn_all", [P, NT, D])
    sh.slot = sb("slot", [P, KT], I32)
    sh.back = sb("back", [P, KT], I32)
    sh.weight = sb("weight", [P, KT])
    sh.tile_expert = sb("tile_expert", [1, SHARED_TILES + ROUTED_TILES], I32)


def route(nc, sh, name, gate, kind, bias=None):
    with ExitStack() as ctx, Signals(nc) as signals:
        sb = lambda n, shape, dt=F32: ctx.enter_context(nc.sbuf_tensor(f"{name}_{n}", shape, dt))
        ps = lambda n, shape, dt=F32: ctx.enter_context(nc.psum_tensor(f"{name}_{n}", shape, dt))
        sem = lambda n: signals(f"{name}_{n}")
        gw = sb("gw", [P, DC, E])
        bias_row = sb("bias", [P, E])
        stats, mv, rstd = sb("stats", [P, ST, 6]), sb("mv", [P, ST, 2]), sb("rstd", [P, ST, 1])
        xn_of_batch = sb("xnb", [P, ST, D])
        xT = sb("xT", [P, DC, S])
        logits = sb("logits", [P, NT, E])
        sel = sb("sel", [P, NT, E])
        val = sb("val", [P, NT, E])
        tmp = sb("tmp", [P, NT, E])
        best = sb("best", [P, NT])
        idx = sb("idx", [P, E])
        idx8 = sb("idx8", [P, E])
        oh = sb("oh", [P, E, KT])
        ohk = sb("ohk", [P, NT, E])
        w2 = sb("w2", [P, K, NT])
        total, incl, pos, big = (sb(n, [P, E, KT]) for n in ("total", "incl", "pos", "big"))
        reset = sb("reset", [P, E, KT])
        one8 = sb("one8", [P, E])
        base, tiles, ends = sb("base", [P, E]), sb("tiles", [P, E]), sb("ends", [P, E])
        rank, ebase, valid, trash, tf = (sb(n, [P, KT]) for n in ("rank", "ebase", "valid", "trash", "tf"))
        tidx = sb("tidx", [1, ROUTED_TILES])
        tcmp = sb("tcmp", [1, ROUTED_TILES, E])
        texp = sb("texp", [1, ROUTED_TILES])
        turned = ps("turned", [P, DC, S])
        p_logit = ps("p_logit", [P, ST, E])
        p_rank, p_total = ps("p_rank", [P, E, KT]), ps("p_total", [P, E, KT])
        w_in, var, rst, consts = sem("w_in"), sem("var"), sem("rst"), sem("consts")
        xn_ready, turned_ready, xT_ready, logit_ready, oh_ready, count_ready, soft, softed = (
            sem(n) for n in ("xn_ready", "turned_ready", "xT_ready", "logit_ready", "oh_ready", "count_ready",
                             "soft", "softed"))
        with nc.Block() as block:
            @block.sync
            def _(sp):
                sp.dma_start(gw[:], gate.rearrange("(c p) e -> p c e", p=P),
                             allow_slow_non_contiguous=True).then_inc(w_in, 16)
                if bias is not None:
                    sp.dma_start(bias_row[:], row_ap(bias)).then_inc(w_in, 16)

            @block.gpsimd
            def _(g):
                g.iota(idx[:], [[1, E]], base=0, channel_multiplier=0, allow_small_or_imprecise_dtypes=True)
                g.iota(idx8[:], [[1, E]], base=E, channel_multiplier=0, allow_small_or_imprecise_dtypes=True)
                g.iota(tidx[:], [[1, ROUTED_TILES]], base=0, channel_multiplier=0, allow_small_or_imprecise_dtypes=True)
                g.iota(base[:], [[CAP, E]], base=0, channel_multiplier=0, allow_small_or_imprecise_dtypes=True)
                g.iota(trash[:], [[P, KT]], base=TRASH, channel_multiplier=1, allow_small_or_imprecise_dtypes=True)
                g.memset(one8[:], 1.0)
                g.memset(reset[:, :, 1:KT], 1.0)
                g.memset(reset[:, :, 0:1], 0.0)
                g.drain().then_inc(consts, 1)
                with g.Fori(0, B) as b:
                    rstd_of(g, sh, mv, rstd, var, rst, b + 1)

            @block.tensor
            def _(pe):
                pe.wait_ge(w_in, 16 if bias is None else 32)
                with pe.Fori(0, B) as b:
                    pe.wait_ge(xn_ready, b + 1)
                    turn(pe, turned, xn_of_batch, sh.ident[:]).then_inc(turned_ready, 1)
                    pe.wait_ge(xT_ready, b + 1)
                    for t in range(ST):
                        last = project_rows(pe, p_logit[:, t, :], xT, gw, t)
                    last.then_inc(logit_ready, 1)
                pe.wait_ge(oh_ready, 1)
                pe.matmul(p_rank[:], sh.above[:], oh[:], start=True, stop=True)
                pe.matmul(p_total[:], sh.ones[:], oh[:], start=True, stop=True).then_inc(count_ready, 1)

            @block.scalar
            def _(a):
                with a.Fori(0, B) as b:
                    a.wait_ge(turned_ready, b + 1)
                    a.copy(xT[:], turned[:]).then_inc(xT_ready, 1)
                a.wait_ge(soft, 1)
                a.activation(tmp[:], tmp[:], ACT.Exp).then_inc(softed, 1)

            @block.vector
            def _(v):
                with v.Fori(0, B) as b:
                    normed(v, lambda t: sh.h[:, ds(b * ST + t, 1), :], xn_of_batch, stats, mv, rstd, var, rst, b + 1)
                    v.tensor_copy(sh.xn_all[:, ds(b * ST, ST), :], xn_of_batch[:]).then_inc(xn_ready, 1)
                    v.wait_ge(logit_ready, b + 1)
                    v.tensor_copy(logits[:, ds(b * ST, ST), :], p_logit[:])
                    v.drain()
                v.wait_ge(consts, 1)
                v.wait_ge(w_in, 16 if bias is None else 32)
                if kind == "sigmoid":
                    v.tensor_scalar(tmp[:], logits[:], -1.0, None, ALU.mult).then_inc(soft, 1)
                    v.wait_ge(softed, 1)
                    v.tensor_scalar(tmp[:], tmp[:], 1.0, None, ALU.add)
                    v.drain()
                    v.reciprocal(val[:], tmp[:])
                    v.drain()
                    v.tensor_tensor(sel[:], val[:], bc(bias_row[:], [P, NT, E]), ALU.add)
                elif kind == "softmax":
                    v.tensor_reduce(best[:], logits[:], AXX, ALU.max)
                    v.drain()
                    v.tensor_tensor(tmp[:], logits[:], best[:].unsqueeze(2).broadcast_to([P, NT, E]),
                                    ALU.subtract).then_inc(soft, 1)
                    v.wait_ge(softed, 1)
                    v.tensor_reduce(best[:], tmp[:], AXX, ALU.add)
                    v.drain()
                    v.reciprocal(best[:], best[:])
                    v.drain()
                    v.tensor_tensor(val[:], tmp[:], best[:].unsqueeze(2).broadcast_to([P, NT, E]), ALU.mult)
                    v.drain()
                    v.tensor_copy(sel[:], val[:])
                else:
                    v.tensor_copy(val[:], logits[:])
                    v.tensor_copy(sel[:], logits[:])
                for k in range(K):
                    v.drain()
                    v.tensor_reduce(best[:], sel[:], AXX, ALU.max)
                    v.drain()
                    v.tensor_tensor(ohk[:], sel[:], best[:].unsqueeze(2).broadcast_to([P, NT, E]), ALU.is_equal)
                    v.drain()
                    v.scalar_tensor_tensor(ohk[:], ohk[:], -float(E), bc(idx8[:], [P, NT, E]), ALU.mult, ALU.add)
                    v.drain()
                    v.tensor_reduce(best[:], ohk[:], AXX, ALU.min)
                    v.drain()
                    v.tensor_tensor(ohk[:], bc(idx[:], [P, NT, E]), best[:].unsqueeze(2).broadcast_to([P, NT, E]),
                                    ALU.is_equal)
                    v.drain()
                    v.tensor_copy(oh[:, :, k * NT:(k + 1) * NT].rearrange("p e t -> p t e"), ohk[:])
                    v.scalar_tensor_tensor(sel[:], ohk[:], -3e38, sel[:], ALU.mult, ALU.add)
                    v.tensor_tensor(ohk[:], ohk[:], val[:], ALU.mult)
                    v.drain()
                    v.tensor_reduce(w2[:, k, :], ohk[:], AXX, ALU.add)
                v.drain().then_inc(oh_ready, 1)
                if kind == "softmax2":
                    v.tensor_tensor(tmp[:, :, 0], w2[:, 1, :], w2[:, 0, :], ALU.subtract)
                    v.tensor_scalar(tmp[:, :, 1:E], logits[:, :, 1:E], 0.0, None, ALU.min)
                    v.drain().then_inc(soft, 1)
                    v.wait_ge(softed, 1)
                    v.tensor_scalar(best[:], tmp[:, :, 0], 1.0, None, ALU.add)
                    v.drain()
                    v.reciprocal(w2[:, 0, :], best[:])
                    v.drain()
                    v.tensor_tensor(w2[:, 1, :], w2[:, 0, :], tmp[:, :, 0], ALU.mult)
                    v.drain()
                v.wait_ge(count_ready, 1)
                v.tensor_copy(total[:], p_total[:])
                v.drain()
                flat = lambda x: x[:].rearrange("p e k -> p (e k)")
                v.tensor_tensor_scan(flat(incl), flat(reset), flat(total), 0.0, ALU.mult, ALU.add)
                v.drain()
                v.tensor_tensor(pos[:], incl[:], total[:], ALU.subtract)
                v.drain()
                v.tensor_tensor(pos[:], pos[:], p_rank[:], ALU.add)
                if kind != "softmax2":
                    v.tensor_scalar(tiles[:], incl[:, :, KT - 1], TILE / 2 - 0.5, 1.0 / TILE, ALU.add, ALU.mult)
                    v.drain()
                    v.tensor_scalar(tiles[:], tiles[:], ROUND, ROUND, ALU.add, ALU.subtract)
                    v.drain()
                    v.tensor_tensor_scan(ends[:], one8[:], tiles[:], 0.0, ALU.mult, ALU.add)
                    v.drain()
                    v.tensor_tensor(base[:], ends[:], tiles[:], ALU.subtract)
                    v.drain()
                    first = SHARED_TILES * TILE if kind == "sigmoid" else 0
                    v.tensor_scalar(base[:], base[:], float(TILE), float(first), ALU.mult, ALU.add)
                    v.tensor_tensor(tcmp[:], ends[0:1, :].unsqueeze(1).broadcast_to([1, ROUTED_TILES, E]),
                                    tidx[:].unsqueeze(2).broadcast_to([1, ROUTED_TILES, E]), ALU.is_le)
                    v.drain()
                    v.tensor_reduce(texp[:], tcmp[:], AXX, ALU.add)
                    v.drain()
                    v.tensor_scalar(texp[:], texp[:], float(E - 1), None, ALU.min)
                    v.drain()
                    if kind == "sigmoid":
                        v.memset(sh.tile_expert[:, 0:SHARED_TILES], E)
                        v.tensor_copy(sh.tile_expert[:, SHARED_TILES:], texp[:])
                    else:
                        v.tensor_copy(sh.tile_expert[:, 0:ROUTED_TILES], texp[:])
                by_choice = lambda x: x[:].rearrange("p e k -> p k e")
                v.drain()
                v.tensor_tensor(big[:], oh[:], pos[:], ALU.mult)
                v.drain()
                v.tensor_reduce(rank[:], by_choice(big), AXX, ALU.add)
                v.drain()
                v.tensor_tensor(big[:], oh[:], base[:].unsqueeze(2).broadcast_to([P, E, KT]), ALU.mult)
                v.drain()
                v.tensor_reduce(ebase[:], by_choice(big), AXX, ALU.add)
                v.drain()
                if kind == "softmax2":
                    v.tensor_scalar(valid[:], rank[:], float(CAP), None, ALU.is_lt)
                    v.tensor_tensor(tf[:], rank[:], ebase[:], ALU.add)
                    v.drain()
                    v.tensor_tensor(tf[:], tf[:], trash[:], ALU.subtract)
                    v.drain()
                    v.tensor_tensor(tf[:], tf[:], valid[:], ALU.mult)
                    v.drain()
                    v.tensor_tensor(tf[:], tf[:], trash[:], ALU.add)
                    v.drain()
                    v.tensor_copy(sh.slot[:], tf[:])
                    v.scalar_tensor_tensor(rank[:], rank[:], float(CAP - 1), ebase[:], ALU.min, ALU.add)
                    v.drain()
                    v.tensor_copy(sh.back[:], rank[:])
                    v.tensor_tensor(sh.weight[:], w2[:].rearrange("p k t -> p (k t)"), valid[:], ALU.mult)
                else:
                    v.tensor_tensor(tf[:], rank[:], ebase[:], ALU.add)
                    v.drain()
                    v.tensor_copy(sh.slot[:], tf[:])
                    v.tensor_copy(sh.back[:], tf[:])
                    v.tensor_copy(sh.weight[:], w2[:].rearrange("p k t -> p (k t)"))
                v.drain()


def dispatch(nc, sh, name, buf, scaled, shared):
    with ExitStack() as ctx, Signals(nc) as signals:
        sem = lambda n: signals(f"{name}_{n}")
        GROUP = 4
        xs = ctx.enter_context(nc.sbuf_tensor(f"{name}_xs", [P, KT, D], F32)) if scaled else None
        xs_ready = sem("xs_ready")
        sent, shared_sent = sem("sent"), sem("shared_sent")
        with nc.Block() as block:
            @block.gpsimd
            def _(g):
                for j in range(KT):
                    if scaled and j % GROUP == 0:
                        g.wait_ge(xs_ready, j // GROUP + 1)
                    src = xs[:, j, :] if scaled else sh.xn_all[:, j % NT, :]
                    g.indirect_dma_start(out=buf, out_offset=bass.IndirectOffsetOnAxis(
                        ap=sh.slot[:, j:j + 1].bitcast(U32), axis=0), in_=src, in_offset=None).then_inc(sent, 16)
                g.wait_ge(sent, 16 * KT)

            @block.sync
            def _(sp):
                if shared:
                    sp.dma_start(buf[0:T, :].rearrange("(t p) d -> p t d", p=P), sh.xn_all[:]).then_inc(shared_sent, 16)
                    sp.wait_ge(shared_sent, 16)

            @block.vector
            def _(v):
                if scaled:
                    for j in range(KT):
                        last = v.tensor_scalar(xs[:, j, :], sh.xn_all[:, j % NT, :], sh.weight[:, j:j + 1], None, ALU.mult)
                        if j % GROUP == GROUP - 1:
                            v.drain().then_inc(xs_ready, 1)


def combine(nc, sh, name, obuf, shared):
    with ExitStack() as ctx, Signals(nc) as signals:
        sem = lambda n: signals(f"{name}_{n}")
        GROUP = 4
        y = ctx.enter_context(nc.sbuf_tensor(f"{name}_y", [P, KT, D], F32))
        ysh = ctx.enter_context(nc.sbuf_tensor(f"{name}_ysh", [P, NT, D], F32)) if shared else None
        came = [sem(f"came{j}") for j in range(KT // GROUP)]
        shared_came = sem("shared_came")
        with nc.Block() as block:
            @block.gpsimd
            def _(g):
                for j in range(KT):
                    g.indirect_dma_start(out=y[:, j, :], out_offset=None, in_=obuf, in_offset=bass.IndirectOffsetOnAxis(
                        ap=sh.back[:, j:j + 1].bitcast(U32), axis=0)).then_inc(came[j // GROUP], 16)

            @block.sync
            def _(sp):
                if shared:
                    sp.dma_start(ysh[:], obuf[0:T, :].rearrange("(t p) d -> p t d", p=P)).then_inc(shared_came, 16)

            @block.vector
            def _(v):
                if shared:
                    v.wait_ge(shared_came, 16)
                    v.tensor_tensor(sh.h[:], sh.h[:], ysh[:], ALU.add)
                    v.drain()
                for j in range(KT):
                    if j % GROUP == 0:
                        v.wait_ge(came[j // GROUP], 16 * GROUP)
                    if j == NT:
                        v.drain()
                    v.scalar_tensor_tensor(sh.h[:, j % NT, :], y[:, j, :], sh.weight[:, j:j + 1], sh.h[:, j % NT, :],
                                           ALU.mult, ALU.add)
                v.drain()


def expert_tiles(nc, sh, name, buf, obuf, wts, n_tiles, gated, b_out=None):
    NM = 3 if gated else 2
    WCOLS = wts.shape[2]
    with ExitStack() as ctx, Signals(nc) as signals:
        sb = lambda n, shape, dt=F32: ctx.enter_context(nc.sbuf_tensor(f"{name}_{n}", shape, dt))
        ps = lambda n, shape, dt=F32: ctx.enter_context(nc.psum_tensor(f"{name}_{n}", shape, dt))
        sem = lambda n: signals(f"{name}_{n}")
        wbuf = [sb(f"w{p}", [P, WCOLS]) for p in range(2)]
        w1 = [w[:, 0:DC * D].rearrange("p (c n) -> p c n", c=DC) for w in wbuf]
        w3 = [w[:, DC * D:2 * DC * D].rearrange("p (c n) -> p c n", c=DC) for w in wbuf]
        w2 = [w[:, (NM - 1) * DC * D:NM * DC * D].rearrange("p (c n) -> p c n", c=DC) for w in wbuf]
        bo = [sb(f"bo{p}", [P, D]) for p in range(2)] if not gated else None
        xin = [sb(f"xin{p}", [P, TB, D]) for p in range(2)]
        xT = [sb(f"xT{p}", [P, DC, TILE]) for p in range(2)]
        sg = sb("sg", [P, DC, TILE])
        hT = sb("hT", [P, DC, TILE])
        y = [sb(f"y{p}", [P, TB, D]) for p in range(2)]
        p_t = [ps(f"p_t{p}", [P, DC, TILE]) for p in range(2)]
        p_g = [ps(f"p_g{p}", [P, DC, TILE]) for p in range(2)]
        p_u = [ps(f"p_u{p}", [P, DC, TILE]) for p in range(2)] if gated else None
        p_o = [ps(f"p_o{p}", [P, TB, D]) for p in range(2)]
        x_in = [sem(f"x_in{p}") for p in range(2)]
        w_in = [sem(f"w_in{p}") for p in range(2)]
        stored = [sem(f"stored{p}") for p in range(2)]
        turned, xT_ready, g_ready, u_ready, sg_ready, h_ready, o_ready, y_ready, bank_free = (
            sem(n) for n in ("turned", "xT_ready", "g_ready", "u_ready", "sg_ready", "h_ready", "o_ready", "y_ready",
                             "bank_free"))
        rows = lambda m, i: m[ds(i * TILE, TILE), :].rearrange("(p t) d -> p t d", t=TB)
        W_DMAS = 1 if gated else 2
        with nc.Block() as block:
            @block.sync
            def _(sp):
                def load(i, p):
                    e = sp.value_load(sh.tile_expert[0:1, ds(i, 1)], min_val=0, max_val=wts.shape[0] - 1)
                    sp.dma_start(wbuf[p][:], wts[ds(e, 1), :, :].rearrange("a p n -> (a p) n")).then_inc(w_in[p], 16)
                    if not gated:
                        sp.dma_start(bo[p][:], b_out[ds(e, 1), :].rearrange("a n -> (a n)").partition_broadcast(P)
                                     ).then_inc(w_in[p], 16)

                def load_x(i, p):
                    sp.dma_start(xin[p][:], rows(buf, i)).then_inc(x_in[p], 16)

                for p in range(2):
                    load_x(p, p)
                    load(p, p)
                with sp.Fori(1, n_tiles // 2) as k:
                    for p in range(2):
                        sp.wait_ge(turned, k * 2 + (p - 1))
                        load_x(k * 2 + p, p)
                        sp.wait_ge(o_ready, k * 2 + (p - 1))
                        if not gated:
                            sp.wait_ge(y_ready, k * 2 + (p - 1))
                        load(k * 2 + p, p)

            @block.tensor
            def _(pe):
                def turn_tile(i, k, p):
                    pe.wait_ge(x_in[p], k * 16 + 16)
                    turn(pe, p_t[p], xin[p], sh.ident[:]).then_inc(turned, 1)

                def tile(i, k, p, ahead):
                    pe.wait_ge(xT_ready, i + 1)
                    pe.wait_ge(w_in[p], k * (16 * W_DMAS) + 16 * W_DMAS)
                    for c in range(DC):
                        last = project(pe, p_g[p][:, c, :], w1[p], xT[p], c * P)
                    last.then_inc(g_ready, 1)
                    if gated:
                        for c in range(DC):
                            last = project(pe, p_u[p][:, c, :], w3[p], xT[p], c * P)
                        last.then_inc(u_ready, 1)
                    if ahead:
                        turn_tile(i + 1, k + p, 1 - p)
                    pe.wait_ge(h_ready, i + 1)
                    for t in range(TB):
                        last = project_rows(pe, p_o[p][:, t, :], hT, w2[p], t)
                    last.then_inc(o_ready, 1)

                turn_tile(0, 0, 0)
                with pe.Fori(0, n_tiles // 2 - 1) as k:
                    for p in range(2):
                        tile(k * 2 + p, k, p, True)
                for p in range(2):
                    tile(n_tiles - 2 + p, n_tiles // 2 - 1, p, p == 0)

            @block.scalar
            def _(a):
                def copy_turned(i, p):
                    a.wait_ge(turned, i + 1)
                    a.copy(xT[p][:], p_t[p][:]).then_inc(xT_ready, 1)

                def store(i, p):
                    a.wait_ge(y_ready, i + 1)
                    a.dma_start(rows(obuf, i), y[p][:]).then_inc(stored[p], 16)

                def tile(i, p, first, ahead):
                    a.wait_ge(g_ready, i + 1)
                    if gated:
                        a.activation(sg[:], p_g[p][:], ACT.Silu).then_inc(sg_ready, 1)
                    else:
                        for c in range(DC):
                            last = a.activation(hT[:, c, :], p_g[p][:, c, :], ACT.Gelu_apprx_tanh,
                                                bias=wbuf[p][:, 4 * D + c:4 * D + c + 1])
                        last.then_inc(h_ready, 1)
                    if ahead:
                        copy_turned(i + 1, 1 - p)
                    if not first:
                        store(i - 1, 1 - p)

                a.preload_act_table(ACT.Silu if gated else ACT.Gelu_apprx_tanh)
                copy_turned(0, 0)
                tile(0, 0, True, True)
                tile(1, 1, False, True)
                with a.Fori(1, n_tiles // 2 - 1) as k:
                    for p in range(2):
                        tile(k * 2 + p, p, False, True)
                for p in range(2):
                    tile(n_tiles - 2 + p, p, False, p == 0)
                store(n_tiles - 1, 1)
                for p in range(2):
                    a.wait_ge(stored[p], 16 * (n_tiles // 2))
                a.preload_act_table(ACT.Exp)

            @block.vector
            def _(v):
                def tile(i, k, p, reused):
                    if gated:
                        v.wait_ge(sg_ready, i + 1)
                        v.wait_ge(u_ready, i + 1)
                        v.tensor_tensor(hT[:], sg[:], p_u[p][:], ALU.mult).then_inc(h_ready, 1)
                    v.wait_ge(o_ready, i + 1)
                    if reused:
                        v.wait_ge(stored[p], k * 16)
                    if gated:
                        v.tensor_copy(y[p][:], p_o[p][:]).then_inc(y_ready, 1)
                    else:
                        v.tensor_tensor(y[p][:], p_o[p][:], bc(bo[p][:], [P, TB, D]), ALU.add).then_inc(y_ready, 1)

                for p in range(2):
                    tile(p, 0, p, False)
                with v.Fori(1, n_tiles // 2) as k:
                    for p in range(2):
                        tile(k * 2 + p, k, p, True)


def clear_slots(nc, sh, buf):
    with ExitStack() as ctx, Signals(nc) as signals:
        zeros = ctx.enter_context(nc.sbuf_tensor("zeros", [P, 8, D], F32))
        zeroed, cleared = signals("zeroed"), signals("cleared")
        with nc.Block() as block:
            @block.vector
            def _(v):
                v.memset(zeros[:], 0.0).then_inc(zeroed, 1)

            @block.sync
            def _(sp):
                sp.wait_ge(zeroed, 1)
                n = SLOTS // (P * 8)
                for j in range(n):
                    sp.dma_start(buf[j * P * 8:(j + 1) * P * 8, :].rearrange("(p r) d -> p r d", p=P),
                                 zeros[:]).then_inc(cleared, 16)
                sp.wait_ge(cleared, 16 * n)


H = 16
HD = D // H
LAT = 32
GROUP_ROWS = 32
NEG = -1e30
SAMPLES = 40


def decay_masks(nc, sh, masks, decay_params, mix_weights):
    N = 2
    with ExitStack() as ctx, Signals(nc) as signals:
        sb = lambda n, shape, dt=F32: ctx.enter_context(nc.sbuf_tensor("dm_" + n, shape, dt))
        sem = lambda n: signals("dm_" + n)
        dist, far = sb("dist", [P, ST, S]), sb("far", [P, ST, S])
        dp, lnd, mw, ex = sb("dp", [P, H * N]), sb("lnd", [P, H * N]), sb("mw", [P, H, N]), sb("ex", [P, H, N])
        top = sb("top", [P, H])
        powers = [sb(f"powers{n}", [P, ST, S]) for n in range(2)]
        came, iota_done, clipped, shifted, exped, logged, dist_ready, power_ready, power_used = (
            sem(n) for n in ("came", "iota_done", "clipped", "shifted", "exped", "logged", "dist_ready",
                             "power_ready", "power_used"))
        with nc.Block() as block:
            @block.sync
            def _(sp):
                sp.dma_start(dp[:], row_ap(decay_params.rearrange("h n -> (h n)"))).then_inc(came, 16)
                sp.dma_start(mw[:].rearrange("p h n -> p (h n)"), row_ap(mix_weights.rearrange("h n -> (h n)"))
                             ).then_inc(came, 16)

            @block.gpsimd
            def _(g):
                g.iota(dist[:], [[P, ST], [-1, S]], base=0, channel_multiplier=1,
                       allow_small_or_imprecise_dtypes=True).then_inc(iota_done, 1)

            @block.scalar
            def _(a):
                a.wait_ge(shifted, 1)
                a.activation(ex[:], mw[:], ACT.Exp).then_inc(exped, 1)
                a.wait_ge(clipped, 1)
                a.activation(lnd[:], dp[:], ACT.Ln).then_inc(logged, 1)
                a.wait_ge(logged, 1)
                a.wait_ge(dist_ready, 1)
                for j in range(H * N):
                    if j >= 2:
                        a.wait_ge(power_used, j - 1)
                    a.activation(powers[j % 2][:], dist[:], ACT.Exp, scale=lnd[:, j:j + 1]).then_inc(power_ready, 1)

            @block.vector
            def _(v):
                v.wait_ge(came, 32)
                v.tensor_scalar(dp[:], dp[:], 0.01, 0.9999, ALU.max, ALU.min).then_inc(clipped, 1)
                v.tensor_reduce(top[:], mw[:], AXX, ALU.max)
                v.drain()
                v.tensor_tensor(mw[:], mw[:], top[:].unsqueeze(2).broadcast_to([P, H, N]), ALU.subtract
                                ).then_inc(shifted, 1)
                v.wait_ge(iota_done, 1)
                v.tensor_scalar(far[:], dist[:], -1.0, None, ALU.mult)
                v.drain()
                v.tensor_tensor(dist[:], dist[:], far[:], ALU.max).then_inc(dist_ready, 1)
                v.wait_ge(exped, 1)
                v.tensor_reduce(top[:], ex[:], AXX, ALU.add)
                v.drain()
                v.reciprocal(top[:], top[:])
                v.drain()
                v.tensor_tensor(ex[:], ex[:], top[:].unsqueeze(2).broadcast_to([P, H, N]), ALU.mult)
                v.drain()
                for h in range(H):
                    v.wait_ge(power_ready, N * h + 1)
                    v.tensor_scalar(masks[:, h, :, :], powers[0][:], ex[:, h, 0:1], None, ALU.mult
                                    ).then_inc(power_used, 1)
                    v.wait_ge(power_ready, N * h + 2)
                    v.wait_ge(power_used, N * h + 1)
                    v.scalar_tensor_tensor(masks[:, h, :, :], powers[1][:], ex[:, h, 1:2], masks[:, h, :, :],
                                           ALU.mult, ALU.add).then_inc(power_used, 1)


def attention(nc, sh, name, kind, w):
    latent, sparse, decayed = kind == "latent", kind == "sparse", kind == "decay"
    V = LAT if latent else HD
    with ExitStack() as ctx, Signals(nc) as signals:
        sb = lambda n, shape, dt=F32: ctx.enter_context(nc.sbuf_tensor(f"{name}_{n}", shape, dt))
        ps = lambda n, shape, dt=F32: ctx.enter_context(nc.psum_tensor(f"{name}_{n}", shape, dt))
        sem = lambda n: signals(f"{name}_{n}")
        stats, mv, rstd = sb("stats", [P, ST, 6]), sb("mv", [P, ST, 2]), sb("rstd", [P, ST, 1])
        xn = sb("xn", [P, ST, D])
        xT = sb("xT", [P, DC, S])
        Wq, Wk, Wv, Wo = (sb(n, [P, DC, D]) for n in ("Wq", "Wk", "Wv", "Wo"))
        bq, bk = sb("bq", [P, DC]), sb("bk", [P, DC])
        bo = sb("bo", [P, D])
        pr = [sb(f"pr{i}", [P, ST, S]) for i in range(2)]
        prT = [sb(f"prT{i}", [P, ST, S]) for i in range(2)]
        negmax = sb("negmax", [P, H, ST])
        rsum = sb("rsum", [P, ST, H])
        rden = sb("rden", [P, ST, H])
        ctxv = sb("ctxv", [P, ST, H, V])
        cT = sb("cT", [P, H * V // P, S])
        A, Bk, C, Dk = (ps(n, [P, 4, S]) for n in ("A", "B", "C", "D"))
        ctx_ps = C[:].rearrange("p a s -> p (a s)")[:, 0:ST * H * V].rearrange("p (t h v) -> p t h v", t=ST, h=H)
        z = {n: sem(n) for n in (
            "w_in", "var", "rst", "xn_ready", "turned", "xT_ready", "q_ps", "k_ps", "v_ps", "q_ready", "k_ready",
            "v_ready", "s_ps", "neg_ready", "exp_ready", "pT_ps", "pT_ready", "o_ps", "ctx_ready", "cT_ps", "cT_ready",
            "out_ps", "masks_ready")}
        n_w = 7 if not latent else 8
        if latent:
            qf, kf, vf = (sb(n, [P, DC, S]) for n in ("qf", "kf", "vf"))
            ql, kl, qr, kr = (sb(n, [P, 4, S]) for n in ("ql", "kl", "qr", "kr"))
            qq = sb("qq", [P, 4, S])
            t1 = sb("t1", [P, 4, S])
            vl = sb("vl", [P, ST, H, LAT])
            bvf = sb("bvf", [P, DC])
            bd_q, bd_kv, bd_o = sb("bd_q", [P, 2, P]), sb("bd_kv", [P, D]), sb("bd_o", [P, 2, P])
            bd_k = sb("bd_k", [P, 2, P])
            bd_qk = sb("bd_qk", [P, P])
            rot, cos, sin = sb("rot", [P, P]), sb("cos", [P, S]), sb("sin", [P, S])
            bl_q, bl_k, bl_qk, bl_o = (sb(n, [P, 1]) for n in ("bl_q", "bl_k", "bl_qk", "bl_o"))
            bl_v = sb("bl_v", [P, LAT])
            mask = sb("mask", [P, ST, S])
            yT = sb("yT", [P, DC, S])
            z.update({n: sem(n) for n in (
                "bd_zero", "bd_in", "ql_ps", "kl_ps", "vl_ps", "rq_ps", "rk_ps", "qk_ps", "vf_ready", "ql_ready",
                "kl_ready", "vl_ready", "qr_ready", "kr_ready", "qq_ready", "y_ps", "y_ready")})
            keys, qrows = kr, [qq, qq]
        else:
            qe, qo, kT = (sb(n, [P, DC, S]) for n in ("qe", "qo", "kT"))
            vr = sb("vr", [P, ST, H, HD])
            bv = sb("bv", [P, D])
            parity = sb("parity", [P, 2])
            keys, qrows = kT, [qe, qo]
        if latent or decayed:
            sm = [sb(f"sm{i}", [P, ST, S]) for i in range(2)]
        if sparse:
            idx_i, idx_f, neg_i = sb("idx_i", [P, SAMPLES], I32), sb("idx_f", [P, SAMPLES]), sb("neg_i", [P, SAMPLES])
            tok = sb("tok", [P, ST])
            pick = sb("pick", [P, ST, SAMPLES])
            xsT, ksT = sb("xsT", [P, DC, SAMPLES]), sb("ksT", [P, DC, SAMPLES])
            smax, ssum = sb("smax", [P, ST, H]), sb("ssum", [P, ST, H])
            mrow, mwork, best8 = sb("mrow", [P, S]), sb("mwork", [H, S]), sb("best8", [H, 8])
            kept, unkept = sb("kept", [P, ST, H]), sb("unkept", [P, ST, H])
            meanv, mv_part = sb("meanv", [P, D]), sb("mv_part", [P, ST, H, HD])
            z.update({n: sem(n) for n in (
                "iotas", "pick_ready", "xs_ps", "xs_ready", "ks_ps", "ks_ready", "ss_ps", "stand_ready", "m_ps",
                "rows_ready", "kept_ps", "mean_ps", "kept_ready", "parity_in")})
        if decayed:
            masks = w["masks"]

        def bank(t, i):
            return t[:, 2 * i:2 * i + 2, :]

        def head_rows(h):
            if latent:
                return h // 4, (h % 4) * GROUP_ROWS, 0
            return h // 8, (h % 8) // 2 * GROUP_ROWS, h % 2

        with nc.Block() as block:
            @block.sync
            def _(sp):
                if latent:
                    for i, t in enumerate((Wq, Wk, Wv)):
                        sp.dma_start(t[:], kxn(w["c_attn_w"])[:, :, i * D:(i + 1) * D]).then_inc(z["w_in"], 16)
                    for i, t in enumerate((bq, bk, bvf)):
                        sp.dma_start(t[:], col_ap(w["c_attn_b"][i * D:(i + 1) * D]),
                                     allow_slow_non_contiguous=True).then_inc(z["w_in"], 16)
                    sp.dma_start(Wo[:], kxn(w["cproj_w"])).then_inc(z["w_in"], 16)
                    sp.dma_start(bo[:], row_ap(w["cproj_b"])).then_inc(z["w_in"], 16)
                    sp.dma_start(rot[:], w["rot"]).then_inc(z["bd_in"], 16)
                    sp.dma_start(cos[:], w["cos"]).then_inc(z["bd_in"], 16)
                    sp.dma_start(sin[:], w["sin"]).then_inc(z["bd_in"], 16)
                    col = lambda x: x.rearrange("(l a) -> l a", a=1)
                    for g in range(4):
                        rows = slice(g * LAT, (g + 1) * LAT)
                        sp.dma_start(bl_q[rows, :], col(w["q2l_b"])).then_inc(z["bd_in"], 16)
                        sp.dma_start(bl_k[rows, :], col(w["kv2l_b"])).then_inc(z["bd_in"], 16)
                        sp.dma_start(bl_qk[rows, :], col(w["wqk_b"])).then_inc(z["bd_in"], 16)
                    for g in range(8):
                        sp.dma_start(bl_o[g * HD:(g + 1) * HD, :], col(w["l2o_b"])).then_inc(z["bd_in"], 16)
                    sp.dma_start(bl_v[:], row_ap(w["kv2l_b"])).then_inc(z["bd_in"], 16)
                    sp.wait_ge(z["bd_zero"], 1)
                    for g in range(8):
                        f = slice(g * HD, (g + 1) * HD)
                        lat = slice(g % 4 * LAT, (g % 4 + 1) * LAT)
                        sp.dma_start(bd_q[f, g // 4, lat], w["q2l_w"]).then_inc(z["bd_in"], 16)
                        sp.dma_start(bd_k[f, g // 4, lat], w["kv2l_w"]).then_inc(z["bd_in"], 16)
                        sp.dma_start(bd_kv[f, g * LAT:(g + 1) * LAT], w["kv2l_w"]).then_inc(z["bd_in"], 16)
                        sp.dma_start(bd_o[lat, g // 4, f], w["l2o_w"]).then_inc(z["bd_in"], 16)
                    for g in range(4):
                        lat = slice(g * LAT, (g + 1) * LAT)
                        sp.dma_start(bd_qk[lat, lat], w["wqk_w"]).then_inc(z["bd_in"], 16)
                else:
                    for t, n in ((Wq, "Wq"), (Wk, "Wk"), (Wv, "Wv"), (Wo, "Wo")):
                        sp.dma_start(t[:], kxn(w[n])).then_inc(z["w_in"], 16)
                    for t, n in ((bq, "bq"), (bk, "bk")):
                        sp.dma_start(t[:], col_ap(w[n]), allow_slow_non_contiguous=True).then_inc(z["w_in"], 16)
                    sp.dma_start(bo[:], row_ap(w["bo"])).then_inc(z["w_in"], 16)
                    sp.dma_start(bv[:], row_ap(w["bv"])).then_inc(z["masks_ready"], 16)
                    sp.dma_start(parity[:], w["parity"]).then_inc(z["masks_ready"], 16)
                    if sparse:
                        sp.dma_start(idx_i[:], row_ap(w["idx_k"])).then_inc(z["masks_ready"], 16)

            BD_DMAS = 3 + 12 + 8 + 1 + 32 + 4
            CONST_DMAS = 3 if sparse else 2

            @block.gpsimd
            def _(g):
                if latent:
                    for t in (bd_q, bd_k, bd_kv, bd_o, bd_qk):
                        g.memset(t[:], 0.0)
                    g.memset(mask[:], 0.0)
                    g.drain().then_inc(z["bd_zero"], 1)
                    g.affine_select(out=mask[:], in_=mask[:], compare_op=ALU.is_ge, fill=NEG, base=0,
                                    pattern=[[P, ST], [-1, S]], channel_multiplier=1).then_inc(z["masks_ready"], 1)
                if sparse:
                    g.iota(tok[:], [[P, ST]], base=0, channel_multiplier=1,
                           allow_small_or_imprecise_dtypes=True).then_inc(z["iotas"], 1)
                with g.Fori(0, B) as b:
                    rstd_of(g, sh, mv, rstd, z["var"], z["rst"], b + 1)

            @block.tensor
            def _(pe):
                def scores(h, b):
                    c, r, odd = head_rows(h)
                    rows = slice(r, r + GROUP_ROWS)
                    for t in range(ST):
                        last = pe.matmul(A[:, 2 * (h % 2) + t, :], qrows[odd][rows, c, t * P:(t + 1) * P],
                                         keys[rows, c, :], start=True, stop=True)
                    last.then_inc(z["s_ps"], 1)

                def turn_probs(h, b):
                    pe.wait_ge(z["exp_ready"], b * H + h + 1)
                    for kb in range(ST):
                        for t in range(ST):
                            last = pe.transpose(bank(Bk, h % 2)[:, kb, t * P:(t + 1) * P],
                                                pr[h % 2][:, t, kb * P:(kb + 1) * P], sh.ident[:])
                    last.then_inc(z["pT_ps"], 1)

                def values(h, b):
                    pe.wait_ge(z["pT_ready"], b * H + h + 1)
                    for t in range(ST):
                        for kb in range(ST):
                            last = pe.matmul(ctx_ps[:, t, h, :], prT[h % 2][:, kb, t * P:(t + 1) * P],
                                             (vl if latent else vr)[:, kb, h, :], start=(kb == 0), stop=(kb == ST - 1))
                    if h == H - 1:
                        last.then_inc(z["o_ps"], 1)

                pe.wait_ge(z["w_in"], 16 * n_w)
                if latent:
                    pe.wait_ge(z["bd_in"], 16 * BD_DMAS)
                if sparse:
                    pe.wait_ge(z["pick_ready"], 1)
                with pe.Fori(0, B) as b:
                    pe.wait_ge(z["xn_ready"], b + 1)
                    turn(pe, bank(Dk, 0), xn, sh.ident[:]).then_inc(z["turned"], 1)
                    if sparse:
                        for c in range(DC):
                            for t in range(ST):
                                last = pe.matmul(C[:, c, 0:SAMPLES], xn[:, t, c * P:(c + 1) * P], pick[:, t, :],
                                                 start=(t == 0), stop=(t == ST - 1))
                        last.then_inc(z["xs_ps"], 1)
                    pe.wait_ge(z["xT_ready"], b + 1)
                    for c in range(DC):
                        last = project(pe, A[:, c, :], Wq, xT, c * P)
                    last.then_inc(z["q_ps"], 1)
                    for c in range(DC):
                        last = project(pe, A[:, 2 + c, :], Wk, xT, c * P)
                    last.then_inc(z["k_ps"], 1)
                    if not latent:
                        for t in range(ST):
                            last = project_rows(pe, Bk[:, t, :], xT, Wv, t)
                        last.then_inc(z["v_ps"], 1)
                        if sparse:
                            pe.wait_ge(z["xs_ready"], b + 1)
                            for c in range(DC):
                                last = project(pe, C[:, 2 + c, 0:SAMPLES], Wk, xsT, c * P)
                            last.then_inc(z["ks_ps"], 1)
                        pe.wait_ge(z["q_ready"], b + 1)
                        pe.wait_ge(z["k_ready"], b + 1)
                        pe.wait_ge(z["v_ready"], b + 1)
                        if sparse:
                            pe.wait_ge(z["ks_ready"], b + 1)
                            for g in range(4):
                                rows = slice(g * GROUP_ROWS, (g + 1) * GROUP_ROWS)
                                out = bank((A, Bk)[g // 2], g % 2).rearrange("p a s -> p (a s)")
                                for t in range(ST):
                                    for c in range(DC):
                                        for odd in range(2):
                                            at = ((t * DC + c) * 2 + odd) * SAMPLES
                                            last = pe.matmul(out[:, at:at + SAMPLES],
                                                             qrows[odd][rows, c, t * P:(t + 1) * P], ksT[rows, c, :],
                                                             start=True, stop=True)
                                last.then_inc(z["ss_ps"], 1)
                            for kb in range(ST):
                                last = pe.matmul(Dk[:, 2, :], sh.ones[:], vr[:, kb, :, :].rearrange("p h d -> p (h d)"),
                                                 start=(kb == 0), stop=(kb == ST - 1))
                            last.then_inc(z["mean_ps"], 1)
                            pe.wait_ge(z["stand_ready"], b + 1)
                            for t in range(ST):
                                last = pe.transpose(Dk[0:H, 0, t * P:(t + 1) * P], smax[:, t, :], sh.ident[:])
                            last.then_inc(z["m_ps"], 1)
                    else:
                        for c in range(DC):
                            last = project(pe, Bk[:, c, :], Wv, xT, c * P)
                        last.then_inc(z["v_ps"], 1)
                        for src, bd, dst, ready, done in ((qf, bd_q, Dk, z["q_ready"], z["ql_ps"]), (kf, bd_k, C, z["k_ready"], z["kl_ps"])):
                            pe.wait_ge(ready, b + 1)
                            for j in range(4):
                                last = pe.matmul(dst[:, j, :], bd[:, j % 2, :], src[:, j // 2, :], start=True, stop=True)
                            last.then_inc(done, 1)
                        pe.wait_ge(z["vf_ready"], b + 1)
                        vl_ps = Bk[:].rearrange("p (t a) s -> p t (a s)", t=ST)
                        for t in range(ST):
                            for c in range(DC):
                                last = pe.matmul(vl_ps[:, t, c * D:(c + 1) * D], vf[:, c, t * P:(t + 1) * P], bd_kv[:],
                                                 start=True, stop=True)
                        last.then_inc(z["vl_ps"], 1)
                        for src, dst, ready, done in ((ql, A, z["ql_ready"], z["rq_ps"]), (kl, Dk, z["kl_ready"], z["rk_ps"])):
                            pe.wait_ge(ready, b + 1)
                            for j in range(4):
                                last = pe.matmul(dst[:, j, :], rot[:], src[:, j, :], start=True, stop=True)
                            last.then_inc(done, 1)
                        pe.wait_ge(z["qr_ready"], b + 1)
                        for j in range(4):
                            last = pe.matmul(C[:, j, :], bd_qk[:], qr[:, j, :], start=True, stop=True)
                        last.then_inc(z["qk_ps"], 1)
                        pe.wait_ge(z["qq_ready"], b + 1)
                        pe.wait_ge(z["kr_ready"], b + 1)
                        pe.wait_ge(z["vl_ready"], b + 1)
                    for h in range(2):
                        scores(h, b)
                    for h in range(H):
                        turn_probs(h, b)
                        if h + 2 < H:
                            scores(h + 2, b)
                        if h >= 1:
                            values(h - 1, b)
                    values(H - 1, b)
                    if sparse:
                        pe.wait_ge(z["rows_ready"], b + 1)
                        for t in range(ST):
                            last = pe.transpose(Dk[:, 0, t * P:(t + 1) * P], mrow[:, t * P:(t + 1) * P], sh.ident[:])
                        last.then_inc(z["kept_ps"], 1)
                    pe.wait_ge(z["ctx_ready"], b + 1)
                    for t in range(ST):
                        for j in range(H * V // P):
                            last = pe.transpose(A[:, j, t * P:(t + 1) * P],
                                                ctxv[:, t, :, :].rearrange("p h v -> p (h v)")[:, j * P:(j + 1) * P],
                                                sh.ident[:])
                    last.then_inc(z["cT_ps"], 1)
                    pe.wait_ge(z["cT_ready"], b + 1)
                    if latent:
                        for c in range(DC):
                            for j in range(2):
                                last = pe.matmul(Bk[:, c, :], bd_o[:, j, :], cT[:, 2 * c + j, :], start=(j == 0),
                                                 stop=(j == 1))
                        last.then_inc(z["y_ps"], 1)
                        pe.wait_ge(z["y_ready"], b + 1)
                    for t in range(ST):
                        last = project_rows(pe, Dk[:, 2 + t, :], yT if latent else cT, Wo, t)
                    last.then_inc(z["out_ps"], 1)

            @block.scalar
            def _(a):
                def exps(h, b):
                    a.wait_ge(z["neg_ready"], b * H + h + 1)
                    for t in range(ST):
                        src = sm[h % 2][:, t, :] if latent or decayed else A[:, 2 * (h % 2) + t, :]
                        last = a.activation(pr[h % 2][:, t, :], src, ACT.Exp, bias=negmax[:, h, t:t + 1],
                                            accum_out=rsum[:, t, h:h + 1])
                    a.drain().then_inc(z["exp_ready"], 1)

                def copy_turned(h, b):
                    a.wait_ge(z["pT_ps"], b * H + h + 1)
                    a.copy(prT[h % 2][:], bank(Bk, h % 2)).then_inc(z["pT_ready"], 1)

                if latent:
                    a.wait_ge(z["bd_in"], 16 * BD_DMAS)
                a.wait_ge(z["w_in"], 16 * n_w)
                with a.Fori(0, B) as b:
                    a.wait_ge(z["turned"], b + 1)
                    a.copy(xT[:], bank(Dk, 0)).then_inc(z["xT_ready"], 1)
                    if sparse:
                        a.wait_ge(z["xs_ps"], b + 1)
                        a.copy(xsT[:], C[:, 0:2, 0:SAMPLES]).then_inc(z["xs_ready"], 1)
                    if latent:
                        for dst, src, off, bias, came, done in (
                                (qf, A, 0, bq, z["q_ps"], z["q_ready"]), (kf, A, 2, bk, z["k_ps"], z["k_ready"]),
                                (vf, Bk, 0, bvf, z["v_ps"], z["vf_ready"])):
                            a.wait_ge(came, b + 1)
                            for c in range(DC):
                                last = a.activation(dst[:, c, :], src[:, off + c, :], ACT.Identity, bias=bias[:, c:c + 1])
                            last.then_inc(done, 1)
                        for dst, src, bias, came, done in (
                                (ql, Dk, bl_q, z["ql_ps"], z["ql_ready"]), (kl, C, bl_k, z["kl_ps"], z["kl_ready"]),
                                (qq, C, bl_qk, z["qk_ps"], z["qq_ready"])):
                            a.wait_ge(came, b + 1)
                            a.activation(dst[:], src[:], ACT.Identity, bias=bias[:, 0:1]).then_inc(done, 1)
                    else:
                        a.wait_ge(z["k_ps"], b + 1)
                        for c in range(DC):
                            last = a.activation(kT[:, c, :], A[:, 2 + c, :], ACT.Identity, bias=bk[:, c:c + 1])
                        last.then_inc(z["k_ready"], 1)
                        if sparse:
                            a.wait_ge(z["ks_ps"], b + 1)
                            for c in range(DC):
                                last = a.activation(ksT[:, c, :], C[:, 2 + c, 0:SAMPLES], ACT.Identity, bias=bk[:, c:c + 1])
                            last.then_inc(z["ks_ready"], 1)
                            a.wait_ge(z["mean_ps"], b + 1)
                            a.activation(meanv[:], Dk[:, 2, :], ACT.Identity, scale=1.0 / S)
                    exps(0, b)
                    for h in range(H):
                        if h + 1 < H:
                            exps(h + 1, b)
                        if latent or decayed:
                            copy_turned(h, b)
                    a.wait_ge(z["cT_ps"], b + 1)
                    a.copy(cT[:], A[:, 0:H * V // P, :]).then_inc(z["cT_ready"], 1)
                    if latent:
                        a.wait_ge(z["y_ps"], b + 1)
                        a.activation(yT[:], Bk[:, 0:DC, :], ACT.Identity, bias=bl_o[:, 0:1]).then_inc(z["y_ready"], 1)

            @block.vector
            def _(v):
                def row_max(h, b):
                    v.wait_ge(z["s_ps"], b * H + h + 1)
                    src = bank(A, h % 2)
                    if latent:
                        v.scalar_tensor_tensor(sm[h % 2][:], src, float(LAT) ** -0.5, mask[:], ALU.mult, ALU.add)
                        v.drain()
                        src = sm[h % 2][:]
                    if decayed:
                        v.tensor_tensor(sm[h % 2][:], src, masks[:, h, :, :], ALU.mult)
                        v.drain()
                        src = sm[h % 2][:]
                    v.tensor_reduce(negmax[:, h, :], src, AXX, ALU.max, negate=True).then_inc(z["neg_ready"], 1)

                def copy_turned(h, b):
                    v.wait_ge(z["pT_ps"], b * H + h + 1)
                    v.tensor_copy(prT[h % 2][:], bank(Bk, h % 2)).then_inc(z["pT_ready"], 1)

                v.wait_ge(z["w_in"], 16 * n_w)
                if latent:
                    v.wait_ge(z["bd_in"], 16 * BD_DMAS)
                    v.wait_ge(z["masks_ready"], 1)
                else:
                    v.wait_ge(z["masks_ready"], 16 * CONST_DMAS)
                if sparse:
                    v.memset(mrow[:], 0.0)
                    v.wait_ge(z["iotas"], 1)
                    v.tensor_copy(idx_f[:], idx_i[:])
                    v.drain()
                    v.tensor_scalar(neg_i[:], idx_f[:], 0.0, float(S), ALU.is_lt, ALU.mult)
                    v.drain()
                    v.tensor_tensor(idx_f[:], idx_f[:], neg_i[:], ALU.add)
                    v.drain()
                    v.tensor_scalar(idx_f[:], idx_f[:], 0.0, float(S - 1), ALU.max, ALU.min)
                    v.drain()
                    for t in range(ST):
                        v.tensor_scalar(pick[:, t, :], idx_f[:], tok[:, t:t + 1], None, ALU.is_equal)
                    v.drain().then_inc(z["pick_ready"], 1)
                with v.Fori(0, B) as b:
                    normed(v, lambda t: sh.h[:, ds(b * ST + t, 1), :], xn, stats, mv, rstd, z["var"], z["rst"], b + 1)
                    v.tensor_tensor(sh.h[:, ds(b * ST, ST), :], sh.h[:, ds(b * ST, ST), :], bc(bo[:], [P, ST, D]), ALU.add)
                    v.drain().then_inc(z["xn_ready"], 1)
                    if latent:
                        for ps_, lat, out, came, have, done in (
                                (A, ql, qr, z["rq_ps"], z["ql_ready"], z["qr_ready"]), (Dk, kl, kr, z["rk_ps"], z["kl_ready"], z["kr_ready"])):
                            v.wait_ge(have, b + 1)
                            v.tensor_tensor(t1[:], lat[:], bc(cos[:], [P, 4, S]), ALU.mult)
                            v.wait_ge(came, b + 1)
                            v.tensor_tensor(out[:], ps_[:], bc(sin[:], [P, 4, S]), ALU.mult)
                            v.drain()
                            v.tensor_tensor(out[:], out[:], t1[:], ALU.add)
                            v.drain().then_inc(done, 1)
                        v.wait_ge(z["vl_ps"], b + 1)
                        v.tensor_tensor(vl[:].rearrange("p t h l -> p (t h) l"),
                                        Bk[:].rearrange("p a (h l) -> p (a h) l", l=LAT),
                                        bc(bl_v[:], [P, ST * H, LAT]), ALU.add).then_inc(z["vl_ready"], 1)
                    else:
                        v.wait_ge(z["q_ps"], b + 1)
                        for i, q in enumerate((qe, qo)):
                            for c in range(DC):
                                v.tensor_scalar(q[:, c, :], A[:, c, :], bq[:, c:c + 1], parity[:, i:i + 1], ALU.add, ALU.mult)
                        v.drain().then_inc(z["q_ready"], 1)
                        v.wait_ge(z["v_ps"], b + 1)
                        v.tensor_tensor(vr[:].rearrange("p t h d -> p t (h d)"), Bk[:, 0:2, :], bc(bv[:], [P, ST, D]),
                                        ALU.add).then_inc(z["v_ready"], 1)
                    if sparse:
                        for g in range(4):
                            v.wait_ge(z["ss_ps"], b * 4 + g + 1)
                            src = bank((A, Bk)[g // 2], g % 2).rearrange("p a s -> p (a s)")[
                                :, 0:ST * 4 * SAMPLES].rearrange("p (t h u) -> p t h u", t=ST, u=SAMPLES)
                            by_group = lambda m: m[:].rearrange("p t (c g o) -> p g t c o", g=4, o=2)[:, g]
                            for t in range(ST):
                                v.tensor_reduce(by_group(smax)[:, t], src[:, t].rearrange("p (c o) u -> p c o u", o=2), AXX, ALU.max)
                                v.tensor_reduce(by_group(ssum)[:, t], src[:, t].rearrange("p (c o) u -> p c o u", o=2), AXX, ALU.add)
                        v.drain()
                        v.scalar_tensor_tensor(smax[:], ssum[:], -1.0 / SAMPLES, smax[:], ALU.mult, ALU.add)
                        v.drain().then_inc(z["stand_ready"], 1)
                    row_max(0, b)
                    for h in range(H):
                        if h + 1 < H:
                            row_max(h + 1, b)
                        if sparse:
                            copy_turned(h, b)
                            if h == 1:
                                v.wait_ge(z["m_ps"], b + 1)
                                v.tensor_copy(mwork[:], Dk[0:H, 0, :])
                                v.drain()
                            if 2 <= h < 2 + SAMPLES // 8:
                                v.max(best8[:], mwork[:])
                                v.drain()
                                v.match_replace(mwork[:], best8[:], mwork[:], NEG)
                                v.drain()
                            if h == 2 + SAMPLES // 8:
                                v.tensor_scalar(mrow[0:H, :], mwork[:], NEG, None, ALU.is_equal).then_inc(z["rows_ready"], 1)
                    v.wait_ge(z["o_ps"], b + 1)
                    v.reciprocal(rden[:], rsum[:])
                    v.drain()
                    v.tensor_tensor(ctxv[:], ctx_ps, rden[:].unsqueeze(3).broadcast_to([P, ST, H, V]), ALU.mult)
                    v.drain()
                    if sparse:
                        v.wait_ge(z["kept_ps"], b + 1)
                        v.tensor_copy(kept[:], Dk[:, 0, :].rearrange("p (t n) -> p t n", t=ST)[:, :, 0:H])
                        v.drain()
                        v.tensor_scalar(unkept[:], kept[:], -1.0, 1.0, ALU.mult, ALU.add)
                        v.drain()
                        v.tensor_tensor(ctxv[:], ctxv[:], kept[:].unsqueeze(3).broadcast_to([P, ST, H, V]), ALU.mult)
                        v.tensor_tensor(mv_part[:], meanv[:].rearrange("p (h d) -> p h d", h=H).unsqueeze(1).broadcast_to(
                            [P, ST, H, V]), unkept[:].unsqueeze(3).broadcast_to([P, ST, H, V]), ALU.mult)
                        v.drain()
                        v.tensor_tensor(ctxv[:], ctxv[:], mv_part[:], ALU.add)
                    v.drain().then_inc(z["ctx_ready"], 1)
                    v.wait_ge(z["out_ps"], b + 1)
                    v.tensor_tensor(sh.h[:, ds(b * ST, ST), :], sh.h[:, ds(b * ST, ST), :], Dk[:, 2:4, :], ALU.add)
                    v.drain()


def capacity_experts(nc, sh, buf, obuf, c_fc, c_proj):
    F = c_fc.shape[2] // DC
    FC = F // P
    CB = CAP // P
    HALF = CAP // 2
    GB = 3
    GROUPS = 2 * FC
    with ExitStack() as ctx, Signals(nc) as signals:
        sb = lambda n, shape, dt=F32: ctx.enter_context(nc.sbuf_tensor("x2_" + n, shape, dt))
        ps = lambda n, shape, dt=F32: ctx.enter_context(nc.psum_tensor("x2_" + n, shape, dt))
        sem = lambda n: signals("x2_" + n)
        wf = [sb(f"wf{p}", [P, DC, F]) for p in range(2)]
        wp = [sb(f"wp{p}", [P, FC, D]) for p in range(2)]
        xin = [sb(f"xin{p}", [P, CB, D]) for p in range(2)]
        xT = [sb(f"xT{p}", [P, DC, CAP]) for p in range(2)]
        hT = sb("hT", [P, FC, CAP])
        r = [sb(f"r{i}", [P, HALF]) for i in range(GB)]
        y = [sb(f"y{p}", [P, CB, D]) for p in range(2)]
        p_t = [ps(f"p_t{c}", [P, 4, P]) for c in range(DC + 1)]
        p_g = [ps(f"p_g{i}", [P, 512]) for i in range(GB)]
        p_o = [ps(f"p_o{i}", [P, D]) for i in range(2)]
        x_in, wf_in, wp_in, stored = ([sem(f"{n}{p}") for p in range(2)] for n in ("x_in", "wf_in", "wp_in", "stored"))
        turned, xT_ready, g_ready, relu_ready, h_ready, o_ready, y_ready = (
            sem(n) for n in ("turned", "xT_ready", "g_ready", "relu_ready", "h_ready", "o_ready", "y_ready"))
        rows = lambda m, e: m[ds(e * CAP, CAP), :].rearrange("(p t) d -> p t d", t=CB)
        with nc.Block() as block:
            @block.sync
            def _(sp):
                def load(e, p, reused):
                    if reused:
                        sp.wait_ge(turned, e - 1)
                    sp.dma_start(xin[p][:], rows(buf, e)).then_inc(x_in[p], 16)
                    if reused:
                        sp.wait_ge(o_ready, e * CB - CB)
                    sp.dma_start(wf[p][:].rearrange("p c n -> p (c n)"), c_fc[ds(e, 1), :, :].rearrange("a p n -> (a p) n")
                                 ).then_inc(wf_in[p], 16)
                    sp.dma_start(wp[p][:].rearrange("p c n -> p (c n)"), c_proj[ds(e, 1), :, :].rearrange("a p n -> (a p) n")
                                 ).then_inc(wp_in[p], 16)

                for p in range(2):
                    load(p, p, False)
                with sp.Fori(1, E // 2) as k:
                    for p in range(2):
                        load(k * 2 + p, p, True)

            @block.tensor
            def _(pe):
                def turn_rows(k, p):
                    pe.wait_ge(x_in[p], k * 16 + 16)
                    for c in range(DC):
                        for t in range(CB):
                            out = p_t[c][:, t, :] if t < 4 else p_t[DC][:, c, :]
                            last = pe.transpose(out, xin[p][:, t, c * P:(c + 1) * P], sh.ident[:])
                    last.then_inc(turned, 1)

                def expert(e, k, p, ahead):
                    pe.wait_ge(xT_ready, e + 1)
                    pe.wait_ge(wf_in[p], k * 16 + 16)
                    for n in range(GROUPS):
                        f, half = n // 2, n % 2
                        if n >= GB:
                            pe.wait_ge(relu_ready, e * GROUPS + n - GB + 1)
                        for c in range(DC):
                            last = pe.matmul(p_g[n % GB][:, 0:HALF], wf[p][:, c, f * P:(f + 1) * P],
                                             xT[p][:, c, half * HALF:(half + 1) * HALF], start=(c == 0), stop=(c == DC - 1))
                        last.then_inc(g_ready, 1)
                    if ahead:
                        turn_rows(k + p, 1 - p)
                    pe.wait_ge(h_ready, e * GROUPS + GROUPS)
                    pe.wait_ge(wp_in[p], k * 16 + 16)
                    for t in range(CB):
                        if t >= 2:
                            pe.wait_ge(y_ready, e * CB + t - 1)
                        for f in range(FC):
                            last = pe.matmul(p_o[t % 2][:], hT[:, f, t * P:(t + 1) * P], wp[p][:, f, :],
                                             start=(f == 0), stop=(f == FC - 1))
                        last.then_inc(o_ready, 1)

                turn_rows(0, 0)
                with pe.Fori(0, E // 2 - 1) as k:
                    for p in range(2):
                        expert(k * 2 + p, k, p, True)
                for p in range(2):
                    expert(E - 2 + p, E // 2 - 1, p, p == 0)

            @block.scalar
            def _(a):
                def copy_turned(e, p):
                    a.wait_ge(turned, e + 1)
                    for c in range(DC):
                        a.copy(xT[p][:, c, 0:4 * P], p_t[c][:].rearrange("p t n -> p (t n)"))
                    a.copy(xT[p][:, :, 4 * P:CAP], p_t[DC][:, 0:DC, :]).then_inc(xT_ready, 1)

                def store(e, p):
                    a.wait_ge(y_ready, e * CB + CB)
                    a.dma_start(rows(obuf, e), y[p][:]).then_inc(stored[p], 16)

                def expert(e, p, first, ahead):
                    for n in range(GROUPS):
                        a.wait_ge(g_ready, e * GROUPS + n + 1)
                        if n >= GB:
                            a.wait_ge(h_ready, e * GROUPS + n - GB + 1)
                        a.activation(r[n % GB][:], p_g[n % GB][:, 0:HALF], ACT.Relu).then_inc(relu_ready, 1)
                    if ahead:
                        copy_turned(e + 1, 1 - p)
                    if not first:
                        store(e - 1, 1 - p)

                copy_turned(0, 0)
                expert(0, 0, True, True)
                expert(1, 1, False, True)
                with a.Fori(1, E // 2 - 1) as k:
                    for p in range(2):
                        expert(k * 2 + p, p, False, True)
                for p in range(2):
                    expert(E - 2 + p, p, False, p == 0)
                store(E - 1, 1)
                for p in range(2):
                    a.wait_ge(stored[p], 16 * (E // 2))

            @block.vector
            def _(v):
                def expert(e, k, p, reused):
                    for n in range(GROUPS):
                        f, half = n // 2, n % 2
                        v.wait_ge(relu_ready, e * GROUPS + n + 1)
                        v.tensor_tensor(hT[:, f, half * HALF:(half + 1) * HALF], r[n % GB][:], r[n % GB][:], ALU.mult
                                        ).then_inc(h_ready, 1)
                    if reused:
                        v.wait_ge(stored[p], k * 16)
                    for t in range(CB):
                        v.wait_ge(o_ready, e * CB + t + 1)
                        v.tensor_copy(y[p][:, t, :], p_o[t % 2][:]).then_inc(y_ready, 1)

                for p in range(2):
                    expert(p, 0, p, False)
                with v.Fori(1, E // 2) as k:
                    for p in range(2):
                        expert(k * 2 + p, k, p, True)


def quantised_ffn(nc, sh, w_gate, w_up, w_down):
    F = w_gate.shape[1]
    FC = F // P
    QA = 127.0
    with ExitStack() as ctx, Signals(nc) as signals:
        sb = lambda n, shape, dt=F32: ctx.enter_context(nc.sbuf_tensor("q_" + n, shape, dt))
        ps = lambda n, shape, dt=F32: ctx.enter_context(nc.psum_tensor("q_" + n, shape, dt))
        sem = lambda n: signals("q_" + n)
        shapes = {"gate": [P, DC, F], "up": [P, DC, F], "down": [P, FC, D]}
        wf = {n: sb(n, s) for n, s in shapes.items()}
        wq = {n: sb(n + "q", s, BF16) for n, s in shapes.items()}
        asum, wmean, wscale = sb("asum", [P, 3]), sb("wmean", [P, 3]), sb("wscale", [P, 3])
        stats, mv, rstd = sb("stats", [P, ST, 6]), sb("mv", [P, ST, 2]), sb("rstd", [P, ST, 1])
        xn = sb("xn", [P, ST, D])
        amax, rscale, gscale, uscale = (sb(n, [P, ST]) for n in ("amax", "rscale", "gscale", "uscale"))
        xq = sb("xq", [P, ST, D], BF16)
        xqT = sb("xqT", [P, DC, S], BF16)
        sg = [sb(f"sg{t}", [P, F]) for t in range(ST)]
        pmax, pscale, dscale = (sb(n, [P, ST]) for n in ("pmax", "pscale", "dscale"))
        pq = [sb(f"pq{t}", [P, F], BF16) for t in range(ST)]
        pqT = [sb(f"pqT{t}", [P, FC, P], BF16) for t in range(ST)]
        p_small = ps("p_small", [P, 512])
        p_x = ps("p_x", [P, DC, S], BF16)
        p_g, p_u = ps("p_g", [P, F]), ps("p_u", [P, F])
        p_pT = ps("p_pT", [P, FC, P], BF16)
        p_d = ps("p_d", [P, D])
        w_in, asum_ready, wsum_ready, var, rst = (sem(n) for n in ("w_in", "asum_ready", "wsum_ready", "var", "rst"))
        wq_ready, xq_ready, turned, xT_ready, g_ready, u_ready, sg_ready, pq_ready, pT_ps, pT_ready, d_ready = (
            sem(n) for n in ("wq_ready", "xq_ready", "turned", "xT_ready", "g_ready", "u_ready", "sg_ready",
                             "pq_ready", "pT_ps", "pT_ready", "d_ready"))
        scales_ready = sem("scales_ready")
        flat = lambda x: x[:].rearrange("p c n -> p (c n)")
        with nc.Block() as block:
            @block.sync
            def _(sp):
                for n, src in (("gate", w_gate), ("up", w_up), ("down", w_down)):
                    sp.dma_start(wf[n][:], kxn(src)).then_inc(w_in, 16)

            @block.gpsimd
            def _(g):
                with g.Fori(0, B) as b:
                    rstd_of(g, sh, mv, rstd, var, rst, b + 1)

            @block.tensor
            def _(pe):
                pe.wait_ge(asum_ready, 1)
                pe.matmul(p_small[:, 0:3], sh.ones[:], asum[:], start=True, stop=True).then_inc(wsum_ready, 1)
                pe.wait_ge(wq_ready, 1)
                with pe.Fori(0, B) as b:
                    pe.wait_ge(xq_ready, b + 1)
                    turn(pe, p_x, xq, sh.identb[:]).then_inc(turned, 1)
                    pe.wait_ge(xT_ready, b + 1)
                    for t in range(ST):
                        if t:
                            pe.wait_ge(pq_ready, b * ST + t)
                        for dst, n, done in ((p_g, "gate", g_ready), (p_u, "up", u_ready)):
                            for f in range(0, F, 512):
                                for c in range(DC):
                                    last = pe.matmul(dst[:, f:f + 512], xqT[:, c, t * P:(t + 1) * P],
                                                     wq[n][:, c, f:f + 512], start=(c == 0), stop=(c == DC - 1))
                            last.then_inc(done, 1)
                        pe.wait_ge(pq_ready, b * ST + t + 1)
                        for f in range(FC):
                            last = pe.transpose(p_pT[:, f, :], pq[t][:, f * P:(f + 1) * P], sh.identb[:])
                        last.then_inc(pT_ps, 1)
                        pe.wait_ge(pT_ready, b * ST + t + 1)
                        for f in range(FC):
                            last = pe.matmul(p_d[:], pqT[t][:, f, :], wq["down"][:, f, :], start=(f == 0), stop=(f == FC - 1))
                        last.then_inc(d_ready, 1)

            @block.scalar
            def _(a):
                a.preload_act_table(ACT.Silu)
                with a.Fori(0, B) as b:
                    a.wait_ge(turned, b + 1)
                    a.copy(xqT[:], p_x[:]).then_inc(xT_ready, 1)
                    a.wait_ge(scales_ready, b + 1)
                    for t in range(ST):
                        a.wait_ge(g_ready, b * ST + t + 1)
                        a.activation(sg[t][:], p_g[:], ACT.Silu, scale=gscale[:, t:t + 1]).then_inc(sg_ready, 1)
                        a.wait_ge(pT_ps, b * ST + t + 1)
                        a.copy(pqT[t][:], p_pT[:]).then_inc(pT_ready, 1)

            @block.vector
            def _(v):
                v.wait_ge(w_in, 48)
                for i, n in enumerate(("gate", "up", "down")):
                    v.tensor_reduce(asum[:, i:i + 1], flat(wf[n]), AXX, ALU.add, apply_absolute_value=True)
                v.drain().then_inc(asum_ready, 1)
                v.wait_ge(wsum_ready, 1)
                v.tensor_scalar(wmean[:], p_small[:, 0:3], 1.0 / (D * F), 1e-5, ALU.mult, ALU.max)
                v.drain()
                v.reciprocal(wscale[:], wmean[:])
                v.drain()
                for i, n in enumerate(("gate", "up", "down")):
                    v.tensor_scalar(flat(wf[n]), flat(wf[n]), wscale[:, i:i + 1], ROUND, ALU.mult, ALU.add)
                v.drain()
                for n in ("gate", "up", "down"):
                    v.tensor_scalar(flat(wf[n]), flat(wf[n]), ROUND, 1.0, ALU.subtract, ALU.min)
                v.drain()
                for n in ("gate", "up", "down"):
                    v.tensor_scalar(flat(wq[n]), flat(wf[n]), -1.0, None, ALU.max)
                v.drain().then_inc(wq_ready, 1)
                with v.Fori(0, B) as b:
                    normed(v, lambda t: sh.h[:, ds(b * ST + t, 1), :], xn, stats, mv, rstd, var, rst, b + 1)
                    v.tensor_reduce(amax[:], xn[:], AXX, ALU.max, apply_absolute_value=True)
                    v.drain()
                    v.tensor_scalar(amax[:], amax[:], 1e-5, 1.0 / QA, ALU.max, ALU.mult)
                    v.drain()
                    v.reciprocal(rscale[:], amax[:])
                    v.tensor_scalar(gscale[:], amax[:], wmean[:, 0:1], None, ALU.mult)
                    v.tensor_scalar(uscale[:], amax[:], wmean[:, 1:2], None, ALU.mult)
                    v.drain().then_inc(scales_ready, 1)
                    for t in range(ST):
                        v.tensor_scalar(xn[:, t, :], xn[:, t, :], rscale[:, t:t + 1], ROUND, ALU.mult, ALU.add)
                    v.drain()
                    v.tensor_scalar(xq[:], xn[:], ROUND, QA, ALU.subtract, ALU.min).then_inc(xq_ready, 1)
                    for t in range(ST):
                        v.wait_ge(sg_ready, b * ST + t + 1)
                        v.wait_ge(u_ready, b * ST + t + 1)
                        v.scalar_tensor_tensor(sg[t][:], p_u[:], uscale[:, t:t + 1], sg[t][:], ALU.mult, ALU.mult)
                        v.drain()
                        v.tensor_reduce(pmax[:, t:t + 1], sg[t][:], AXX, ALU.max, apply_absolute_value=True)
                        v.drain()
                        v.tensor_scalar(pmax[:, t:t + 1], pmax[:, t:t + 1], 1e-5, 1.0 / QA, ALU.max, ALU.mult)
                        v.drain()
                        v.reciprocal(pscale[:, t:t + 1], pmax[:, t:t + 1])
                        v.tensor_scalar(dscale[:, t:t + 1], pmax[:, t:t + 1], wmean[:, 2:3], None, ALU.mult)
                        v.drain()
                        v.tensor_scalar(sg[t][:], sg[t][:], pscale[:, t:t + 1], ROUND, ALU.mult, ALU.add)
                        v.drain()
                        v.tensor_scalar(pq[t][:], sg[t][:], ROUND, QA, ALU.subtract, ALU.min).then_inc(pq_ready, 1)
                        v.wait_ge(d_ready, b * ST + t + 1)
                        v.scalar_tensor_tensor(sh.h[:, ds(b * ST + t, 1), :], p_d[:].unsqueeze(1), dscale[:, t:t + 1],
                                               sh.h[:, ds(b * ST + t, 1), :], ALU.mult, ALU.add)
                    v.drain()


def tower(nc, a, out):
    buf = nc.dram_tensor("slots", (SLOTS + K * T, D), F32).ap()
    obuf = nc.dram_tensor("slot_results", (SLOTS, D), F32).ap()
    with ExitStack() as ctx:
        sh = Shared()
        setup_constants(nc, ctx, sh)
        clear_slots(nc, sh, buf)
        embedding(nc, sh, a["x"], a["L0_tok_weight"])
        time_and_channel_mix(nc, sh, {n: a["L0_attn_" + n] for n in (
            "Wr", "Ww", "Wk", "Wv", "Wo", "Wrec", "Wkey", "Wval", "time_decay", "ln1_g", "ln1_b", "ln2_g", "ln2_b")})
        with ExitStack() as moe:
            routing_state(nc, moe, sh, "s0")
            route(nc, sh, "r0", a["L0_ffn_gate_w"], "sigmoid", a["L0_ffn_expert_bias"])
            dispatch(nc, sh, "d0", buf, True, 1)
            expert_tiles(nc, sh, "x0", buf, obuf, a["L0_ffn_experts"], SHARED_TILES + ROUTED_TILES, True)
            combine(nc, sh, "c0", obuf, 1)
        attention(nc, sh, "a1", "latent", {n: a["L1_attn_" + n] for n in (
            "c_attn_w", "c_attn_b", "q2l_w", "q2l_b", "kv2l_w", "kv2l_b", "l2o_w", "l2o_b", "wqk_w", "wqk_b",
            "cproj_w", "cproj_b", "rot", "cos", "sin")})
        with ExitStack() as moe:
            routing_state(nc, moe, sh, "s1")
            route(nc, sh, "r1", a["L1_ffn_router_w"], "softmax")
            dispatch(nc, sh, "d1", buf, False, 0)
            expert_tiles(nc, sh, "x1", buf, obuf, a["L1_ffn_experts"], ROUTED_TILES, False, a["L1_ffn_b_out"])
            combine(nc, sh, "c1", obuf, 0)
        attention(nc, sh, "a2", "sparse", {n: a["L2_attn_" + n] for n in (
            "Wq", "bq", "Wk", "bk", "Wv", "bv", "Wo", "bo", "idx_k")} | {"parity": a["parity"]})
        with ExitStack() as moe:
            routing_state(nc, moe, sh, "s2")
            route(nc, sh, "r2", a["L2_ffn_w_g"], "softmax2")
            dispatch(nc, sh, "d2", buf, False, 0)
            capacity_experts(nc, sh, buf, obuf, a["L2_ffn_c_fc"], a["L2_ffn_c_proj"])
            combine(nc, sh, "c2", obuf, 0)
        with nc.sbuf_tensor("masks", [P, H, ST, S], F32) as masks:
            decay_masks(nc, sh, masks, a["L3_attn_decay_params"], a["L3_attn_mix_weights"])
            attention(nc, sh, "a3", "decay", {n: a["L3_attn_" + n] for n in (
                "Wq", "bq", "Wk", "bk", "Wv", "bv", "Wo", "bo")} | {"parity": a["parity"], "masks": masks})
        quantised_ffn(nc, sh, a["L3_ffn_w_gate"], a["L3_ffn_w_up"], a["L3_ffn_w_down"])
        store_out(nc, sh, out)


_TURNED = ["L0_attn_Wr", "L0_attn_Ww", "L0_attn_Wk", "L0_attn_Wv", "L0_attn_Wo", "L0_attn_Wkey", "L0_attn_Wval",
           "L0_attn_Wrec", "L0_ffn_gate_w", "L1_attn_c_attn_w", "L1_attn_q2l_w", "L1_attn_kv2l_w", "L1_attn_l2o_w",
           "L1_attn_wqk_w", "L1_attn_cproj_w", "L2_attn_Wq", "L2_attn_Wk", "L2_attn_Wv", "L2_attn_Wo", "L2_ffn_w_g",
           "L3_attn_Wq", "L3_attn_Wk", "L3_attn_Wv", "L3_attn_Wo", "L3_ffn_w_gate", "L3_ffn_w_up", "L3_ffn_w_down"]
_AS_IS = ["x", "L0_tok_weight", "L0_attn_ln1_g", "L0_attn_ln1_b", "L0_attn_ln2_g", "L0_attn_ln2_b",
          "L0_attn_time_decay", "L0_ffn_expert_bias", "L1_attn_c_attn_b", "L1_attn_q2l_b", "L1_attn_kv2l_b",
          "L1_attn_l2o_b", "L1_attn_wqk_b", "L1_attn_cproj_b", "L1_ffn_router_w", "L1_ffn_b_out",
          "L2_attn_bq", "L2_attn_bk", "L2_attn_bv", "L2_attn_bo", "L2_attn_idx_k", "L3_attn_bq", "L3_attn_bk",
          "L3_attn_bv", "L3_attn_bo", "L3_attn_decay_params", "L3_attn_mix_weights"]


def _chunked(*mats):
    parts = [m.reshape(m.shape[0], -1, 128, m.shape[2]).transpose(0, 2, 1, 3).reshape(m.shape[0], 128, -1)
             for m in mats]
    return np.ascontiguousarray(np.concatenate(parts, axis=2))


def kernel(**inputs):
    import concourse.bacc as bacc
    from concourse.bass_utils import run_bass_kernel_spmd as run

    nc = bacc.Bacc("TRN2", target_bir_lowering=False, num_devices=1)
    a = {n: np.asarray(v) for n, v in inputs.items()}
    turned = lambda m: np.swapaxes(m, -1, -2)
    arrays = {}
    for name in _AS_IS:
        arrays[name] = np.ascontiguousarray(a[name])
    for name in _TURNED:
        arrays[name] = np.ascontiguousarray(turned(a[name]))
    arrays["L0_ffn_experts"] = _chunked(*(turned(np.concatenate([a[f"L0_ffn_w{m}"], a[f"L0_ffn_sw{m}"][None]]))
                                          for m in (1, 3, 2)))
    b_in = a["L1_ffn_b_in"].reshape(E, DC, P).transpose(0, 2, 1)
    arrays["L1_ffn_experts"] = np.ascontiguousarray(np.concatenate(
        [_chunked(a["L1_ffn_w_in"], a["L1_ffn_w_out"]), b_in], axis=2))
    arrays["L2_ffn_c_fc"] = _chunked(a["L2_ffn_c_fc"])
    arrays["L2_ffn_c_proj"] = _chunked(a["L2_ffn_c_proj"])
    pair = np.arange(P) % LAT // 2
    angle = (np.arange(S, dtype=np.float32)[None, :]
             * (1.0 / 10000.0 ** (2.0 * pair / LAT)).astype(np.float32)[:, None]).astype(np.float32)
    arrays["L1_attn_cos"] = np.cos(angle).astype(np.float32)
    arrays["L1_attn_sin"] = np.sin(angle).astype(np.float32)
    swap = np.zeros((P, P), np.float32)
    even = np.arange(0, P, 2)
    swap[even + 1, even], swap[even, even + 1] = -1.0, 1.0
    arrays["L1_attn_rot"] = swap
    odd = (np.arange(P) // HD % 2).astype(bool)
    arrays["parity"] = np.where(np.stack([~odd, odd], axis=1), np.float32(HD ** -0.5), np.float32(0.0))
    handles = {n: nc.dram_tensor(n, v.shape, mybir.dt.from_np(v.dtype), kind="ExternalInput").ap()
               for n, v in arrays.items()}
    out = nc.dram_tensor("out", (B, S, D), F32, kind="ExternalOutput").ap()
    tower(nc, handles, out)
    result = run(nc, [arrays], core_ids=[0])
    return result.results[0]["out"]
```

```python
from contextlib import ExitStack

import numpy as np

import concourse.bass as bass
from concourse import mybir

F32 = mybir.dt.float32
BF16 = mybir.dt.bfloat16
I32 = mybir.dt.int32
U32 = mybir.dt.uint32
ALU = mybir.AluOpType
ACT = mybir.ActivationFunctionType
AXX = mybir.AxisListType.X
ds = bass.ds

P = 128
D = 256
DC = D // P
B = 8
S = 256
ST = S // P
T = B * S
NT = T // P
LN_EPS = 1e-5
ROUND = 1.5 * 2.0 ** 23


class Shared:
    pass


class Signals:

    def __init__(self, nc):
        self.nc, self.held = nc, []

    def __call__(self, name):
        self.held.append(self.nc.alloc_semaphore(name))
        return self.held[-1]

    def __enter__(self):
        return self

    def __exit__(self, *failed):
        if not failed[0]:
            self.nc.clear_and_free_semaphores(self.held)
            self.nc.all_engine_barrier()
        return False


def bc(ap, shape):
    return ap.unsqueeze(1).broadcast_to(shape)


def row_ap(vec, parts=P):
    return vec.partition_broadcast(parts)


def col_ap(vec):
    return vec.rearrange("(c p) -> p c", p=P)


def kxn(w):
    return w.rearrange("(c p) n -> p c n", p=P)


def normed(v, src, out, stats, mv, rstd, var_sem, rstd_sem, count):
    for t in range(ST):
        v.bn_stats(stats[:, t, :], src(t))
    v.drain()
    for t in range(ST):
        v.bn_aggr(mv[:, t, :], stats[:, t, :])
    v.drain()
    v.tensor_scalar(mv[:, :, 1:2], mv[:, :, 1:2], LN_EPS, None, ALU.add).then_inc(var_sem, 1)
    v.wait_ge(rstd_sem, count)
    for t in range(ST):
        v.tensor_scalar(out[:, t, :], src(t), mv[:, t, 0:1], rstd[:, t, 0:1], ALU.subtract, ALU.mult)
    v.drain()


def rstd_of(g, sh, mv, rstd, var_sem, rstd_sem, count):
    g.wait_ge(var_sem, count)
    g.tensor_tensor(rstd[:], mv[:, :, 1:2], sh.minus_half[:], ALU.pow).then_inc(rstd_sem, 1)


def turn(pe, out, src, ident):
    for c in range(DC):
        for t in range(ST):
            last = pe.transpose(out[:, c, t * P:(t + 1) * P], src[:, t, c * P:(c + 1) * P], ident)
    return last


def project(pe, out, w, xT, m0, m=P):
    chunks = xT.shape[1]
    for c in range(chunks):
        last = pe.matmul(out, w[:, c, m0:m0 + m], xT[:, c, :], start=(c == 0), stop=(c == chunks - 1))
    return last


def project_rows(pe, out, xT, w, t):
    chunks = xT.shape[1]
    for c in range(chunks):
        last = pe.matmul(out, xT[:, c, t * P:(t + 1) * P], w[:, c, :], start=(c == 0), stop=(c == chunks - 1))
    return last


def setup_constants(nc, ctx, sh):
    sb = lambda name, shape, dt=F32: ctx.enter_context(nc.sbuf_tensor(name, shape, dt))
    sh.h = sb("h", [P, NT, D])
    sh.ident = sb("ident", [P, P])
    sh.identb = sb("identb", [P, P], BF16)
    sh.ones = sb("ones", [P, P])
    sh.above = sb("above", [P, P])
    sh.minus_half = sb("minus_half", [P, ST, 1])
    filled = nc.alloc_semaphore("filled")
    with nc.Block() as block:
        @block.gpsimd
        def _(g):
            g.memset(sh.ident[:], 0.0)
            g.memset(sh.identb[:], 0.0)
            g.memset(sh.ones[:], 1.0)
            g.memset(sh.above[:], 1.0)
            g.memset(sh.minus_half[:], -0.5)
            g.drain().then_inc(filled, 1)
            g.wait_ge(filled, 1)
            for m in (sh.ident, sh.identb):
                g.affine_select(out=m[:], in_=m[:], compare_op=ALU.not_equal, fill=1.0, base=0,
                                pattern=[[-1, P]], channel_multiplier=1)
            g.affine_select(out=sh.above[:], in_=sh.above[:], compare_op=ALU.is_gt, fill=0.0, base=0,
                            pattern=[[1, P]], channel_multiplier=-1)

        @block.scalar
        def _(a):
            a.preload_act_table(ACT.Exp)


def embedding(nc, sh, x, table, load_next):
    BLK, QMAX, PART = 32, 31.0, 4
    NB = PART * D // BLK
    with ExitStack() as ctx, Signals(nc) as signals:
        sb = lambda name, shape, dt=F32: ctx.enter_context(nc.sbuf_tensor(name, shape, dt))
        ids = sb("e_ids", [P, NT], I32)
        raw = sb("e_raw", [P, NT, D])
        amax = sb("e_amax", [P, NB])
        scale = sb("e_scale", [P, NB])
        safe = sb("e_safe", [P, NB])
        inv = sb("e_inv", [P, NB])
        q = sb("e_q", [P, NB, BLK])
        ids_in = signals("e_ids_in")
        rows_in = [signals(f"e_rows_in{k}") for k in range(NT // PART)]
        next_in = signals("e_next_in")
        with nc.Block() as block:
            @block.sync
            def _(sp):
                sp.dma_start(ids[:], x.rearrange("b (t p) -> p (b t)", p=P),
                             allow_slow_non_contiguous=True).then_inc(ids_in, 16)
                sp.wait_ge(next_in, 16 * load_next(sp, next_in))

            @block.gpsimd
            def _(g):
                g.wait_ge(ids_in, 16)
                for t in range(NT):
                    g.indirect_dma_start(out=raw[:, t, :], out_offset=None, in_=table,
                                         in_offset=bass.IndirectOffsetOnAxis(ap=ids[:, t:t + 1].bitcast(U32), axis=0)
                                         ).then_inc(rows_in[t // PART], 16)

            @block.vector
            def _(v):
                for k in range(NT // PART):
                    rows = raw[:, k * PART:(k + 1) * PART, :].rearrange("p t (n j) -> p (t n) j", j=BLK)
                    out = sh.h[:, k * PART:(k + 1) * PART, :].rearrange("p t (n j) -> p (t n) j", j=BLK)
                    v.wait_ge(rows_in[k], 16 * PART)
                    v.tensor_reduce(amax[:], rows, AXX, ALU.max, apply_absolute_value=True)
                    v.drain()
                    v.tensor_scalar(scale[:], amax[:], 1.0 / QMAX, None, ALU.mult)
                    v.drain()
                    v.scalar_tensor_tensor(safe[:], scale[:], 0.0, scale[:], ALU.is_equal, ALU.add)
                    v.drain()
                    v.reciprocal(inv[:], safe[:])
                    v.drain()
                    v.tensor_tensor(q[:], rows, inv[:].unsqueeze(2).broadcast_to([P, NB, BLK]), ALU.mult)
                    v.drain()
                    v.tensor_scalar(q[:], q[:], ROUND, ROUND, ALU.add, ALU.subtract)
                    v.drain()
                    v.tensor_scalar(q[:], q[:], QMAX, -QMAX, ALU.min, ALU.max)
                    v.drain()
                    v.tensor_tensor(out, q[:], scale[:].unsqueeze(2).broadcast_to([P, NB, BLK]), ALU.mult)
                    v.drain()


def time_mix_weights(nc, ctx, w):
    F = w["Wkey"].shape[1]
    sb = lambda name, shape: ctx.enter_context(nc.sbuf_tensor("a0_" + name, shape, F32))
    W = {n: sb(n, [P, DC, D]) for n in ("Wr", "Ww", "Wk", "Wv", "Wo", "Wrec")}
    W["Wkey"] = sb("Wkey", [P, DC, F])
    W["Wval"] = sb("Wval", [P, F // P, D])
    W |= {n: sb(n, [P, D]) for n in ("ln1_g", "ln1_b", "ln2_g", "ln2_b")}
    W["time_decay"] = sb("tdecay", [P, DC])
    return W


def load_time_mix(sp, W, w, w_in):
    sp.dma_start(W["time_decay"][:], col_ap(w["time_decay"]), allow_slow_non_contiguous=True).then_inc(w_in, 16)
    for n in ("ln1_g", "ln1_b", "ln2_g", "ln2_b"):
        sp.dma_start(W[n][:], row_ap(w[n])).then_inc(w_in, 16)
    for n in ("Ww", "Wk", "Wr", "Wv", "Wo", "Wkey", "Wrec", "Wval"):
        sp.dma_start(W[n][:], kxn(w[n])).then_inc(w_in, 16)
    return len(W)


def time_and_channel_mix(nc, sh, W, buf):
    FC = W["Wval"].shape[1]
    with ExitStack() as ctx, Signals(nc) as signals:
        sb = lambda name, shape, dt=F32: ctx.enter_context(nc.sbuf_tensor("a0_" + name, shape, dt))
        ps = lambda name, shape, dt=F32: ctx.enter_context(nc.psum_tensor("a0_" + name, shape, dt))
        sem = lambda name: signals("a0_" + name)
        decay = sb("decay", [P, DC])
        decays = sb("decays", [P, DC, S])
        zeros = sb("zeros", [P, 8, D])
        stats, mv, rstd = sb("stats", [P, ST, 6]), sb("mv", [P, ST, 2]), sb("rstd", [P, ST, 1])
        x0 = sb("x0", [P, NT, D])
        x1 = sb("x1", [P, ST, D])
        xn1, xn2 = sb("xn1", [P, ST, D]), sb("xn2", [P, ST, D])
        xT1, xT2 = sb("xT1", [P, DC, S]), sb("xT2", [P, DC, S])
        tr, ew, e, ev = (sb(n, [P, DC, S]) for n in ("tr", "ew", "e", "ev"))
        wk, num, den = sb("wk", [P, DC, S]), sb("num", [P, DC, S]), sb("den", [P, DC, S])
        rw = sb("rw", [P, DC, S])
        kr = sb("kr", [P, FC, S])
        ksq = sb("ksq", [P, FC, S])
        trec = sb("trec", [P, ST, D])
        cm = sb("cm", [P, ST, D])
        turned1, turned2 = ps("turned1", [P, DC, S]), ps("turned2", [P, DC, S])
        p_w, p_k, p_r, p_v = (ps(n, [P, DC, S]) for n in ("p_w", "p_k", "p_r", "p_v"))
        p_orec, p_val = ps("p_orec", [P, ST, D]), ps("p_val", [P, ST, D])
        p_key = (p_w, p_r, p_k, p_v)
        var, rst, decay_ready = sem("var"), sem("rst"), sem("decay_ready")
        xn1_ready, xn2_ready, turned1_ready, turned2_ready, xT1_ready, xT2_ready = (
            sem(n) for n in ("xn1_ready", "xn2_ready", "turned1_ready", "turned2_ready", "xT1_ready", "xT2_ready"))
        proj_ready, ew_ready, kw_ready, e_ready, tr_ready, ev_ready, rw_ready = (
            sem(n) for n in ("proj_ready", "ew_ready", "kw_ready", "e_ready", "tr_ready", "ev_ready", "rw_ready"))
        o_ready, key_ready, ksq_ready, rec_ready, trec_ready, val_ready = (
            sem(n) for n in ("o_ready", "key_ready", "ksq_ready", "rec_ready", "trec_ready", "val_ready"))
        zeroed, cleared = sem("zeroed"), sem("cleared")
        PAIRS = FC // 2
        with nc.Block() as block:
            @block.sync
            def _(sp):
                sp.wait_ge(zeroed, 1)
                n = SLOTS // (P * 8)
                for j in range(n):
                    sp.dma_start(buf[j * P * 8:(j + 1) * P * 8, :].rearrange("(p r) d -> p r d", p=P),
                                 zeros[:]).then_inc(cleared, 16)
                sp.wait_ge(cleared, 16 * n)

            @block.gpsimd
            def _(g):
                g.memset(zeros[:], 0.0).then_inc(zeroed, 1)
                for k in range(4):
                    rstd_of(g, sh, mv, rstd, var, rst, k + 1)
                with g.Fori(0, B - 2) as i:
                    for k in range(3):
                        rstd_of(g, sh, mv, rstd, var, rst, i * 3 + 5 + k)
                for k in range(2):
                    rstd_of(g, sh, mv, rstd, var, rst, (B - 2) * 3 + 5 + k)

            @block.tensor
            def _(pe):
                def turn_first(j):
                    pe.wait_ge(xn1_ready, j + 1)
                    turn(pe, turned1, xn1, sh.ident[:]).then_inc(turned1_ready, 1)

                def products(bank, name, xT):
                    for c in range(DC):
                        last = project(pe, bank[:, c, :], W[name], xT, c * P)
                    last.then_inc(proj_ready, 1)

                def turn_second(i):
                    pe.wait_ge(xn2_ready, i + 1)
                    turn(pe, turned2, xn2, sh.ident[:]).then_inc(turned2_ready, 1)

                def step(i, first=False, ahead=True):
                    if ahead:
                        turn_first(i + 1)
                    pe.wait_ge(rw_ready, i + 1)
                    if not first:
                        pe.wait_ge(trec_ready, i)
                    for t in range(ST):
                        last = project_rows(pe, p_orec[:, t, :], rw, W["Wo"], t)
                    last.then_inc(o_ready, 1)
                    if ahead:
                        pe.wait_ge(xT1_ready, i + 2)
                        products(p_w, "Ww", xT1)
                        products(p_k, "Wk", xT1)
                        products(p_r, "Wr", xT1)
                    turn_second(i)
                    if ahead:
                        products(p_v, "Wv", xT1)
                    pe.wait_ge(xT2_ready, i + 1)
                    read = (ew_ready, tr_ready, kw_ready, ev_ready)
                    for j in range(PAIRS):
                        if ahead:
                            pe.wait_ge(read[j], i + 2)
                        for c in range(2):
                            last = project(pe, p_key[j][:, c, :], W["Wkey"], xT2, (2 * j + c) * P)
                        last.then_inc(key_ready, 1)
                    for t in range(ST):
                        last = project_rows(pe, p_orec[:, t, :], xT2, W["Wrec"], t)
                    last.then_inc(rec_ready, 1)
                    pe.wait_ge(ksq_ready, i * PAIRS + PAIRS)
                    for t in range(ST):
                        last = project_rows(pe, p_val[:, t, :], ksq, W["Wval"], t)
                    last.then_inc(val_ready, 1)

                turn_first(0)
                pe.wait_ge(xT1_ready, 1)
                for bank, name in ((p_w, "Ww"), (p_k, "Wk"), (p_r, "Wr"), (p_v, "Wv")):
                    products(bank, name, xT1)
                step(0, first=True)
                with pe.Fori(1, B - 1) as i:
                    step(i)
                step(B - 1, ahead=False)

            @block.scalar
            def _(a):
                def time_mix(j):
                    a.wait_ge(turned1_ready, j + 1)
                    a.copy(xT1[:], turned1[:]).then_inc(xT1_ready, 1)
                    a.wait_ge(proj_ready, j * 4 + 1)
                    a.activation(ew[:], p_w[:], ACT.Exp).then_inc(ew_ready, 1)
                    a.wait_ge(kw_ready, j + 1)
                    a.activation(e[:], wk[:], ACT.Exp).then_inc(e_ready, 1)
                    a.wait_ge(proj_ready, j * 4 + 3)
                    a.activation(tr[:], p_r[:], ACT.Tanh, scale=0.5).then_inc(tr_ready, 1)

                def channel_mix(i):
                    a.wait_ge(turned2_ready, i + 1)
                    a.copy(xT2[:], turned2[:]).then_inc(xT2_ready, 1)
                    for j in range(PAIRS):
                        a.wait_ge(key_ready, i * PAIRS + j + 1)
                        pair = slice(2 * j, 2 * j + 2)
                        a.activation(kr[:, pair, :], p_key[j][:], ACT.Relu)
                        a.drain()
                        a.activation(ksq[:, pair, :], kr[:, pair, :], ACT.Square).then_inc(ksq_ready, 1)
                    a.wait_ge(rec_ready, i + 1)
                    a.activation(trec[:], p_orec[:], ACT.Tanh, scale=0.5).then_inc(trec_ready, 1)

                a.activation(decay[:], W["time_decay"][:], ACT.Exp).then_inc(decay_ready, 1)
                time_mix(0)
                with a.Fori(0, B - 1) as i:
                    time_mix(i + 1)
                    channel_mix(i)
                channel_mix(B - 1)

            @block.vector
            def _(v):
                def moments(src):
                    for t in range(ST):
                        v.bn_stats(stats[:, t, :], src(t))
                    v.drain()
                    for t in range(ST):
                        v.bn_aggr(mv[:, t, :], stats[:, t, :])
                    v.drain()
                    v.tensor_scalar(mv[:, :, 1:2], mv[:, :, 1:2], LN_EPS, None, ALU.add).then_inc(var, 1)

                def normed_with_gain(out, src, gain, bias, count):
                    moments(src)
                    for t in range(ST):
                        v.scalar_tensor_tensor(out[:, t, :], src(t), mv[:, t, 0:1], gain[:], ALU.subtract, ALU.mult)
                    v.drain()
                    v.wait_ge(rst, count)
                    for t in range(ST):
                        v.scalar_tensor_tensor(out[:, t, :], out[:, t, :], rstd[:, t, 0:1], bias[:], ALU.mult, ALU.add)

                def first_norms(j, count):
                    x = lambda t: x0[:, ds(j * ST + t, 1), :]
                    src = lambda t: sh.h[:, ds(j * ST + t, 1), :]
                    moments(src)
                    v.wait_ge(rst, count)
                    for t in range(ST):
                        v.tensor_scalar(x(t), src(t), mv[:, t, 0:1], rstd[:, t, 0:1], ALU.subtract, ALU.mult)
                    v.drain()
                    moments(x)
                    for t in range(ST):
                        v.scalar_tensor_tensor(xn1[:, t:t + 1, :], x(t), mv[:, t, 0:1], W["ln1_g"][:].unsqueeze(1),
                                               ALU.subtract, ALU.mult)
                    v.drain()
                    v.wait_ge(rst, count + 1)
                    for t in range(ST):
                        last = v.scalar_tensor_tensor(xn1[:, t, :], xn1[:, t, :], rstd[:, t, 0:1], W["ln1_b"][:],
                                                      ALU.mult, ALU.add)
                    v.drain().then_inc(xn1_ready, 1)

                def time_mix(j):
                    v.wait_ge(ew_ready, j + 1)
                    v.wait_ge(proj_ready, j * 4 + 2)
                    v.tensor_tensor(wk[:], p_k[:], ew[:], ALU.subtract).then_inc(kw_ready, 1)
                    v.wait_ge(e_ready, j + 1)
                    for c in range(DC):
                        v.tensor_tensor_scan(den[:, c, :], decays[:, c, :], e[:, c, :], 0.0, ALU.mult, ALU.add)
                    v.drain()
                    v.tensor_scalar(den[:], den[:], 1e-8, None, ALU.add)
                    v.drain()
                    v.reciprocal(den[:], den[:])
                    v.wait_ge(proj_ready, j * 4 + 4)
                    v.tensor_tensor(ev[:], p_v[:], e[:], ALU.mult).then_inc(ev_ready, 1)
                    v.drain()
                    for c in range(DC):
                        v.tensor_tensor_scan(num[:, c, :], decays[:, c, :], ev[:, c, :], 0.0, ALU.mult, ALU.add)
                    v.drain()
                    v.tensor_tensor(num[:], num[:], den[:], ALU.mult)
                    v.drain()
                    v.wait_ge(tr_ready, j + 1)
                    v.scalar_tensor_tensor(rw[:], tr[:], 1.0, num[:], ALU.add, ALU.mult).then_inc(rw_ready, 1)

                def step(i, count, ahead=True, norms=True):
                    v.wait_ge(o_ready, i + 1)
                    v.scalar_tensor_tensor(x1[:], p_orec[:], 0.5, x0[:, ds(i * ST, ST), :], ALU.mult, ALU.add)
                    v.drain()
                    normed_with_gain(xn2, lambda t: x1[:, t, :], W["ln2_g"], W["ln2_b"], count)
                    v.drain().then_inc(xn2_ready, 1)
                    if ahead:
                        time_mix(i + 1)
                    v.tensor_tensor(x1[:], x1[:], sh.h[:, ds(i * ST, ST), :], ALU.add)
                    if norms:
                        first_norms(i + 2, count + 1)
                    v.wait_ge(trec_ready, i + 1)
                    v.wait_ge(val_ready, i + 1)
                    v.scalar_tensor_tensor(cm[:], trec[:], 1.0, p_val[:], ALU.add, ALU.mult)
                    v.drain()
                    v.scalar_tensor_tensor(sh.h[:, ds(i * ST, ST), :], cm[:], 0.5, x1[:], ALU.mult, ALU.add)
                    v.drain()

                first_norms(0, 1)
                v.wait_ge(decay_ready, 1)
                for c in range(DC):
                    v.tensor_copy(decays[:, c, :], decay[:, c:c + 1].broadcast_to([P, S]))
                v.drain()
                time_mix(0)
                first_norms(1, 3)
                with v.Fori(0, B - 2) as i:
                    step(i, i * 3 + 5)
                step(B - 2, (B - 2) * 3 + 5, norms=False)
                step(B - 1, (B - 2) * 3 + 6, ahead=False, norms=False)


def store_out(nc, sh, out):
    with ExitStack() as ctx, Signals(nc) as signals:
        stored = signals("stored")
        with nc.Block() as block:
            @block.sync
            def _(sp):
                for k in range(2):
                    half = slice(k * NT // 2, (k + 1) * NT // 2)
                    sp.dma_start(out.rearrange("b (t p) d -> p (b t) d", p=P)[:, half, :], sh.h[:, half, :]).then_inc(stored, 16)
                sp.wait_ge(stored, 32)


E = 8
K = 2
TILE = 256
TB = TILE // P
KT = K * NT
SHARED_TILES = T // TILE
ROUTED_TILES = K * T // TILE + E
CAP = 640
SLOTS = (SHARED_TILES + ROUTED_TILES) * TILE
TRASH = SLOTS


def routing_state(nc, ctx, sh, name):
    sb = lambda n, shape, dt=F32: ctx.enter_context(nc.sbuf_tensor(f"{name}_{n}", shape, dt))
    sh.xn_all = sb("xn_all", [P, NT, D])
    sh.slot = sb("slot", [P, KT], I32)
    sh.back = sb("back", [P, KT], I32)
    sh.weight = sb("weight", [P, KT])
    sh.tile_expert = sb("tile_expert", [1, SHARED_TILES + ROUTED_TILES], I32)


def route(nc, sh, name, gate, kind, bias=None):
    with ExitStack() as ctx, Signals(nc) as signals:
        sb = lambda n, shape, dt=F32: ctx.enter_context(nc.sbuf_tensor(f"{name}_{n}", shape, dt))
        ps = lambda n, shape, dt=F32: ctx.enter_context(nc.psum_tensor(f"{name}_{n}", shape, dt))
        sem = lambda n: signals(f"{name}_{n}")
        gw = sb("gw", [P, DC, E])
        bias_row = sb("bias", [P, E])
        stats, mv, rstd, xn, xT = ([sb(f"{n}{p}", shape) for p in range(2)] for n, shape in (
            ("stats", [P, ST, 6]), ("mv", [P, ST, 2]), ("rstd", [P, ST, 1]), ("xn", [P, ST, D]), ("xT", [P, DC, S])))
        logits = sb("logits", [P, NT, E])
        sel = sb("sel", [P, NT, E])
        val = sb("val", [P, NT, E])
        tmp = sb("tmp", [P, NT, E])
        best = sb("best", [P, NT])
        idx = sb("idx", [P, E])
        idx8 = sb("idx8", [P, E])
        oh = sb("oh", [P, E, KT])
        ohk = sb("ohk", [P, NT, E])
        w2 = sb("w2", [P, K, NT])
        total, incl, pos, big = (sb(n, [P, E, KT]) for n in ("total", "incl", "pos", "big"))
        reset = sb("reset", [P, E, KT])
        one8 = sb("one8", [P, E])
        base, tiles, ends = sb("base", [P, E]), sb("tiles", [P, E]), sb("ends", [P, E])
        rank, ebase, valid, trash, tf = (sb(n, [P, KT]) for n in ("rank", "ebase", "valid", "trash", "tf"))
        tidx = sb("tidx", [1, ROUTED_TILES])
        tcmp = sb("tcmp", [1, ROUTED_TILES, E])
        texp = sb("texp", [1, ROUTED_TILES])
        turned = [ps(f"turned{p}", [P, DC, S]) for p in range(2)]
        p_logit = ps("p_logit", [P, NT, E])
        p_rank, p_total = ps("p_rank", [P, E, KT]), ps("p_total", [P, E, KT])
        w_in, var, rst, consts = sem("w_in"), sem("var"), sem("rst"), sem("consts")
        xn_ready, xn_free, turned_ready, xT_ready, logit_ready, oh_ready, count_ready, soft, softed = (
            sem(n) for n in ("xn_ready", "xn_free", "turned_ready", "xT_ready", "logit_ready", "oh_ready",
                             "count_ready", "soft", "softed"))
        with nc.Block() as block:
            @block.sync
            def _(sp):
                sp.dma_start(gw[:], gate.rearrange("(c p) e -> p c e", p=P),
                             allow_slow_non_contiguous=True).then_inc(w_in, 16)
                if bias is not None:
                    sp.dma_start(bias_row[:], row_ap(bias)).then_inc(w_in, 16)

            @block.gpsimd
            def _(g):
                g.iota(idx[:], [[1, E]], base=0, channel_multiplier=0, allow_small_or_imprecise_dtypes=True)
                g.iota(idx8[:], [[1, E]], base=E, channel_multiplier=0, allow_small_or_imprecise_dtypes=True)
                g.iota(tidx[:], [[1, ROUTED_TILES]], base=0, channel_multiplier=0, allow_small_or_imprecise_dtypes=True)
                g.iota(base[:], [[CAP, E]], base=0, channel_multiplier=0, allow_small_or_imprecise_dtypes=True)
                g.iota(trash[:], [[P, KT]], base=TRASH, channel_multiplier=1, allow_small_or_imprecise_dtypes=True)
                g.memset(one8[:], 1.0)
                g.memset(reset[:, :, 1:KT], 1.0)
                g.memset(reset[:, :, 0:1], 0.0)
                g.drain().then_inc(consts, 1)
                with g.Fori(0, B // 2) as k:
                    for p in range(2):
                        rstd_of(g, sh, mv[p], rstd[p], var, rst, k * 2 + p + 1)

            @block.tensor
            def _(pe):
                pe.wait_ge(w_in, 16 if bias is None else 32)
                with pe.Fori(0, B // 2) as k:
                    for p in range(2):
                        pe.wait_ge(xn_ready, k * 2 + p + 1)
                        turn(pe, turned[p], xn[p], sh.ident[:]).then_inc(turned_ready, 1)
                    for p in range(2):
                        pe.wait_ge(xT_ready, k * 2 + p + 1)
                        for t in range(ST):
                            out = p_logit[:, ds(k * 2 * ST + p * ST + t, 1), :].rearrange("p a e -> p (a e)")
                            last = project_rows(pe, out, xT[p], gw, t)
                        last.then_inc(logit_ready, 1)
                pe.wait_ge(oh_ready, 1)
                pe.matmul(p_rank[:], sh.above[:], oh[:], start=True, stop=True)
                pe.matmul(p_total[:], sh.ones[:], oh[:], start=True, stop=True).then_inc(count_ready, 1)

            @block.scalar
            def _(a):
                a.drain().then_inc(xn_free, 2)
                with a.Fori(0, B // 2) as k:
                    for p in range(2):
                        a.wait_ge(turned_ready, k * 2 + p + 1)
                        a.copy(xT[p][:], turned[p][:]).then_inc(xT_ready, 1)
                        a.copy(sh.xn_all[:, ds(k * 2 * ST + p * ST, ST), :], xn[p][:]).then_inc(xn_free, 1)
                a.wait_ge(soft, 1)
                a.activation(tmp[:], tmp[:], ACT.Exp).then_inc(softed, 1)

            @block.vector
            def _(v):
                with v.Fori(0, B // 2) as k:
                    rows = lambda p, t: sh.h[:, ds(k * 2 * ST + p * ST + t, 1), :]
                    for p in range(2):
                        for t in range(ST):
                            v.bn_stats(stats[p][:, t, :], rows(p, t))
                        v.drain()
                        for t in range(ST):
                            v.bn_aggr(mv[p][:, t, :], stats[p][:, t, :])
                        v.drain()
                        v.tensor_scalar(mv[p][:, :, 1:2], mv[p][:, :, 1:2], LN_EPS, None, ALU.add).then_inc(var, 1)
                    for p in range(2):
                        v.wait_ge(xn_free, k * 2 + p + 1)
                        v.wait_ge(rst, k * 2 + p + 1)
                        for t in range(ST):
                            last = v.tensor_scalar(xn[p][:, t:t + 1, :], rows(p, t), mv[p][:, t, 0:1], rstd[p][:, t, 0:1],
                                                   ALU.subtract, ALU.mult)
                        last.then_inc(xn_ready, 1)
                v.wait_ge(logit_ready, B)
                v.tensor_copy(logits[:], p_logit[:])
                v.drain()
                v.wait_ge(consts, 1)
                v.wait_ge(w_in, 16 if bias is None else 32)
                if kind == "sigmoid":
                    v.tensor_scalar(tmp[:], logits[:], -1.0, None, ALU.mult).then_inc(soft, 1)
                    v.wait_ge(softed, 1)
                    v.tensor_scalar(tmp[:], tmp[:], 1.0, None, ALU.add)
                    v.drain()
                    v.reciprocal(val[:], tmp[:])
                    v.drain()
                    v.tensor_tensor(sel[:], val[:], bc(bias_row[:], [P, NT, E]), ALU.add)
                elif kind == "softmax":
                    v.tensor_reduce(best[:], logits[:], AXX, ALU.max)
                    v.drain()
                    v.tensor_tensor(tmp[:], logits[:], best[:].unsqueeze(2).broadcast_to([P, NT, E]),
                                    ALU.subtract).then_inc(soft, 1)
                    v.wait_ge(softed, 1)
                    v.tensor_reduce(best[:], tmp[:], AXX, ALU.add)
                    v.drain()
                    v.reciprocal(best[:], best[:])
                    v.drain()
                    v.tensor_tensor(val[:], tmp[:], best[:].unsqueeze(2).broadcast_to([P, NT, E]), ALU.mult)
                    v.drain()
                    v.tensor_copy(sel[:], val[:])
                else:
                    v.tensor_copy(val[:], logits[:])
                    v.tensor_copy(sel[:], logits[:])
                for k in range(K):
                    v.drain()
                    v.tensor_reduce(best[:], sel[:], AXX, ALU.max)
                    v.drain()
                    v.tensor_tensor(ohk[:], sel[:], best[:].unsqueeze(2).broadcast_to([P, NT, E]), ALU.is_equal)
                    v.drain()
                    v.scalar_tensor_tensor(ohk[:], ohk[:], -float(E), bc(idx8[:], [P, NT, E]), ALU.mult, ALU.add)
                    v.drain()
                    v.tensor_reduce(best[:], ohk[:], AXX, ALU.min)
                    v.drain()
                    v.tensor_tensor(ohk[:], bc(idx[:], [P, NT, E]), best[:].unsqueeze(2).broadcast_to([P, NT, E]),
                                    ALU.is_equal)
                    v.drain()
                    v.tensor_copy(oh[:, :, k * NT:(k + 1) * NT].rearrange("p e t -> p t e"), ohk[:])
                    v.scalar_tensor_tensor(sel[:], ohk[:], -3e38, sel[:], ALU.mult, ALU.add)
                    v.tensor_tensor(ohk[:], ohk[:], val[:], ALU.mult)
                    v.drain()
                    v.tensor_reduce(w2[:, k, :], ohk[:], AXX, ALU.add)
                v.drain().then_inc(oh_ready, 1)
                if kind == "softmax2":
                    v.tensor_tensor(tmp[:, :, 0], w2[:, 1, :], w2[:, 0, :], ALU.subtract)
                    v.tensor_scalar(tmp[:, :, 1:E], logits[:, :, 1:E], 0.0, None, ALU.min)
                    v.drain().then_inc(soft, 1)
                    v.wait_ge(softed, 1)
                    v.tensor_scalar(best[:], tmp[:, :, 0], 1.0, None, ALU.add)
                    v.drain()
                    v.reciprocal(w2[:, 0, :], best[:])
                    v.drain()
                    v.tensor_tensor(w2[:, 1, :], w2[:, 0, :], tmp[:, :, 0], ALU.mult)
                    v.drain()
                v.wait_ge(count_ready, 1)
                v.tensor_copy(total[:], p_total[:])
                v.drain()
                flat = lambda x: x[:].rearrange("p e k -> p (e k)")
                v.tensor_tensor_scan(flat(incl), flat(reset), flat(total), 0.0, ALU.mult, ALU.add)
                v.drain()
                v.tensor_tensor(pos[:], incl[:], total[:], ALU.subtract)
                v.drain()
                v.tensor_tensor(pos[:], pos[:], p_rank[:], ALU.add)
                if kind != "softmax2":
                    v.tensor_scalar(tiles[:], incl[:, :, KT - 1], TILE / 2 - 0.5, 1.0 / TILE, ALU.add, ALU.mult)
                    v.drain()
                    v.tensor_scalar(tiles[:], tiles[:], ROUND, ROUND, ALU.add, ALU.subtract)
                    v.drain()
                    v.tensor_tensor_scan(ends[:], one8[:], tiles[:], 0.0, ALU.mult, ALU.add)
                    v.drain()
                    v.tensor_tensor(base[:], ends[:], tiles[:], ALU.subtract)
                    v.drain()
                    first = SHARED_TILES * TILE if kind == "sigmoid" else 0
                    v.tensor_scalar(base[:], base[:], float(TILE), float(first), ALU.mult, ALU.add)
                    v.tensor_tensor(tcmp[:], ends[0:1, :].unsqueeze(1).broadcast_to([1, ROUTED_TILES, E]),
                                    tidx[:].unsqueeze(2).broadcast_to([1, ROUTED_TILES, E]), ALU.is_le)
                    v.drain()
                    v.tensor_reduce(texp[:], tcmp[:], AXX, ALU.add)
                    v.drain()
                    v.tensor_scalar(texp[:], texp[:], float(E - 1), None, ALU.min)
                    v.drain()
                    if kind == "sigmoid":
                        v.memset(sh.tile_expert[:, 0:SHARED_TILES], E)
                        v.tensor_copy(sh.tile_expert[:, SHARED_TILES:], texp[:])
                    else:
                        v.tensor_copy(sh.tile_expert[:, 0:ROUTED_TILES], texp[:])
                by_choice = lambda x: x[:].rearrange("p e k -> p k e")
                v.drain()
                v.tensor_tensor(big[:], oh[:], pos[:], ALU.mult)
                v.drain()
                v.tensor_reduce(rank[:], by_choice(big), AXX, ALU.add)
                v.drain()
                v.tensor_tensor(big[:], oh[:], base[:].unsqueeze(2).broadcast_to([P, E, KT]), ALU.mult)
                v.drain()
                v.tensor_reduce(ebase[:], by_choice(big), AXX, ALU.add)
                v.drain()
                if kind == "softmax2":
                    v.tensor_scalar(valid[:], rank[:], float(CAP), None, ALU.is_lt)
                    v.tensor_tensor(tf[:], rank[:], ebase[:], ALU.add)
                    v.drain()
                    v.tensor_tensor(tf[:], tf[:], trash[:], ALU.subtract)
                    v.drain()
                    v.tensor_tensor(tf[:], tf[:], valid[:], ALU.mult)
                    v.drain()
                    v.tensor_tensor(tf[:], tf[:], trash[:], ALU.add)
                    v.drain()
                    v.tensor_copy(sh.slot[:], tf[:])
                    v.scalar_tensor_tensor(rank[:], rank[:], float(CAP - 1), ebase[:], ALU.min, ALU.add)
                    v.drain()
                    v.tensor_copy(sh.back[:], rank[:])
                    v.tensor_tensor(sh.weight[:], w2[:].rearrange("p k t -> p (k t)"), valid[:], ALU.mult)
                else:
                    v.tensor_tensor(tf[:], rank[:], ebase[:], ALU.add)
                    v.drain()
                    v.tensor_copy(sh.slot[:], tf[:])
                    v.tensor_copy(sh.back[:], tf[:])
                    v.tensor_copy(sh.weight[:], w2[:].rearrange("p k t -> p (k t)"))
                v.drain()


def dispatch(nc, sh, name, buf, scaled, shared):
    with ExitStack() as ctx, Signals(nc) as signals:
        sem = lambda n: signals(f"{name}_{n}")
        GROUP = 4
        xs = ctx.enter_context(nc.sbuf_tensor(f"{name}_xs", [P, KT, D], F32)) if scaled else None
        xs_ready = sem("xs_ready")
        sent, shared_sent = sem("sent"), sem("shared_sent")
        with nc.Block() as block:
            @block.gpsimd
            def _(g):
                for j in range(KT):
                    if scaled and j % GROUP == 0:
                        g.wait_ge(xs_ready, j // GROUP + 1)
                    src = xs[:, j, :] if scaled else sh.xn_all[:, j % NT, :]
                    g.indirect_dma_start(out=buf, out_offset=bass.IndirectOffsetOnAxis(
                        ap=sh.slot[:, j:j + 1].bitcast(U32), axis=0), in_=src, in_offset=None).then_inc(sent, 16)
                g.wait_ge(sent, 16 * KT)

            @block.sync
            def _(sp):
                if shared:
                    sp.dma_start(buf[0:T, :].rearrange("(t p) d -> p t d", p=P), sh.xn_all[:]).then_inc(shared_sent, 16)
                    sp.wait_ge(shared_sent, 16)

            @block.vector
            def _(v):
                if scaled:
                    for j in range(KT):
                        last = v.tensor_scalar(xs[:, j, :], sh.xn_all[:, j % NT, :], sh.weight[:, j:j + 1], None, ALU.mult)
                        if j % GROUP == GROUP - 1:
                            v.drain().then_inc(xs_ready, 1)


def combine(nc, sh, name, obuf, shared):
    with ExitStack() as ctx, Signals(nc) as signals:
        sem = lambda n: signals(f"{name}_{n}")
        GROUP = 4
        y = ctx.enter_context(nc.sbuf_tensor(f"{name}_y", [P, KT, D], F32))
        ysh = ctx.enter_context(nc.sbuf_tensor(f"{name}_ysh", [P, NT, D], F32)) if shared else None
        came = [sem(f"came{j}") for j in range(KT // GROUP)]
        shared_came = sem("shared_came")
        with nc.Block() as block:
            @block.gpsimd
            def _(g):
                for j in range(KT):
                    g.indirect_dma_start(out=y[:, j, :], out_offset=None, in_=obuf, in_offset=bass.IndirectOffsetOnAxis(
                        ap=sh.back[:, j:j + 1].bitcast(U32), axis=0)).then_inc(came[j // GROUP], 16)

            @block.sync
            def _(sp):
                if shared:
                    sp.dma_start(ysh[:], obuf[0:T, :].rearrange("(t p) d -> p t d", p=P)).then_inc(shared_came, 16)

            @block.vector
            def _(v):
                if shared:
                    v.wait_ge(shared_came, 16)
                    v.tensor_tensor(sh.h[:], sh.h[:], ysh[:], ALU.add)
                    v.drain()
                for j in range(KT):
                    if j % GROUP == 0:
                        v.wait_ge(came[j // GROUP], 16 * GROUP)
                    if j == NT:
                        v.drain()
                    v.scalar_tensor_tensor(sh.h[:, j % NT, :], y[:, j, :], sh.weight[:, j:j + 1], sh.h[:, j % NT, :],
                                           ALU.mult, ALU.add)
                v.drain()


def expert_tiles(nc, sh, name, buf, obuf, wts, n_tiles, gated, b_out=None):
    NM = 3 if gated else 2
    WCOLS = wts.shape[2]
    with ExitStack() as ctx, Signals(nc) as signals:
        sb = lambda n, shape, dt=F32: ctx.enter_context(nc.sbuf_tensor(f"{name}_{n}", shape, dt))
        ps = lambda n, shape, dt=F32: ctx.enter_context(nc.psum_tensor(f"{name}_{n}", shape, dt))
        sem = lambda n: signals(f"{name}_{n}")
        wbuf = [sb(f"w{p}", [P, WCOLS]) for p in range(2)]
        w1 = [w[:, 0:DC * D].rearrange("p (c n) -> p c n", c=DC) for w in wbuf]
        w3 = [w[:, DC * D:2 * DC * D].rearrange("p (c n) -> p c n", c=DC) for w in wbuf]
        w2 = [w[:, (NM - 1) * DC * D:NM * DC * D].rearrange("p (c n) -> p c n", c=DC) for w in wbuf]
        bo = [sb(f"bo{p}", [P, D]) for p in range(2)] if not gated else None
        xin = [sb(f"xin{p}", [P, TB, D]) for p in range(2)]
        xT = [sb(f"xT{p}", [P, DC, TILE]) for p in range(2)]
        sg = sb("sg", [P, DC, TILE])
        hT = sb("hT", [P, DC, TILE])
        y = [sb(f"y{p}", [P, TB, D]) for p in range(2)]
        p_t = [ps(f"p_t{p}", [P, DC, TILE]) for p in range(2)]
        p_g = [ps(f"p_g{p}", [P, DC, TILE]) for p in range(2)]
        p_u = [ps(f"p_u{p}", [P, DC, TILE]) for p in range(2)] if gated else None
        p_o = [ps(f"p_o{p}", [P, TB, D]) for p in range(2)]
        x_in = [sem(f"x_in{p}") for p in range(2)]
        w_in = [sem(f"w_in{p}") for p in range(2)]
        stored = [sem(f"stored{p}") for p in range(2)]
        turned, xT_ready, g_ready, u_ready, sg_ready, h_ready, o_ready, y_ready, bank_free = (
            sem(n) for n in ("turned", "xT_ready", "g_ready", "u_ready", "sg_ready", "h_ready", "o_ready", "y_ready",
                             "bank_free"))
        rows = lambda m, i: m[ds(i * TILE, TILE), :].rearrange("(p t) d -> p t d", t=TB)
        W_DMAS = 1 if gated else 2
        with nc.Block() as block:
            @block.sync
            def _(sp):
                def load(i, p):
                    e = sp.value_load(sh.tile_expert[0:1, ds(i, 1)], min_val=0, max_val=wts.shape[0] - 1)
                    sp.dma_start(wbuf[p][:], wts[ds(e, 1), :, :].rearrange("a p n -> (a p) n")).then_inc(w_in[p], 16)
                    if not gated:
                        sp.dma_start(bo[p][:], b_out[ds(e, 1), :].rearrange("a n -> (a n)").partition_broadcast(P)
                                     ).then_inc(w_in[p], 16)

                def load_x(i, p):
                    sp.dma_start(xin[p][:], rows(buf, i)).then_inc(x_in[p], 16)

                for p in range(2):
                    load_x(p, p)
                    load(p, p)
                with sp.Fori(1, n_tiles // 2) as k:
                    for p in range(2):
                        sp.wait_ge(turned, k * 2 + (p - 1))
                        load_x(k * 2 + p, p)
                        sp.wait_ge(o_ready, k * 2 + (p - 1))
                        if not gated:
                            sp.wait_ge(y_ready, k * 2 + (p - 1))
                        load(k * 2 + p, p)

            @block.tensor
            def _(pe):
                def turn_tile(i, k, p):
                    pe.wait_ge(x_in[p], k * 16 + 16)
                    turn(pe, p_t[p], xin[p], sh.ident[:]).then_inc(turned, 1)

                def tile(i, k, p, ahead):
                    pe.wait_ge(xT_ready, i + 1)
                    pe.wait_ge(w_in[p], k * (16 * W_DMAS) + 16 * W_DMAS)
                    for c in range(DC):
                        last = project(pe, p_g[p][:, c, :], w1[p], xT[p], c * P)
                    last.then_inc(g_ready, 1)
                    if gated:
                        for c in range(DC):
                            last = project(pe, p_u[p][:, c, :], w3[p], xT[p], c * P)
                        last.then_inc(u_ready, 1)
                    if ahead:
                        turn_tile(i + 1, k + p, 1 - p)
                    pe.wait_ge(h_ready, i + 1)
                    for t in range(TB):
                        last = project_rows(pe, p_o[p][:, t, :], hT, w2[p], t)
                    last.then_inc(o_ready, 1)

                turn_tile(0, 0, 0)
                with pe.Fori(0, n_tiles // 2 - 1) as k:
                    for p in range(2):
                        tile(k * 2 + p, k, p, True)
                for p in range(2):
                    tile(n_tiles - 2 + p, n_tiles // 2 - 1, p, p == 0)

            @block.scalar
            def _(a):
                def copy_turned(i, p):
                    a.wait_ge(turned, i + 1)
                    a.copy(xT[p][:], p_t[p][:]).then_inc(xT_ready, 1)

                def store(i, p):
                    a.wait_ge(y_ready, i + 1)
                    a.dma_start(rows(obuf, i), y[p][:]).then_inc(stored[p], 16)

                def tile(i, p, first, ahead):
                    a.wait_ge(g_ready, i + 1)
                    if gated:
                        a.activation(sg[:], p_g[p][:], ACT.Silu).then_inc(sg_ready, 1)
                    else:
                        for c in range(DC):
                            last = a.activation(hT[:, c, :], p_g[p][:, c, :], ACT.Gelu_apprx_tanh,
                                                bias=wbuf[p][:, 4 * D + c:4 * D + c + 1])
                        last.then_inc(h_ready, 1)
                    if ahead:
                        copy_turned(i + 1, 1 - p)
                    if not first:
                        store(i - 1, 1 - p)

                a.preload_act_table(ACT.Silu if gated else ACT.Gelu_apprx_tanh)
                copy_turned(0, 0)
                tile(0, 0, True, True)
                tile(1, 1, False, True)
                with a.Fori(1, n_tiles // 2 - 1) as k:
                    for p in range(2):
                        tile(k * 2 + p, p, False, True)
                for p in range(2):
                    tile(n_tiles - 2 + p, p, False, p == 0)
                store(n_tiles - 1, 1)
                for p in range(2):
                    a.wait_ge(stored[p], 16 * (n_tiles // 2))
                a.preload_act_table(ACT.Exp)

            @block.vector
            def _(v):
                def tile(i, k, p, reused):
                    if gated:
                        v.wait_ge(sg_ready, i + 1)
                        v.wait_ge(u_ready, i + 1)
                        v.tensor_tensor(hT[:], sg[:], p_u[p][:], ALU.mult).then_inc(h_ready, 1)
                    v.wait_ge(o_ready, i + 1)
                    if reused:
                        v.wait_ge(stored[p], k * 16)
                    if gated:
                        v.tensor_copy(y[p][:], p_o[p][:]).then_inc(y_ready, 1)
                    else:
                        v.tensor_tensor(y[p][:], p_o[p][:], bc(bo[p][:], [P, TB, D]), ALU.add).then_inc(y_ready, 1)

                for p in range(2):
                    tile(p, 0, p, False)
                with v.Fori(1, n_tiles // 2) as k:
                    for p in range(2):
                        tile(k * 2 + p, k, p, True)




H = 16
HD = D // H
LAT = 32
GROUP_ROWS = 32
NEG = -1e30
SAMPLES = 40


def decay_masks(nc, sh, masks, decay_params, mix_weights):
    N = 2
    with ExitStack() as ctx, Signals(nc) as signals:
        sb = lambda n, shape, dt=F32: ctx.enter_context(nc.sbuf_tensor("dm_" + n, shape, dt))
        sem = lambda n: signals("dm_" + n)
        dist, far = sb("dist", [P, ST, S]), sb("far", [P, ST, S])
        dp, lnd, mw, ex = sb("dp", [P, H * N]), sb("lnd", [P, H * N]), sb("mw", [P, H, N]), sb("ex", [P, H, N])
        top = sb("top", [P, H])
        powers = [sb(f"powers{n}", [P, ST, S]) for n in range(2)]
        came, iota_done, clipped, shifted, exped, logged, dist_ready, power_ready, power_used = (
            sem(n) for n in ("came", "iota_done", "clipped", "shifted", "exped", "logged", "dist_ready",
                             "power_ready", "power_used"))
        with nc.Block() as block:
            @block.sync
            def _(sp):
                sp.dma_start(dp[:], row_ap(decay_params.rearrange("h n -> (h n)"))).then_inc(came, 16)
                sp.dma_start(mw[:].rearrange("p h n -> p (h n)"), row_ap(mix_weights.rearrange("h n -> (h n)"))
                             ).then_inc(came, 16)

            @block.gpsimd
            def _(g):
                g.iota(dist[:], [[P, ST], [-1, S]], base=0, channel_multiplier=1,
                       allow_small_or_imprecise_dtypes=True).then_inc(iota_done, 1)

            @block.scalar
            def _(a):
                a.wait_ge(shifted, 1)
                a.activation(ex[:], mw[:], ACT.Exp).then_inc(exped, 1)
                a.wait_ge(clipped, 1)
                a.activation(lnd[:], dp[:], ACT.Ln).then_inc(logged, 1)
                a.wait_ge(logged, 1)
                a.wait_ge(dist_ready, 1)
                for j in range(H * N):
                    if j >= 2:
                        a.wait_ge(power_used, j - 1)
                    a.activation(powers[j % 2][:], dist[:], ACT.Exp, scale=lnd[:, j:j + 1]).then_inc(power_ready, 1)

            @block.vector
            def _(v):
                v.wait_ge(came, 32)
                v.tensor_scalar(dp[:], dp[:], 0.01, 0.9999, ALU.max, ALU.min).then_inc(clipped, 1)
                v.tensor_reduce(top[:], mw[:], AXX, ALU.max)
                v.drain()
                v.tensor_tensor(mw[:], mw[:], top[:].unsqueeze(2).broadcast_to([P, H, N]), ALU.subtract
                                ).then_inc(shifted, 1)
                v.wait_ge(iota_done, 1)
                v.tensor_scalar(far[:], dist[:], -1.0, None, ALU.mult)
                v.drain()
                v.tensor_tensor(dist[:], dist[:], far[:], ALU.max).then_inc(dist_ready, 1)
                v.wait_ge(exped, 1)
                v.tensor_reduce(top[:], ex[:], AXX, ALU.add)
                v.drain()
                v.reciprocal(top[:], top[:])
                v.drain()
                v.tensor_tensor(ex[:], ex[:], top[:].unsqueeze(2).broadcast_to([P, H, N]), ALU.mult)
                v.drain()
                for h in range(H):
                    v.wait_ge(power_ready, N * h + 1)
                    v.tensor_scalar(masks[:, h, :, :], powers[0][:], ex[:, h, 0:1], None, ALU.mult
                                    ).then_inc(power_used, 1)
                    v.wait_ge(power_ready, N * h + 2)
                    v.wait_ge(power_used, N * h + 1)
                    v.scalar_tensor_tensor(masks[:, h, :, :], powers[1][:], ex[:, h, 1:2], masks[:, h, :, :],
                                           ALU.mult, ALU.add).then_inc(power_used, 1)


def attention(nc, sh, name, kind, w):
    latent, sparse, decayed = kind == "latent", kind == "sparse", kind == "decay"
    V = LAT if latent else HD
    CC = H * V // P
    KEYS = [P * (t + 1) if latent else S for t in range(ST)]
    SCOL = [sum(KEYS[:t]) for t in range(ST)]
    SW = sum(KEYS)
    with ExitStack() as ctx, Signals(nc) as signals:
        sb = lambda n, shape, dt=F32: ctx.enter_context(nc.sbuf_tensor(f"{name}_{n}", shape, dt))
        ps = lambda n, shape, dt=F32: ctx.enter_context(nc.psum_tensor(f"{name}_{n}", shape, dt))
        sem = lambda n: signals(f"{name}_{n}")
        stats, mv, rstd = sb("stats", [P, ST, 6]), sb("mv", [P, ST, 2]), sb("rstd", [P, ST, 1])
        xn = sb("xn", [P, ST, D])
        xT = sb("xT", [P, DC, S])
        Wq, Wk, Wv, Wo = (sb(n, [P, DC, D]) for n in ("Wq", "Wk", "Wv", "Wo"))
        bq, bk = sb("bq", [P, DC]), sb("bk", [P, DC])
        bo = sb("bo", [P, D])
        pr = [sb(f"pr{i}", [P, SW]) for i in range(2)]
        prT = [sb(f"prT{i}", [P, SW]) for i in range(2)]
        negmax = sb("negmax", [P, H, ST])
        rsum = [sb(f"rsum{p}", [P, ST, H]) for p in range(2)]
        rden = sb("rden", [P, ST, H])
        rwide = sb("rwide", [P, ST, H, V])
        rT = sb("rT", [P, CC, S])
        cT = sb("cT", [P, CC, S])
        A, Bk, Dk = (ps(n, [P, 2, 512]) for n in ("A", "B", "D"))
        C = ps("C", [P, 2, 512])
        halves = lambda bank: bank.rearrange("p (a s) -> p a s", a=2)
        chunks4 = lambda t: t[:].rearrange("p b (a s) -> p (b a) s", a=2)
        D0, D1, C1 = halves(Dk[:, 0, :]), halves(Dk[:, 1, :]), halves(C[:, 1, :])
        c_ps = chunks4(C)[:, 0:CC, :]
        z = {n: sem(n) for n in (
            "w_in", "var", "rst", "xn_ready", "turned", "xT_ready", "q_ps", "k_ps", "v_ps", "q_ready", "k_ready",
            "v_ready", "s_ps", "neg_ready", "exp_ready", "pT_ps", "pT_ready", "o_ps", "rwide_ready", "r_ps", "rT_ready",
            "ctx_read", "ctx_ready", "out_ps", "out_read", "consts")}
        n_w = 7 if not latent else 8
        if latent:
            qf, kf, vf = (sb(n, [P, DC, S]) for n in ("qf", "kf", "vf"))
            ql, kl, qr, t1, t2 = (sb(n, [P, 4, S]) for n in ("ql", "kl", "qr", "t1", "t2"))
            kr, qq = ([sb(f"{n}{p}", [P, 4, S]) for p in range(2)] for n in ("kr", "qq"))
            vl = [sb(f"vl{p}", [P, ST, H, LAT]) for p in range(2)]
            bvf = sb("bvf", [P, DC])
            bd_q, bd_kv, bd_o = sb("bd_q", [P, 2, P]), sb("bd_kv", [P, D]), sb("bd_o", [P, 2, P])
            bd_k = sb("bd_k", [P, 2, P])
            bd_qk = sb("bd_qk", [P, P])
            rot, cos, sin = sb("rot", [P, P]), sb("cos", [P, S]), sb("sin", [P, S])
            bl_q, bl_k, bl_qk, bl_o = (sb(n, [P, 1]) for n in ("bl_q", "bl_k", "bl_qk", "bl_o"))
            bl_v = sb("bl_v", [P, LAT])
            mask = sb("mask", [P, SW])
            yT = sb("yT", [P, DC, S])
            z.update({n: sem(n) for n in (
                "bd_zero", "bd_in", "ql_ps", "kl_ps", "vl_ps", "rq_ps", "rk_ps", "qk_ps", "vf_ready", "ql_ready",
                "kl_ready", "vl_ready", "qcos_ready", "kcos_ready", "qsin_ready", "ksin_ready", "qr_ready", "kr_ready",
                "qq_ready", "y_ps", "y_ready")})
            keys, qrows = kr, [qq, qq]
        else:
            qe, qo, kT = ([sb(f"{n}{p}", [P, DC, S]) for p in range(2)] for n in ("qe", "qo", "kT"))
            ve, vo = ([sb(f"{n}{p}", [P, ST, H // 2, 2, HD]) for p in range(2)] for n in ("ve", "vo"))
            bv = sb("bv", [P, D])
            parity = sb("parity", [P, 2])
            bqp = sb("bqp", [P, 2, DC])
            z.update({n: sem(n) for n in ("bqp_ready",)})
            keys, qrows = kT, [qe, qo]
        if latent or decayed:
            sm = [sb(f"sm{i}", [P, SW]) for i in range(2)]
        if sparse:
            idx_i, idx_f, neg_i = sb("idx_i", [P, SAMPLES], I32), sb("idx_f", [P, SAMPLES]), sb("neg_i", [P, SAMPLES])
            tok = sb("tok", [P, ST])
            pick = sb("pick", [P, ST, SAMPLES])
            xsT, ksT = sb("xsT", [P, DC, SAMPLES]), sb("ksT", [P, DC, SAMPLES])
            qs = sb("qs", [P, DC, S])
            bqs = sb("bqs", [P, DC])
            kd = sb("kd", [P, DC, 8, SAMPLES])
            own = sb("own", [P, 8])
            headsel = sb("headsel", [H, D])
            smax, ssum = sb("smax", [P, ST, H]), sb("ssum", [P, ST, H])
            mwork, best8 = sb("mwork", [H, S]), sb("best8", [H, 8])
            mrow = [sb(f"mrow{p}", [H, S]) for p in range(2)]
            xsum = sb("xsum", [P, DC])
            bvc = sb("bvc", [P, DC])
            meanT = [sb(f"meanT{p}", [P, 2, DC]) for p in range(2)]
            mpart = sb("mpart", [P, DC, S])
            z.update({n: sem(n) for n in (
                "iotas", "pick_ready", "xs_ps", "xs_ready", "ks_ps", "ks_ready", "kd_ready", "ss_ps", "ss_read",
                "stand_ready", "m_ps", "m_read", "rows_ready", "kept_ps", "kept_read", "mean_ps", "mean_ready")})
        if decayed:
            masks = w["masks"]

        def head_rows(h):
            if latent:
                return h // 4, (h % 4) * GROUP_ROWS, 0
            return h // 8, (h % 8) // 2 * GROUP_ROWS, h % 2

        def walk(engine, first, sequence, last):
            first()
            sequence(0, 0, False, True)
            with engine.Fori(0, B // 2 - 1) as k:
                sequence(k * 2 + 1, 1, True, True)
                sequence(k * 2 + 2, 0, True, True)
            sequence(B - 1, (B - 1) % 2, True, False)
            last()

        with nc.Block() as block:
            @block.sync
            def _(sp):
                if latent:
                    for i, t in enumerate((Wq, Wk, Wv)):
                        sp.dma_start(t[:], kxn(w["c_attn_w"])[:, :, i * D:(i + 1) * D]).then_inc(z["w_in"], 16)
                    for i, t in enumerate((bq, bk, bvf)):
                        sp.dma_start(t[:], col_ap(w["c_attn_b"][i * D:(i + 1) * D]),
                                     allow_slow_non_contiguous=True).then_inc(z["w_in"], 16)
                    sp.dma_start(Wo[:], kxn(w["cproj_w"])).then_inc(z["w_in"], 16)
                    sp.dma_start(bo[:], row_ap(w["cproj_b"])).then_inc(z["w_in"], 16)
                    sp.dma_start(rot[:], w["rot"]).then_inc(z["bd_in"], 16)
                    sp.dma_start(cos[:], w["cos"]).then_inc(z["bd_in"], 16)
                    sp.dma_start(sin[:], w["sin"]).then_inc(z["bd_in"], 16)
                    col = lambda x: x.rearrange("(l a) -> l a", a=1)
                    for g in range(4):
                        rows = slice(g * LAT, (g + 1) * LAT)
                        sp.dma_start(bl_q[rows, :], col(w["q2l_b"])).then_inc(z["bd_in"], 16)
                        sp.dma_start(bl_k[rows, :], col(w["kv2l_b"])).then_inc(z["bd_in"], 16)
                        sp.dma_start(bl_qk[rows, :], col(w["wqk_b"])).then_inc(z["bd_in"], 16)
                    for g in range(8):
                        sp.dma_start(bl_o[g * HD:(g + 1) * HD, :], col(w["l2o_b"])).then_inc(z["bd_in"], 16)
                    sp.dma_start(bl_v[:], row_ap(w["kv2l_b"])).then_inc(z["bd_in"], 16)
                    sp.wait_ge(z["bd_zero"], 1)
                    for g in range(8):
                        f = slice(g * HD, (g + 1) * HD)
                        lat = slice(g % 4 * LAT, (g % 4 + 1) * LAT)
                        sp.dma_start(bd_q[f, g // 4, lat], w["q2l_w"]).then_inc(z["bd_in"], 16)
                        sp.dma_start(bd_k[f, g // 4, lat], w["kv2l_w"]).then_inc(z["bd_in"], 16)
                        sp.dma_start(bd_kv[f, g * LAT:(g + 1) * LAT], w["kv2l_w"]).then_inc(z["bd_in"], 16)
                        sp.dma_start(bd_o[lat, g // 4, f], w["l2o_w"]).then_inc(z["bd_in"], 16)
                    for g in range(4):
                        lat = slice(g * LAT, (g + 1) * LAT)
                        sp.dma_start(bd_qk[lat, lat], w["wqk_w"]).then_inc(z["bd_in"], 16)
                else:
                    for t, n in ((bq, "bq"), (bk, "bk")):
                        sp.dma_start(t[:], col_ap(w[n]), allow_slow_non_contiguous=True).then_inc(z["w_in"], 16)
                    for t, n in ((Wq, "Wq"), (Wk, "Wk"), (Wv, "Wv"), (Wo, "Wo")):
                        sp.dma_start(t[:], kxn(w[n])).then_inc(z["w_in"], 16)
                    sp.dma_start(bo[:], row_ap(w["bo"])).then_inc(z["w_in"], 16)
                    sp.dma_start(bv[:], row_ap(w["bv"])).then_inc(z["consts"], 16)
                    sp.dma_start(parity[:], w["parity"]).then_inc(z["consts"], 16)
                    if sparse:
                        sp.dma_start(idx_i[:], row_ap(w["idx_k"])).then_inc(z["consts"], 16)
                        sp.dma_start(bvc[:], col_ap(w["bv"]), allow_slow_non_contiguous=True).then_inc(z["consts"], 16)

            BD_DMAS = 3 + 12 + 8 + 1 + 32 + 4
            CONST_DMAS = 4 if sparse else 2

            @block.gpsimd
            def _(g):
                if latent:
                    for t in (bd_q, bd_k, bd_kv, bd_o, bd_qk):
                        g.memset(t[:], 0.0)
                    g.memset(mask[:], 0.0)
                    g.drain().then_inc(z["bd_zero"], 1)
                    for t in range(ST):
                        m = mask[:, SCOL[t]:SCOL[t] + KEYS[t]]
                        g.affine_select(out=m, in_=m, compare_op=ALU.is_ge, fill=NEG, base=t * P,
                                        pattern=[[-1, KEYS[t]]], channel_multiplier=1)
                    g.drain().then_inc(z["consts"], 1)
                if sparse:
                    g.iota(tok[:], [[P, ST]], base=0, channel_multiplier=1, allow_small_or_imprecise_dtypes=True)
                    g.memset(own[:], 1.0)
                    g.memset(headsel[:], 1.0)
                    g.drain()
                    g.affine_select(out=own[:], in_=own[:], compare_op=ALU.is_ge, fill=0.0, base=0,
                                    pattern=[[-HD, 8]], channel_multiplier=1)
                    g.affine_select(out=headsel[:], in_=headsel[:], compare_op=ALU.is_ge, fill=0.0, base=0,
                                    pattern=[[1, D]], channel_multiplier=-HD)
                    g.drain()
                    g.affine_select(out=own[:], in_=own[:], compare_op=ALU.is_ge, fill=0.0, base=HD - 1,
                                    pattern=[[HD, 8]], channel_multiplier=-1)
                    g.affine_select(out=headsel[:], in_=headsel[:], compare_op=ALU.is_ge, fill=0.0, base=HD - 1,
                                    pattern=[[-1, D]], channel_multiplier=HD)
                    g.drain().then_inc(z["iotas"], 1)
                if latent:
                    g.wait_ge(z["bd_in"], 16 * BD_DMAS)
                with g.Fori(0, B) as b:
                    rstd_of(g, sh, mv, rstd, z["var"], z["rst"], b + 1)
                    if latent:
                        g.wait_ge(z["ql_ready"], b + 1)
                        g.tensor_tensor(t1[:], ql[:], bc(cos[:], [P, 4, S]), ALU.mult).then_inc(z["qcos_ready"], 1)
                        g.wait_ge(z["qcos_ready"], b + 1)
                        g.wait_ge(z["qsin_ready"], b + 1)
                        g.tensor_tensor(qr[:], t1[:], t2[:], ALU.add).then_inc(z["qr_ready"], 1)
                        g.wait_ge(z["kl_ready"], b + 1)
                        g.wait_ge(z["qr_ready"], b + 1)
                        g.tensor_tensor(t1[:], kl[:], bc(cos[:], [P, 4, S]), ALU.mult).then_inc(z["kcos_ready"], 1)

            @block.tensor
            def _(pe):
                def scores(b, p, h):
                    c, r, odd = head_rows(h)
                    rows = slice(r, r + GROUP_ROWS)
                    for t in range(ST):
                        last = pe.matmul(A[:, h % 2, SCOL[t]:SCOL[t] + KEYS[t]], qrows[odd][p][rows, c, t * P:(t + 1) * P],
                                         keys[p][rows, c, 0:KEYS[t]], start=True, stop=True)
                    last.then_inc(z["s_ps"], 1)

                def first_scores(b, p):
                    pe.wait_ge(z["qq_ready" if latent else "q_ready"], b + 1)
                    pe.wait_ge(z["kr_ready" if latent else "k_ready"], b + 1)
                    pe.wait_ge(z["vl_ready" if latent else "v_ready"], b + 1)
                    scores(b, p, 0)

                def turn_probs(b, h):
                    pe.wait_ge(z["exp_ready"], b * H + h + 1)
                    for t in range(ST):
                        for kb in range(KEYS[t] // P):
                            at = t * P if kb == 0 else S + (t * P if not latent else 0)
                            last = pe.transpose(Bk[:, h % 2, at:at + P], pr[h % 2][:, SCOL[t] + kb * P:SCOL[t] + (kb + 1) * P],
                                                sh.ident[:])
                    last.then_inc(z["pT_ps"], 1)

                def values(b, p, h):
                    pe.wait_ge(z["pT_ready"], b * H + h + 1)
                    c, r, odd = head_rows(h)
                    out = c_ps[r:r + GROUP_ROWS, c, :]
                    for kb in range(ST):
                        v_ = vl[p][:, kb, h, :] if latent else (ve, vo)[odd][p][:, kb, h // 2, :, :].rearrange("p a d -> p (a d)")
                        q0 = S - P if latent and kb else 0
                        last = pe.matmul(out[:, q0:S], v_, prT[h % 2][:, kb * S:kb * S + S - q0],
                                         start=(kb == 0 and (latent or not odd)),
                                         stop=(kb == ST - 1 and (latent or odd == 1)))
                    if h == H - 1:
                        last.then_inc(z["o_ps"], 1)

                def prepare(b, p, step):
                    if step == 4:
                        pe.wait_ge(z["xn_ready"], b + 1)
                        turn(pe, D0, xn, sh.ident[:]).then_inc(z["turned"], 1)
                        if sparse:
                            for c in range(DC):
                                for t in range(ST):
                                    last = pe.matmul(D1[:, c, 0:SAMPLES], xn[:, t, c * P:(c + 1) * P], pick[:, t, :],
                                                     start=(t == 0), stop=(t == ST - 1))
                            last.then_inc(z["xs_ps"], 1)
                    if step == 5:
                        pe.wait_ge(z["xT_ready"], b + 1)
                        for c in range(DC):
                            last = project(pe, (D1 if latent else C1)[:, c, :], Wq, xT, c * P)
                        last.then_inc(z["q_ps"], 1)
                    if step == 6:
                        for c in range(DC):
                            last = project(pe, D0[:, c, :], Wk, xT, c * P)
                        last.then_inc(z["k_ps"], 1)
                    if latent:
                        whole = chunks4(Dk)
                        if step == 7:
                            pe.wait_ge(z["q_ready"], b + 1)
                            for c in range(DC):
                                last = project(pe, D1[:, c, :], Wv, xT, c * P)
                            last.then_inc(z["v_ps"], 1)
                        for at, src, stat, ready, done in (
                                (8, qf, bd_q, ("k_ready", "vf_ready"), "ql_ps"), (9, kf, bd_k, ("ql_ready",), "kl_ps"),
                                (11, ql, rot, ("vl_ready",), "rq_ps"), (12, kl, rot, ("qsin_ready",), "rk_ps"),
                                (13, qr, bd_qk, ("qr_ready", "ksin_ready"), "qk_ps")):
                            if step == at:
                                for n in ready:
                                    pe.wait_ge(z[n], b + 1)
                                for j in range(4):
                                    blocks = stat in (bd_q, bd_k)
                                    last = pe.matmul(whole[:, j, :], stat[:, j % 2, :] if blocks else stat[:],
                                                     src[:, j // 2 if blocks else j, :], start=True, stop=True)
                                last.then_inc(z[done], 1)
                        if step == 10:
                            pe.wait_ge(z["kl_ready"], b + 1)
                            for t in range(ST):
                                for c in range(DC):
                                    last = pe.matmul(Dk[:, t, c * D:(c + 1) * D], vf[:, c, t * P:(t + 1) * P], bd_kv[:],
                                                     start=True, stop=True)
                            last.then_inc(z["vl_ps"], 1)
                        return
                    if step == 7:
                        if sparse:
                            pe.wait_ge(z["xs_ready"], b + 1)
                        for t in range(ST):
                            last = project_rows(pe, D1[:, t, :], xT, Wv, t)
                        last.then_inc(z["v_ps"], 1)
                    if sparse and step == 8:
                        pe.wait_ge(z["q_ready"], b + 1)
                        for c in range(DC):
                            project(pe, C1[:, c, 0:SAMPLES], Wk, xsT, c * P)
                        for c in range(DC):
                            for k in range(DC):
                                last = pe.matmul(C1[:, c, 64:65], Wv[:, k, c * P:(c + 1) * P], xsum[:, k:k + 1],
                                                 start=(k == 0), stop=(k == DC - 1))
                        last.then_inc(z["ks_ps"], 1)
                    if sparse and step in (10, 11):
                        t = step - 10
                        pe.wait_ge(z["kd_ready"], b + 1)
                        pe.wait_ge(z["v_ready"], b + 1)
                        if t:
                            pe.wait_ge(z["ss_read"], b * ST + 1)
                        else:
                            pe.wait_ge(z["k_ready"], b + 1)
                        for c in range(DC):
                            out = (Dk[:, 0, :], C[:, 1, :])[c] if t == 0 else (Dk[:, 1, :], Dk[:, 0, :])[c]
                            last = pe.matmul(out[:, 0:8 * SAMPLES], qs[:, c, t * P:(t + 1) * P],
                                             kd[:, c, :, :].rearrange("p h u -> p (h u)"), start=True, stop=True)
                        last.then_inc(z["ss_ps"], 1)
                    if sparse and step == 12:
                        pe.wait_ge(z["stand_ready"], b + 1)
                        for t in range(ST):
                            last = pe.transpose(D1[0:H, 0, t * P:(t + 1) * P], smax[:, t, :], sh.ident[:])
                        last.then_inc(z["m_ps"], 1)

                def tail(b, p, step):
                    if step == 0:
                        pe.wait_ge(z["rwide_ready"], b + 1)
                        for t in range(ST):
                            for c in range(CC):
                                last = pe.transpose(chunks4(Dk)[:, c, t * P:(t + 1) * P],
                                                    rwide[:, t, :, :].rearrange("p h v -> p (h v)")[:, c * P:(c + 1) * P],
                                                    sh.ident[:])
                        last.then_inc(z["r_ps"], 1)
                        if sparse:
                            pe.wait_ge(z["rows_ready"], b + 1)
                            for c in range(DC):
                                last = pe.matmul(D1[:, c, :], headsel[:, c * P:(c + 1) * P], mrow[p][:], start=True, stop=True)
                            last.then_inc(z["kept_ps"], 1)
                    if step == 2:
                        pe.wait_ge(z["ctx_ready"], b + 1)
                        if latent:
                            for c in range(DC):
                                for j in range(2):
                                    last = pe.matmul(D0[:, c, :], bd_o[:, j, :], cT[:, 2 * c + j, :], start=(j == 0),
                                                     stop=(j == 1))
                            last.then_inc(z["y_ps"], 1)
                    if step == 3:
                        if latent:
                            pe.wait_ge(z["y_ready"], b + 1)
                        for t in range(ST):
                            last = project_rows(pe, (D1 if latent else C1)[:, t, :], yT if latent else cT, Wo, t)
                        last.then_inc(z["out_ps"], 1)

                def sequence(b, p, before, after):
                    for h in range(H):
                        turn_probs(b, h)
                        if h + 2 < H:
                            scores(b, p, h + 2)
                        elif after:
                            if h + 2 == H:
                                first_scores(b + 1, 1 - p)
                            else:
                                scores(b + 1, 1 - p, 1)
                        if h >= 1:
                            if h == 1 and before:
                                pe.wait_ge(z["ctx_read"], b)
                            values(b, p, h - 1)
                        elif before:
                            values(b - 1, 1 - p, H - 1)
                        if before:
                            tail(b - 1, 1 - p, h)
                        if after:
                            if h == 5 and before:
                                pe.wait_ge(z["out_read"], b)
                            prepare(b + 1, 1 - p, h)

                def first():
                    pe.wait_ge(z["w_in"], 16 * n_w)
                    if latent:
                        pe.wait_ge(z["bd_in"], 16 * BD_DMAS)
                    if sparse:
                        pe.wait_ge(z["pick_ready"], 1)
                    for step in range(H):
                        prepare(0, 0, step)
                    first_scores(0, 0)
                    scores(0, 0, 1)

                def last():
                    values(B - 1, 1, H - 1)
                    for step in range(H):
                        tail(B - 1, 1, step)

                walk(pe, first, sequence, last)

            @block.scalar
            def _(a):
                def exps(b, p, h):
                    a.wait_ge(z["neg_ready"], b * H + h + 1)
                    for t in range(ST):
                        cols = slice(SCOL[t], SCOL[t] + KEYS[t])
                        src = sm[h % 2][:, cols] if latent or decayed else A[:, h % 2, cols]
                        a.activation(pr[h % 2][:, cols], src, ACT.Exp, bias=negmax[:, h, t:t + 1],
                                     accum_out=rsum[p][:, t, h:h + 1])
                    a.drain().then_inc(z["exp_ready"], 1)

                def copy_turned(b, h):
                    a.wait_ge(z["pT_ps"], b * H + h + 1)
                    a.copy(prT[h % 2][:], Bk[:, h % 2, 0:SW]).then_inc(z["pT_ready"], 1)

                def prepare(b, p, step):
                    if step == 4:
                        a.wait_ge(z["turned"], b + 1)
                        if sparse:
                            for c in range(DC):
                                a.activation(xT[:, c, :], D0[:, c, :], ACT.Identity, accum_out=xsum[:, c:c + 1])
                            a.drain().then_inc(z["xT_ready"], 1)
                            a.wait_ge(z["xs_ps"], b + 1)
                            a.copy(xsT[:], D1[:, :, 0:SAMPLES]).then_inc(z["xs_ready"], 1)
                        else:
                            a.copy(xT[:], D0).then_inc(z["xT_ready"], 1)
                    if latent:
                        for at, dst, src, bias, came, done in (
                                (5, qf, D1, bq, "q_ps", "q_ready"), (6, kf, D0, bk, "k_ps", "k_ready"),
                                (7, vf, D1, bvf, "v_ps", "vf_ready")):
                            if step == at:
                                a.wait_ge(z[came], b + 1)
                                for c in range(DC):
                                    last = a.activation(dst[:, c, :], src[:, c, :], ACT.Identity, bias=bias[:, c:c + 1])
                                last.then_inc(z[done], 1)
                        for at, dst, bias, came, done in (
                                (8, ql, bl_q, "ql_ps", "ql_ready"), (9, kl, bl_k, "kl_ps", "kl_ready"),
                                (13, qq[p], bl_qk, "qk_ps", "qq_ready")):
                            if step == at:
                                a.wait_ge(z[came], b + 1)
                                a.activation(dst[:], chunks4(Dk), ACT.Identity, bias=bias[:, 0:1]).then_inc(z[done], 1)
                        return
                    if step == 5:
                        a.wait_ge(z["q_ps"], b + 1)
                        for i, q in enumerate((qe[p], qo[p])):
                            for c in range(DC):
                                last = a.activation(q[:, c, :], C1[:, c, :], ACT.Identity, bias=bqp[:, i, c:c + 1],
                                                    scale=parity[:, i:i + 1])
                        if sparse:
                            for c in range(DC):
                                last = a.activation(qs[:, c, :], C1[:, c, :], ACT.Identity, bias=bqs[:, c:c + 1],
                                                    scale=float(HD) ** -0.5)
                        last.then_inc(z["q_ready"], 1)
                    if step == 6:
                        a.wait_ge(z["k_ps"], b + 1)
                        for c in range(DC):
                            last = a.activation(kT[p][:, c, :], D0[:, c, :], ACT.Identity, bias=bk[:, c:c + 1])
                        last.then_inc(z["k_ready"], 1)
                    if sparse and step == 8:
                        a.wait_ge(z["ks_ps"], b + 1)
                        for c in range(DC):
                            a.activation(ksT[:, c, :], C1[:, c, 0:SAMPLES], ACT.Identity, bias=bk[:, c:c + 1])
                            a.activation(meanT[p][:, 0, c:c + 1], C1[:, c, 64:65], ACT.Identity, bias=bvc[:, c:c + 1],
                                         scale=1.0 / S)
                        a.drain().then_inc(z["ks_ready"], 1)

                def tail(b, p, step):
                    if step == 0:
                        a.wait_ge(z["r_ps"], b + 1)
                        a.copy(rT[:], chunks4(Dk)[:, 0:CC, :]).then_inc(z["rT_ready"], 1)
                    if latent and step == 2:
                        a.wait_ge(z["y_ps"], b + 1)
                        a.activation(yT[:], D0, ACT.Identity, bias=bl_o[:, 0:1]).then_inc(z["y_ready"], 1)

                def sequence(b, p, before, after):
                    for h in range(H):
                        if h + 1 < H:
                            exps(b, p, h + 1)
                        elif after:
                            exps(b + 1, 1 - p, 0)
                        if latent or decayed:
                            copy_turned(b, h)
                        if before:
                            tail(b - 1, 1 - p, h)
                        if after:
                            prepare(b + 1, 1 - p, h)

                def first():
                    a.wait_ge(z["w_in"], 16 * n_w)
                    if latent:
                        a.wait_ge(z["bd_in"], 16 * BD_DMAS)
                    else:
                        a.wait_ge(z["bqp_ready"], 1)
                    for step in range(H):
                        prepare(0, 0, step)
                    exps(0, 0, 0)

                def last():
                    for step in range(H):
                        tail(B - 1, 1, step)

                walk(a, first, sequence, last)

            @block.vector
            def _(v):
                def row_max(b, h):
                    v.wait_ge(z["s_ps"], b * H + h + 1)
                    src = A[:, h % 2, 0:SW]
                    if latent:
                        v.scalar_tensor_tensor(sm[h % 2][:], src, float(LAT) ** -0.5, mask[:], ALU.mult, ALU.add)
                    if decayed:
                        v.tensor_tensor(sm[h % 2][:], src, masks[:, h, :, :].rearrange("p t k -> p (t k)"), ALU.mult)
                    if latent or decayed:
                        v.drain()
                        src = sm[h % 2][:]
                    if latent:
                        for t in range(ST):
                            v.tensor_reduce(negmax[:, h, t:t + 1], src[:, SCOL[t]:SCOL[t] + KEYS[t]], AXX, ALU.max, negate=True)
                        v.drain().then_inc(z["neg_ready"], 1)
                    else:
                        v.tensor_reduce(negmax[:, h, :], src.rearrange("p (t k) -> p t k", t=ST), AXX, ALU.max,
                                        negate=True).then_inc(z["neg_ready"], 1)

                def copy_turned(b, h):
                    v.wait_ge(z["pT_ps"], b * H + h + 1)
                    v.tensor_copy(prT[h % 2][:], Bk[:, h % 2, 0:SW]).then_inc(z["pT_ready"], 1)

                def sum_samples(b, t):
                    v.wait_ge(z["ss_ps"], b * ST + t + 1)
                    for c in range(DC):
                        bank = (Dk[:, 0, :], C[:, 1, :])[c] if t == 0 else (Dk[:, 1, :], Dk[:, 0, :])[c]
                        src = bank[:, 0:8 * SAMPLES].rearrange("p (h u) -> p h u", u=SAMPLES)
                        v.tensor_reduce(smax[:, t, 8 * c:8 * c + 8], src, AXX, ALU.max)
                        v.tensor_reduce(ssum[:, t, 8 * c:8 * c + 8], src, AXX, ALU.add)
                    v.drain().then_inc(z["ss_read"], 1)

                def prepare(b, p, step):
                    if step == 1:
                        for t in range(ST):
                            v.bn_stats(stats[:, t, :], sh.h[:, ds(b * ST + t, 1), :])
                        v.drain()
                        for t in range(ST):
                            v.bn_aggr(mv[:, t, :], stats[:, t, :])
                        v.drain()
                        v.tensor_scalar(mv[:, :, 1:2], mv[:, :, 1:2], LN_EPS, None, ALU.add).then_inc(z["var"], 1)
                    if step == 2:
                        v.wait_ge(z["rst"], b + 1)
                        for t in range(ST):
                            v.tensor_scalar(xn[:, t, :], sh.h[:, ds(b * ST + t, 1), :], mv[:, t, 0:1], rstd[:, t, 0:1],
                                            ALU.subtract, ALU.mult)
                        v.drain().then_inc(z["xn_ready"], 1)
                        v.tensor_tensor(sh.h[:, ds(b * ST, ST), :], sh.h[:, ds(b * ST, ST), :], bc(bo[:], [P, ST, D]), ALU.add)
                        v.drain()
                    if latent:
                        if step == 10:
                            v.wait_ge(z["vl_ps"], b + 1)
                            v.tensor_tensor(vl[p][:].rearrange("p t h l -> p (t h) l"),
                                            Dk[:].rearrange("p a (h l) -> p (a h) l", l=LAT),
                                            bc(bl_v[:], [P, ST * H, LAT]), ALU.add).then_inc(z["vl_ready"], 1)
                        if step == 11:
                            v.wait_ge(z["rq_ps"], b + 1)
                            v.tensor_tensor(t2[:], chunks4(Dk), bc(sin[:], [P, 4, S]), ALU.mult).then_inc(z["qsin_ready"], 1)
                        if step == 12:
                            v.wait_ge(z["rk_ps"], b + 1)
                            v.tensor_tensor(kr[p][:], chunks4(Dk), bc(sin[:], [P, 4, S]), ALU.mult).then_inc(z["ksin_ready"], 1)
                            v.drain()
                        if step == 13:
                            v.wait_ge(z["kcos_ready"], b + 1)
                            v.tensor_tensor(kr[p][:], kr[p][:], t1[:], ALU.add).then_inc(z["kr_ready"], 1)
                        return
                    if step == 7:
                        v.wait_ge(z["v_ps"], b + 1)
                        for i, dst in enumerate((ve[p], vo[p])):
                            for t in range(ST):
                                v.tensor_tensor(dst[:, t, :, i, :], D1[:, t, :].rearrange("p (n a d) -> p n a d", a=2, d=HD)[:, :, i, :],
                                                bv[:].rearrange("p (n a d) -> p n a d", a=2, d=HD)[:, :, i, :], ALU.add)
                        v.drain().then_inc(z["v_ready"], 1)
                    if sparse:
                        if step == 8:
                            v.wait_ge(z["ks_ready"], b + 1)
                            for c in range(DC):
                                v.tensor_tensor(kd[:, c, :, :], bc(ksT[:, c, :], [P, 8, SAMPLES]),
                                                own[:].unsqueeze(2).broadcast_to([P, 8, SAMPLES]), ALU.mult)
                            v.tensor_scalar(meanT[p][:, 1, :], meanT[p][:, 0, :], -1.0, None, ALU.mult)
                            v.drain().then_inc(z["kd_ready"], 1)
                        if step == 10:
                            sum_samples(b, 0)
                        if step == 11:
                            sum_samples(b, 1)
                            v.scalar_tensor_tensor(smax[:], ssum[:], -1.0 / SAMPLES, smax[:], ALU.mult, ALU.add)
                            v.drain().then_inc(z["stand_ready"], 1)
                        if step == 12:
                            v.wait_ge(z["m_ps"], b + 1)
                            v.tensor_copy(mwork[:], D1[0:H, 0, :])
                            v.drain()
                        for _ in range({12: 1, 13: 2, 14: 2}.get(step, 0)):
                            v.max(best8[:], mwork[:])
                            v.drain()
                            v.match_replace(mwork[:], best8[:], mwork[:], NEG)
                            v.drain()
                        if step == 14:
                            v.tensor_scalar(mrow[p][:], mwork[:], NEG, None, ALU.is_equal)
                            v.drain().then_inc(z["rows_ready"], 1)

                def reciprocals(b, p):
                    v.wait_ge(z["exp_ready"], b * H + H)
                    v.reciprocal(rden[:], rsum[p][:])
                    v.drain()
                    v.tensor_copy(rwide[:], rden[:].unsqueeze(3).broadcast_to([P, ST, H, V]))
                    v.drain().then_inc(z["rwide_ready"], 1)

                def tail(b, p, step):
                    if step == 0:
                        v.wait_ge(z["rT_ready"], b + 1)
                        v.wait_ge(z["o_ps"], b + 1)
                        v.tensor_tensor(cT[:], c_ps, rT[:], ALU.mult)
                        v.drain().then_inc(z["ctx_read"], 1)
                        if sparse:
                            v.wait_ge(z["kept_ps"], b + 1)
                            v.tensor_tensor(cT[:], cT[:], D1, ALU.mult)
                            for c in range(DC):
                                v.tensor_scalar(mpart[:, c, :], D1[:, c, :], meanT[p][:, 1, c:c + 1], meanT[p][:, 0, c:c + 1],
                                                ALU.mult, ALU.add)
                            v.drain()
                            v.tensor_tensor(cT[:], cT[:], mpart[:], ALU.add)
                            v.drain()
                        v.drain().then_inc(z["ctx_ready"], 1)
                    if step == 4:
                        v.wait_ge(z["out_ps"], b + 1)
                        v.tensor_tensor(sh.h[:, ds(b * ST, ST), :], sh.h[:, ds(b * ST, ST), :], D1 if latent else C1, ALU.add)
                        v.drain().then_inc(z["out_read"], 1)

                def sequence(b, p, before, after):
                    for h in range(H):
                        if h + 1 < H:
                            row_max(b, h + 1)
                        elif after:
                            row_max(b + 1, 0)
                        if sparse:
                            copy_turned(b, h)
                        if before:
                            tail(b - 1, 1 - p, h)
                        if after:
                            prepare(b + 1, 1 - p, h)
                    reciprocals(b, p)

                def first():
                    v.wait_ge(z["w_in"], 16 * n_w)
                    if latent:
                        v.wait_ge(z["bd_in"], 16 * BD_DMAS)
                        v.wait_ge(z["consts"], 1)
                    else:
                        v.wait_ge(z["consts"], 16 * CONST_DMAS)
                        for i in range(2):
                            v.tensor_scalar(bqp[:, i, :], bq[:], parity[:, i:i + 1], None, ALU.mult)
                        for t in (*ve, *vo):
                            v.memset(t[:], 0.0)
                        if sparse:
                            v.tensor_scalar(bqs[:], bq[:], float(HD) ** -0.5, None, ALU.mult)
                        v.drain().then_inc(z["bqp_ready"], 1)
                    if sparse:
                        v.wait_ge(z["iotas"], 1)
                        v.tensor_copy(idx_f[:], idx_i[:])
                        v.drain()
                        v.tensor_scalar(neg_i[:], idx_f[:], 0.0, float(S), ALU.is_lt, ALU.mult)
                        v.drain()
                        v.tensor_tensor(idx_f[:], idx_f[:], neg_i[:], ALU.add)
                        v.drain()
                        v.tensor_scalar(idx_f[:], idx_f[:], 0.0, float(S - 1), ALU.max, ALU.min)
                        v.drain()
                        for t in range(ST):
                            v.tensor_scalar(pick[:, t, :], idx_f[:], tok[:, t:t + 1], None, ALU.is_equal)
                        v.drain().then_inc(z["pick_ready"], 1)
                    for step in range(H):
                        prepare(0, 0, step)
                    row_max(0, 0)

                def last():
                    for step in range(H):
                        tail(B - 1, 1, step)

                walk(v, first, sequence, last)


def capacity_experts(nc, sh, buf, obuf, c_fc, c_proj):
    F = c_fc.shape[2] // DC
    FC = F // P
    CB = CAP // P
    HALF = CAP // 2
    GB = 3
    GROUPS = 2 * FC
    with ExitStack() as ctx, Signals(nc) as signals:
        sb = lambda n, shape, dt=F32: ctx.enter_context(nc.sbuf_tensor("x2_" + n, shape, dt))
        ps = lambda n, shape, dt=F32: ctx.enter_context(nc.psum_tensor("x2_" + n, shape, dt))
        sem = lambda n: signals("x2_" + n)
        wf = [sb(f"wf{p}", [P, DC, F]) for p in range(2)]
        wp = [sb(f"wp{p}", [P, FC, D]) for p in range(2)]
        xin = [sb(f"xin{p}", [P, CB, D]) for p in range(2)]
        xT = [sb(f"xT{p}", [P, DC, CAP]) for p in range(2)]
        hT = sb("hT", [P, FC, CAP])
        r = [sb(f"r{i}", [P, HALF]) for i in range(GB)]
        y = [sb(f"y{p}", [P, CB, D]) for p in range(2)]
        p_t = [ps(f"p_t{c}", [P, 4, P]) for c in range(DC + 1)]
        p_g = [ps(f"p_g{i}", [P, 512]) for i in range(GB)]
        p_o = [ps(f"p_o{i}", [P, D]) for i in range(2)]
        x_in, wf_in, wp_in, stored = ([sem(f"{n}{p}") for p in range(2)] for n in ("x_in", "wf_in", "wp_in", "stored"))
        turned, xT_ready, g_ready, relu_ready, h_ready, o_ready, y_ready = (
            sem(n) for n in ("turned", "xT_ready", "g_ready", "relu_ready", "h_ready", "o_ready", "y_ready"))
        rows = lambda m, e: m[ds(e * CAP, CAP), :].rearrange("(p t) d -> p t d", t=CB)
        with nc.Block() as block:
            @block.sync
            def _(sp):
                def load(e, p, reused):
                    if reused:
                        sp.wait_ge(turned, e - 1)
                    sp.dma_start(xin[p][:], rows(buf, e)).then_inc(x_in[p], 16)
                    if reused:
                        sp.wait_ge(o_ready, e * CB - CB)
                    sp.dma_start(wf[p][:].rearrange("p c n -> p (c n)"), c_fc[ds(e, 1), :, :].rearrange("a p n -> (a p) n")
                                 ).then_inc(wf_in[p], 16)
                    sp.dma_start(wp[p][:].rearrange("p c n -> p (c n)"), c_proj[ds(e, 1), :, :].rearrange("a p n -> (a p) n")
                                 ).then_inc(wp_in[p], 16)

                for p in range(2):
                    load(p, p, False)
                with sp.Fori(1, E // 2) as k:
                    for p in range(2):
                        load(k * 2 + p, p, True)

            @block.tensor
            def _(pe):
                def turn_rows(k, p):
                    pe.wait_ge(x_in[p], k * 16 + 16)
                    for c in range(DC):
                        for t in range(CB):
                            out = p_t[c][:, t, :] if t < 4 else p_t[DC][:, c, :]
                            last = pe.transpose(out, xin[p][:, t, c * P:(c + 1) * P], sh.ident[:])
                    last.then_inc(turned, 1)

                def expert(e, k, p, ahead):
                    pe.wait_ge(xT_ready, e + 1)
                    pe.wait_ge(wf_in[p], k * 16 + 16)
                    for n in range(GROUPS):
                        f, half = n // 2, n % 2
                        if n >= GB:
                            pe.wait_ge(relu_ready, e * GROUPS + n - GB + 1)
                        for c in range(DC):
                            last = pe.matmul(p_g[n % GB][:, 0:HALF], wf[p][:, c, f * P:(f + 1) * P],
                                             xT[p][:, c, half * HALF:(half + 1) * HALF], start=(c == 0), stop=(c == DC - 1))
                        last.then_inc(g_ready, 1)
                    if ahead:
                        turn_rows(k + p, 1 - p)
                    pe.wait_ge(h_ready, e * GROUPS + GROUPS)
                    pe.wait_ge(wp_in[p], k * 16 + 16)
                    for t in range(CB):
                        if t >= 2:
                            pe.wait_ge(y_ready, e * CB + t - 1)
                        for f in range(FC):
                            last = pe.matmul(p_o[t % 2][:], hT[:, f, t * P:(t + 1) * P], wp[p][:, f, :],
                                             start=(f == 0), stop=(f == FC - 1))
                        last.then_inc(o_ready, 1)

                turn_rows(0, 0)
                with pe.Fori(0, E // 2 - 1) as k:
                    for p in range(2):
                        expert(k * 2 + p, k, p, True)
                for p in range(2):
                    expert(E - 2 + p, E // 2 - 1, p, p == 0)

            @block.scalar
            def _(a):
                def copy_turned(e, p):
                    a.wait_ge(turned, e + 1)
                    for c in range(DC):
                        a.copy(xT[p][:, c, 0:4 * P], p_t[c][:].rearrange("p t n -> p (t n)"))
                    a.copy(xT[p][:, :, 4 * P:CAP], p_t[DC][:, 0:DC, :]).then_inc(xT_ready, 1)

                def store(e, p):
                    a.wait_ge(y_ready, e * CB + CB)
                    a.dma_start(rows(obuf, e), y[p][:]).then_inc(stored[p], 16)

                def expert(e, p, first, ahead):
                    for n in range(GROUPS):
                        a.wait_ge(g_ready, e * GROUPS + n + 1)
                        if n >= GB:
                            a.wait_ge(h_ready, e * GROUPS + n - GB + 1)
                        a.activation(r[n % GB][:], p_g[n % GB][:, 0:HALF], ACT.Relu).then_inc(relu_ready, 1)
                    if ahead:
                        copy_turned(e + 1, 1 - p)
                    if not first:
                        store(e - 1, 1 - p)

                copy_turned(0, 0)
                expert(0, 0, True, True)
                expert(1, 1, False, True)
                with a.Fori(1, E // 2 - 1) as k:
                    for p in range(2):
                        expert(k * 2 + p, p, False, True)
                for p in range(2):
                    expert(E - 2 + p, p, False, p == 0)
                store(E - 1, 1)
                for p in range(2):
                    a.wait_ge(stored[p], 16 * (E // 2))

            @block.vector
            def _(v):
                def expert(e, k, p, reused):
                    for n in range(GROUPS):
                        f, half = n // 2, n % 2
                        v.wait_ge(relu_ready, e * GROUPS + n + 1)
                        v.tensor_tensor(hT[:, f, half * HALF:(half + 1) * HALF], r[n % GB][:], r[n % GB][:], ALU.mult
                                        ).then_inc(h_ready, 1)
                    if reused:
                        v.wait_ge(stored[p], k * 16)
                    for t in range(CB):
                        v.wait_ge(o_ready, e * CB + t + 1)
                        v.tensor_copy(y[p][:, t, :], p_o[t % 2][:]).then_inc(y_ready, 1)

                for p in range(2):
                    expert(p, 0, p, False)
                with v.Fori(1, E // 2) as k:
                    for p in range(2):
                        expert(k * 2 + p, k, p, True)


def quantised_ffn(nc, sh, w_gate, w_up, w_down):
    F = w_gate.shape[1]
    FC = F // P
    QA = 127.0
    HALF = 512
    HALVES = F // HALF
    TURNS = 4
    with ExitStack() as ctx, Signals(nc) as signals:
        sb = lambda n, shape, dt=F32: ctx.enter_context(nc.sbuf_tensor("q_" + n, shape, dt))
        ps = lambda n, shape, dt=F32: ctx.enter_context(nc.psum_tensor("q_" + n, shape, dt))
        sem = lambda n: signals("q_" + n)
        shapes = {"gate": [P, DC, F], "up": [P, DC, F], "down": [P, FC, D]}
        wf = {n: sb(n, s) for n, s in shapes.items()}
        wq = {n: sb(n + "q", s, BF16) for n, s in shapes.items()}
        asum, wmean, wscale = sb("asum", [P, 3]), sb("wmean", [P, 3]), sb("wscale", [P, 3])
        stats, mv, rstd = sb("stats", [P, NT, 6]), sb("mv", [P, NT, 2]), sb("rstd", [P, NT, 1])
        minus_half = sb("minus_half", [P, NT, 1])
        xn = sb("xn", [P, NT, D])
        amax, rscale, gscale, uscale = (sb(n, [P, NT]) for n in ("amax", "rscale", "gscale", "uscale"))
        xq = sb("xq", [P, NT, D], BF16)
        xqT = sb("xqT", [P, NT, DC, P], BF16)
        sg = [sb(f"sg{p}", [P, F]) for p in range(2)]
        gs = [sb(f"gs{p}", [P, 1]) for p in range(2)]
        pmax, pscale, dscale = ([sb(f"{n}{p}", [P, 1]) for p in range(2)] for n in ("pmax", "pscale", "dscale"))
        pq = [sb(f"pq{p}", [P, F], BF16) for p in range(2)]
        pqT = [sb(f"pqT{p}", [P, FC, P], BF16) for p in range(2)]
        p_g, p_u = ([ps(f"{n}{i}", [P, HALF]) for i in range(HALVES)] for n in ("p_g", "p_u"))
        p_T = [ps(f"p_T{p}", [P, FC, P], BF16) for p in range(2)]
        p_d = [ps(f"p_d{p}", [P, 512]) for p in range(2)]
        w_in, asum_ready, wsum_ready, var, rst, halves_set = (
            sem(n) for n in ("w_in", "asum_ready", "wsum_ready", "var", "rst", "halves_set"))
        wq_ready, xq_ready, turned, xT_ready, g_ready, u_ready, sg_ready, bank_free, pq_ready, pT_ps, pT_ready, d_ready = (
            sem(n) for n in ("wq_ready", "xq_ready", "turned", "xT_ready", "g_ready", "u_ready", "sg_ready",
                             "bank_free", "pq_ready", "pT_ps", "pT_ready", "d_ready"))
        scales_ready = sem("scales_ready")
        flat = lambda x: x[:].rearrange("p c n -> p (c n)")

        def blocks(engine, first, step):
            first()
            with engine.Fori(0, NT // 2 - 1) as k:
                for p in range(2):
                    step(k * 2 + p, p, True)
            for p in range(2):
                step(NT - 2 + p, p, p == 0)

        with nc.Block() as block:
            @block.sync
            def _(sp):
                for n, src in (("gate", w_gate), ("up", w_up), ("down", w_down)):
                    sp.dma_start(wf[n][:], kxn(src)).then_inc(w_in, 16)

            @block.gpsimd
            def _(g):
                g.memset(minus_half[:], -0.5).then_inc(halves_set, 1)
                g.wait_ge(halves_set, 1)
                g.wait_ge(var, 1)
                g.tensor_tensor(rstd[:], mv[:, :, 1:2], minus_half[:], ALU.pow).then_inc(rst, 1)

            @block.tensor
            def _(pe):
                pe.wait_ge(xq_ready, 1)
                for r in range(NT // TURNS):
                    if r >= 2:
                        pe.wait_ge(xT_ready, r - 1)
                    for i in range(TURNS):
                        for c in range(DC):
                            last = pe.transpose(p_T[r % 2][:, i * DC + c, :], xq[:, r * TURNS + i, c * P:(c + 1) * P],
                                                sh.identb[:])
                    last.then_inc(turned, 1)
                pe.wait_ge(asum_ready, 1)
                pe.matmul(p_d[0][:, 0:3], sh.ones[:], asum[:], start=True, stop=True).then_inc(wsum_ready, 1)
                pe.wait_ge(wq_ready, 1)
                pe.wait_ge(xT_ready, NT // TURNS)

                def gate_and_up(n):
                    for i in range(HALVES):
                        pe.wait_ge(bank_free, n * HALVES + i + 1)
                        for dst, name, done in ((p_g, "gate", g_ready), (p_u, "up", u_ready)):
                            for c in range(DC):
                                last = pe.matmul(dst[i][:], xqT[:, ds(n, 1), c, :].rearrange("p a t -> p (a t)"),
                                                 wq[name][:, c, i * HALF:(i + 1) * HALF], start=(c == 0), stop=(c == DC - 1))
                            last.then_inc(done, 1)

                def step(n, p, ahead):
                    if ahead:
                        gate_and_up(n + 1)
                    pe.wait_ge(pq_ready, n + 1)
                    for f in range(FC):
                        last = pe.transpose(p_T[p][:, f, :], pq[p][:, f * P:(f + 1) * P], sh.identb[:])
                    last.then_inc(pT_ps, 1)
                    pe.wait_ge(pT_ready, n + 1)
                    for f in range(FC):
                        last = pe.matmul(p_d[p][:, 0:D], pqT[p][:, f, :], wq["down"][:, f, :], start=(f == 0),
                                         stop=(f == FC - 1))
                    last.then_inc(d_ready, 1)

                blocks(pe, lambda: gate_and_up(0), step)

            @block.scalar
            def _(a):
                a.preload_act_table(ACT.Silu)
                for r in range(NT // TURNS):
                    a.wait_ge(turned, r + 1)
                    a.copy(xqT[:, r * TURNS:(r + 1) * TURNS, :, :], p_T[r % 2][:].rearrange("p (i c) t -> p i c t", c=DC)
                           ).then_inc(xT_ready, 1)
                a.wait_ge(scales_ready, 1)

                def gated(n, p):
                    a.copy(gs[p][:], gscale[:, ds(n, 1)])
                    a.drain()
                    for i in range(HALVES):
                        a.wait_ge(g_ready, n * HALVES + i + 1)
                        a.activation(sg[p][:, i * HALF:(i + 1) * HALF], p_g[i][:], ACT.Silu, scale=gs[p][:, 0:1]
                                     ).then_inc(sg_ready, 1)

                def step(n, p, ahead):
                    if ahead:
                        gated(n + 1, 1 - p)
                    a.wait_ge(pT_ps, n + 1)
                    a.copy(pqT[p][:], p_T[p][:]).then_inc(pT_ready, 1)

                blocks(a, lambda: gated(0, 0), step)

            @block.vector
            def _(v):
                v.drain().then_inc(bank_free, HALVES)
                for t in range(NT):
                    v.bn_stats(stats[:, t, :], sh.h[:, t, :])
                v.drain()
                for t in range(NT):
                    v.bn_aggr(mv[:, t, :], stats[:, t, :])
                v.drain()
                v.tensor_scalar(mv[:, :, 1:2], mv[:, :, 1:2], LN_EPS, None, ALU.add).then_inc(var, 1)
                v.wait_ge(rst, 1)
                for t in range(NT):
                    v.tensor_scalar(xn[:, t, :], sh.h[:, t, :], mv[:, t, 0:1], rstd[:, t, 0:1], ALU.subtract, ALU.mult)
                v.drain()
                v.tensor_reduce(amax[:], xn[:], AXX, ALU.max, apply_absolute_value=True)
                v.drain()
                v.tensor_scalar(amax[:], amax[:], 1e-5, 1.0 / QA, ALU.max, ALU.mult)
                v.drain()
                v.reciprocal(rscale[:], amax[:])
                v.drain()
                for t in range(NT):
                    v.tensor_scalar(xn[:, t, :], xn[:, t, :], rscale[:, t:t + 1], ROUND, ALU.mult, ALU.add)
                v.drain()
                v.tensor_scalar(xq[:], xn[:], ROUND, QA, ALU.subtract, ALU.min).then_inc(xq_ready, 1)
                v.wait_ge(w_in, 48)
                for i, n in enumerate(("gate", "up", "down")):
                    v.tensor_reduce(asum[:, i:i + 1], flat(wf[n]), AXX, ALU.add, apply_absolute_value=True)
                v.drain().then_inc(asum_ready, 1)
                v.wait_ge(wsum_ready, 1)
                v.tensor_scalar(wmean[:], p_d[0][:, 0:3], 1.0 / (D * F), 1e-5, ALU.mult, ALU.max)
                v.drain()
                v.reciprocal(wscale[:], wmean[:])
                v.tensor_scalar(gscale[:], amax[:], wmean[:, 0:1], None, ALU.mult)
                v.tensor_scalar(uscale[:], amax[:], wmean[:, 1:2], None, ALU.mult)
                v.drain().then_inc(scales_ready, 1)
                for i, n in enumerate(("gate", "up", "down")):
                    v.tensor_scalar(flat(wf[n]), flat(wf[n]), wscale[:, i:i + 1], ROUND, ALU.mult, ALU.add)
                v.drain()
                for n in ("gate", "up", "down"):
                    v.tensor_scalar(flat(wf[n]), flat(wf[n]), ROUND, 1.0, ALU.subtract, ALU.min)
                v.drain()
                for n in ("gate", "up", "down"):
                    v.tensor_scalar(flat(wq[n]), flat(wf[n]), -1.0, None, ALU.max)
                v.drain().then_inc(wq_ready, 1)

                def levels(n, p):
                    for i in range(HALVES):
                        half = sg[p][:, i * HALF:(i + 1) * HALF]
                        v.wait_ge(sg_ready, n * HALVES + i + 1)
                        v.wait_ge(u_ready, n * HALVES + i + 1)
                        v.scalar_tensor_tensor(half, p_u[i][:], uscale[:, ds(n, 1)], half, ALU.mult, ALU.mult
                                               ).then_inc(bank_free, 1)
                    v.drain()
                    v.tensor_reduce(pmax[p][:], sg[p][:], AXX, ALU.max, apply_absolute_value=True)
                    v.drain()
                    v.tensor_scalar(pmax[p][:], pmax[p][:], 1e-5, 1.0 / QA, ALU.max, ALU.mult)
                    v.drain()
                    v.reciprocal(pscale[p][:], pmax[p][:])
                    v.tensor_scalar(dscale[p][:], pmax[p][:], wmean[:, 2:3], None, ALU.mult)
                    v.drain()
                    v.tensor_scalar(sg[p][:], sg[p][:], pscale[p][:, 0:1], ROUND, ALU.mult, ALU.add)
                    v.drain()
                    v.tensor_scalar(pq[p][:], sg[p][:], ROUND, QA, ALU.subtract, ALU.min).then_inc(pq_ready, 1)

                def step(n, p, ahead):
                    if ahead:
                        levels(n + 1, 1 - p)
                    v.wait_ge(d_ready, n + 1)
                    v.scalar_tensor_tensor(sh.h[:, ds(n, 1), :], p_d[p][:, 0:D].unsqueeze(1), dscale[p][:, 0:1],
                                           sh.h[:, ds(n, 1), :], ALU.mult, ALU.add)

                blocks(v, lambda: levels(0, 0), step)
                v.drain()




def tower(nc, a, out):
    buf = nc.dram_tensor("slots", (SLOTS + K * T, D), F32).ap()
    obuf = nc.dram_tensor("slot_results", (SLOTS, D), F32).ap()
    with ExitStack() as ctx:
        sh = Shared()
        setup_constants(nc, ctx, sh)
        with ExitStack() as mix:
            w = {n: a["L0_attn_" + n] for n in (
                "Wr", "Ww", "Wk", "Wv", "Wo", "Wrec", "Wkey", "Wval", "time_decay", "ln1_g", "ln1_b", "ln2_g", "ln2_b")}
            W = time_mix_weights(nc, mix, w)
            embedding(nc, sh, a["x"], a["L0_tok_weight"], lambda sp, w_in: load_time_mix(sp, W, w, w_in))
            time_and_channel_mix(nc, sh, W, buf)
        with ExitStack() as moe:
            routing_state(nc, moe, sh, "s0")
            route(nc, sh, "r0", a["L0_ffn_gate_w"], "sigmoid", a["L0_ffn_expert_bias"])
            dispatch(nc, sh, "d0", buf, True, 1)
            expert_tiles(nc, sh, "x0", buf, obuf, a["L0_ffn_experts"], SHARED_TILES + ROUTED_TILES, True)
            combine(nc, sh, "c0", obuf, 1)
        attention(nc, sh, "a1", "latent", {n: a["L1_attn_" + n] for n in (
            "c_attn_w", "c_attn_b", "q2l_w", "q2l_b", "kv2l_w", "kv2l_b", "l2o_w", "l2o_b", "wqk_w", "wqk_b",
            "cproj_w", "cproj_b", "rot", "cos", "sin")})
        with ExitStack() as moe:
            routing_state(nc, moe, sh, "s1")
            route(nc, sh, "r1", a["L1_ffn_router_w"], "softmax")
            dispatch(nc, sh, "d1", buf, False, 0)
            expert_tiles(nc, sh, "x1", buf, obuf, a["L1_ffn_experts"], ROUTED_TILES, False, a["L1_ffn_b_out"])
            combine(nc, sh, "c1", obuf, 0)
        attention(nc, sh, "a2", "sparse", {n: a["L2_attn_" + n] for n in (
            "Wq", "bq", "Wk", "bk", "Wv", "bv", "Wo", "bo", "idx_k")} | {"parity": a["parity"]})
        with ExitStack() as moe:
            routing_state(nc, moe, sh, "s2")
            route(nc, sh, "r2", a["L2_ffn_w_g"], "softmax2")
            dispatch(nc, sh, "d2", buf, False, 0)
            capacity_experts(nc, sh, buf, obuf, a["L2_ffn_c_fc"], a["L2_ffn_c_proj"])
            combine(nc, sh, "c2", obuf, 0)
        with nc.sbuf_tensor("masks", [P, H, ST, S], F32) as masks:
            decay_masks(nc, sh, masks, a["L3_attn_decay_params"], a["L3_attn_mix_weights"])
            attention(nc, sh, "a3", "decay", {n: a["L3_attn_" + n] for n in (
                "Wq", "bq", "Wk", "bk", "Wv", "bv", "Wo", "bo")} | {"parity": a["parity"], "masks": masks})
        quantised_ffn(nc, sh, a["L3_ffn_w_gate"], a["L3_ffn_w_up"], a["L3_ffn_w_down"])
        store_out(nc, sh, out)


_TURNED = ["L0_attn_Wr", "L0_attn_Ww", "L0_attn_Wk", "L0_attn_Wv", "L0_attn_Wo", "L0_attn_Wkey", "L0_attn_Wval",
           "L0_attn_Wrec", "L0_ffn_gate_w", "L1_attn_c_attn_w", "L1_attn_q2l_w", "L1_attn_kv2l_w", "L1_attn_l2o_w",
           "L1_attn_wqk_w", "L1_attn_cproj_w", "L2_attn_Wq", "L2_attn_Wk", "L2_attn_Wv", "L2_attn_Wo", "L2_ffn_w_g",
           "L3_attn_Wq", "L3_attn_Wk", "L3_attn_Wv", "L3_attn_Wo", "L3_ffn_w_gate", "L3_ffn_w_up", "L3_ffn_w_down"]
_AS_IS = ["x", "L0_tok_weight", "L0_attn_ln1_g", "L0_attn_ln1_b", "L0_attn_ln2_g", "L0_attn_ln2_b",
          "L0_attn_time_decay", "L0_ffn_expert_bias", "L1_attn_c_attn_b", "L1_attn_q2l_b", "L1_attn_kv2l_b",
          "L1_attn_l2o_b", "L1_attn_wqk_b", "L1_attn_cproj_b", "L1_ffn_router_w", "L1_ffn_b_out",
          "L2_attn_bq", "L2_attn_bk", "L2_attn_bv", "L2_attn_bo", "L2_attn_idx_k", "L3_attn_bq", "L3_attn_bk",
          "L3_attn_bv", "L3_attn_bo", "L3_attn_decay_params", "L3_attn_mix_weights"]


def _chunked(*mats):
    parts = [m.reshape(m.shape[0], -1, 128, m.shape[2]).transpose(0, 2, 1, 3).reshape(m.shape[0], 128, -1)
             for m in mats]
    return np.ascontiguousarray(np.concatenate(parts, axis=2))


def kernel(**inputs):
    import concourse.bacc as bacc
    from concourse.bass_utils import run_bass_kernel_spmd as run

    nc = bacc.Bacc("TRN2", target_bir_lowering=False, num_devices=1)
    a = {n: np.asarray(v) for n, v in inputs.items()}
    turned = lambda m: np.swapaxes(m, -1, -2)
    arrays = {}
    for name in _AS_IS:
        arrays[name] = np.ascontiguousarray(a[name])
    for name in _TURNED:
        arrays[name] = np.ascontiguousarray(turned(a[name]))
    arrays["L0_ffn_experts"] = _chunked(*(turned(np.concatenate([a[f"L0_ffn_w{m}"], a[f"L0_ffn_sw{m}"][None]]))
                                          for m in (1, 3, 2)))
    b_in = a["L1_ffn_b_in"].reshape(E, DC, P).transpose(0, 2, 1)
    arrays["L1_ffn_experts"] = np.ascontiguousarray(np.concatenate(
        [_chunked(a["L1_ffn_w_in"], a["L1_ffn_w_out"]), b_in], axis=2))
    arrays["L2_ffn_c_fc"] = _chunked(a["L2_ffn_c_fc"])
    arrays["L2_ffn_c_proj"] = _chunked(a["L2_ffn_c_proj"])
    pair = np.arange(P) % LAT // 2
    angle = (np.arange(S, dtype=np.float32)[None, :]
             * (1.0 / 10000.0 ** (2.0 * pair / LAT)).astype(np.float32)[:, None]).astype(np.float32)
    arrays["L1_attn_cos"] = np.cos(angle).astype(np.float32)
    arrays["L1_attn_sin"] = np.sin(angle).astype(np.float32)
    swap = np.zeros((P, P), np.float32)
    even = np.arange(0, P, 2)
    swap[even + 1, even], swap[even, even + 1] = -1.0, 1.0
    arrays["L1_attn_rot"] = swap
    odd = (np.arange(P) // HD % 2).astype(bool)
    arrays["parity"] = np.where(np.stack([~odd, odd], axis=1), np.float32(HD ** -0.5), np.float32(0.0))
    handles = {n: nc.dram_tensor(n, v.shape, mybir.dt.from_np(v.dtype), kind="ExternalInput").ap()
               for n, v in arrays.items()}
    out = nc.dram_tensor("out", (B, S, D), F32, kind="ExternalOutput").ap()
    tower(nc, handles, out)
    result = run(nc, [arrays], core_ids=[0])
    return result.results[0]["out"]
```

```python
from contextlib import ExitStack

import numpy as np

import concourse.bass as bass
from concourse import mybir

F32 = mybir.dt.float32
BF16 = mybir.dt.bfloat16
I32 = mybir.dt.int32
U32 = mybir.dt.uint32
ALU = mybir.AluOpType
ACT = mybir.ActivationFunctionType
AXX = mybir.AxisListType.X
ds = bass.ds

P = 128
D = 256
DC = D // P
B = 8
S = 256
ST = S // P
T = B * S
NT = T // P
LN_EPS = 1e-5
ROUND = 1.5 * 2.0 ** 23


class Shared:
    pass


class Signals:

    def __init__(self, nc):
        self.nc, self.held = nc, []

    def __call__(self, name):
        self.held.append(self.nc.alloc_semaphore(name))
        return self.held[-1]

    def __enter__(self):
        return self

    def __exit__(self, *failed):
        if not failed[0]:
            self.nc.clear_and_free_semaphores(self.held)
            self.nc.all_engine_barrier()
        return False


def bc(ap, shape):
    return ap.unsqueeze(1).broadcast_to(shape)


def row_ap(vec, parts=P):
    return vec.partition_broadcast(parts)


def col_ap(vec):
    return vec.rearrange("(c p) -> p c", p=P)


def kxn(w):
    return w.rearrange("(c p) n -> p c n", p=P)


def rstd_of(g, sh, mv, rstd, var_sem, rstd_sem, count):
    g.wait_ge(var_sem, count)
    g.tensor_tensor(rstd[:], mv[:, :, 1:2], sh.minus_half[:], ALU.pow).then_inc(rstd_sem, 1)


def turn(pe, out, src, ident):
    for c in range(DC):
        for t in range(ST):
            last = pe.transpose(out[:, c, t * P:(t + 1) * P], src[:, t, c * P:(c + 1) * P], ident)
    return last


def project(pe, out, w, xT, m0, m=P):
    chunks = xT.shape[1]
    for c in range(chunks):
        last = pe.matmul(out, w[:, c, m0:m0 + m], xT[:, c, :], start=(c == 0), stop=(c == chunks - 1))
    return last


def project_rows(pe, out, xT, w, t):
    chunks = xT.shape[1]
    for c in range(chunks):
        last = pe.matmul(out, xT[:, c, t * P:(t + 1) * P], w[:, c, :], start=(c == 0), stop=(c == chunks - 1))
    return last


def setup_constants(nc, ctx, sh):
    sb = lambda name, shape, dt=F32: ctx.enter_context(nc.sbuf_tensor(name, shape, dt))
    sh.h = sb("h", [P, NT, D])
    sh.ident = sb("ident", [P, P])
    sh.identb = sb("identb", [P, P], BF16)
    sh.ones = sb("ones", [P, P])
    sh.above = sb("above", [P, P])
    sh.minus_half = sb("minus_half", [P, ST, 1])
    filled = nc.alloc_semaphore("filled")
    with nc.Block() as block:
        @block.gpsimd
        def _(g):
            g.memset(sh.ident[:], 0.0)
            g.memset(sh.identb[:], 0.0)
            g.memset(sh.ones[:], 1.0)
            g.memset(sh.above[:], 1.0)
            g.memset(sh.minus_half[:], -0.5)
            g.drain().then_inc(filled, 1)
            g.wait_ge(filled, 1)
            for m in (sh.ident, sh.identb):
                g.affine_select(out=m[:], in_=m[:], compare_op=ALU.not_equal, fill=1.0, base=0,
                                pattern=[[-1, P]], channel_multiplier=1)
            g.affine_select(out=sh.above[:], in_=sh.above[:], compare_op=ALU.is_gt, fill=0.0, base=0,
                            pattern=[[1, P]], channel_multiplier=-1)

        @block.scalar
        def _(a):
            a.preload_act_table(ACT.Exp)


def time_and_channel_mix(nc, sh, x, table, w, buf):
    F = w["Wkey"].shape[1]
    FC = F // P
    BLK, QMAX = 32, 31.0
    NB = ST * D // BLK
    with ExitStack() as ctx, Signals(nc) as signals:
        sb = lambda name, shape, dt=F32: ctx.enter_context(nc.sbuf_tensor("a0_" + name, shape, dt))
        ps = lambda name, shape, dt=F32: ctx.enter_context(nc.psum_tensor("a0_" + name, shape, dt))
        sem = lambda name: signals("a0_" + name)
        W = {n: sb(n, [P, DC, D]) for n in ("Wr", "Ww", "Wk", "Wv", "Wo", "Wrec")}
        W["Wkey"] = sb("Wkey", [P, DC, F])
        W["Wval"] = sb("Wval", [P, FC, D])
        W |= {n: sb(n, [P, D]) for n in ("ln1_g", "ln1_b", "ln2_g", "ln2_b")}
        W["time_decay"] = sb("tdecay", [P, DC])
        ids = sb("ids", [P, NT], I32)
        raw = sb("raw", [P, NT, D])
        amax, scale, safe, inv = (sb(n, [P, NB]) for n in ("amax", "scale", "safe", "inv"))
        q = sb("q", [P, NB, BLK])
        decay = sb("decay", [P, DC])
        decays = sb("decays", [P, DC, S])
        zeros = sb("zeros", [P, 8, D])
        stats, mv, rstd = sb("stats", [P, ST, 6]), sb("mv", [P, ST, 2]), sb("rstd", [P, ST, 1])
        x0 = sb("x0", [P, NT, D])
        x1 = sb("x1", [P, ST, D])
        xn1, xn2 = sb("xn1", [P, ST, D]), sb("xn2", [P, ST, D])
        xT1, xT2 = sb("xT1", [P, DC, S]), sb("xT2", [P, DC, S])
        tr, ew, e, ev = (sb(n, [P, DC, S]) for n in ("tr", "ew", "e", "ev"))
        wk, num, den = sb("wk", [P, DC, S]), sb("num", [P, DC, S]), sb("den", [P, DC, S])
        rw = sb("rw", [P, DC, S])
        kr = sb("kr", [P, FC, S])
        ksq = sb("ksq", [P, FC, S])
        trec = sb("trec", [P, ST, D])
        cm = sb("cm", [P, ST, D])
        turned1, turned2 = ps("turned1", [P, DC, S]), ps("turned2", [P, DC, S])
        p_w, p_k, p_r, p_v = (ps(n, [P, DC, S]) for n in ("p_w", "p_k", "p_r", "p_v"))
        p_orec, p_val = ps("p_orec", [P, ST, D]), ps("p_val", [P, ST, D])
        p_key = (p_w, p_r, p_k, p_v)
        var, rst, decay_ready = sem("var"), sem("rst"), sem("decay_ready")
        xn1_ready, xn2_ready, turned1_ready, turned2_ready, xT1_ready, xT2_ready = (
            sem(n) for n in ("xn1_ready", "xn2_ready", "turned1_ready", "turned2_ready", "xT1_ready", "xT2_ready"))
        proj_ready, ew_ready, kw_ready, e_ready, tr_ready, ev_ready, rw_ready = (
            sem(n) for n in ("proj_ready", "ew_ready", "kw_ready", "e_ready", "tr_ready", "ev_ready", "rw_ready"))
        o_ready, key_ready, ksq_ready, rec_ready, trec_ready, val_ready = (
            sem(n) for n in ("o_ready", "key_ready", "ksq_ready", "rec_ready", "trec_ready", "val_ready"))
        zeroed, cleared = sem("zeroed"), sem("cleared")
        ids_in, vectors_in, first_in, rest_in = (sem(n) for n in ("ids_in", "vectors_in", "first_in", "rest_in"))
        rows_in = [sem(f"rows_in{k}") for k in range(3)]
        VECTORS = ("ln1_g", "ln1_b", "ln2_g", "ln2_b")
        FIRST, REST = ("Ww", "Wk", "Wr", "Wv"), ("Wo", "Wkey", "Wrec", "Wval")
        PAIRS = FC // 2
        with nc.Block() as block:
            @block.sync
            def _(sp):
                sp.dma_start(ids[:], x.rearrange("b (t p) -> p (b t)", p=P),
                             allow_slow_non_contiguous=True).then_inc(ids_in, 16)
                for names, done in ((FIRST, first_in), (VECTORS, vectors_in)):
                    for n in names:
                        sp.dma_start(W[n][:], row_ap(w[n]) if names is VECTORS else kxn(w[n])).then_inc(done, 16)
                sp.dma_start(W["time_decay"][:], col_ap(w["time_decay"]),
                             allow_slow_non_contiguous=True).then_inc(vectors_in, 16)
                for n in REST:
                    sp.dma_start(W[n][:], kxn(w[n])).then_inc(rest_in, 16)
                sp.wait_ge(zeroed, 1)
                n = SLOTS // (P * 8)
                for j in range(n):
                    sp.dma_start(buf[j * P * 8:(j + 1) * P * 8, :].rearrange("(p r) d -> p r d", p=P),
                                 zeros[:]).then_inc(cleared, 16)
                sp.wait_ge(cleared, 16 * n)

            @block.gpsimd
            def _(g):
                def gather(b):
                    for t in range(b * ST, (b + 1) * ST):
                        g.indirect_dma_start(out=raw[:, t, :], out_offset=None, in_=table,
                                             in_offset=bass.IndirectOffsetOnAxis(ap=ids[:, t:t + 1].bitcast(U32), axis=0)
                                             ).then_inc(rows_in[min(b, 2)], 16)

                g.wait_ge(ids_in, 16)
                gather(0)
                gather(1)
                for k in range(2):
                    rstd_of(g, sh, mv, rstd, var, rst, k + 1)
                for b in range(2, B):
                    gather(b)
                g.memset(zeros[:], 0.0).then_inc(zeroed, 1)
                for k in range(2, 4):
                    rstd_of(g, sh, mv, rstd, var, rst, k + 1)
                with g.Fori(0, B - 2) as i:
                    for k in range(3):
                        rstd_of(g, sh, mv, rstd, var, rst, i * 3 + 5 + k)
                for k in range(2):
                    rstd_of(g, sh, mv, rstd, var, rst, (B - 2) * 3 + 5 + k)

            @block.tensor
            def _(pe):
                def turn_first(j):
                    pe.wait_ge(xn1_ready, j + 1)
                    turn(pe, turned1, xn1, sh.ident[:]).then_inc(turned1_ready, 1)

                def products(bank, name, xT):
                    for c in range(DC):
                        last = project(pe, bank[:, c, :], W[name], xT, c * P)
                    last.then_inc(proj_ready, 1)

                def turn_second(i):
                    pe.wait_ge(xn2_ready, i + 1)
                    turn(pe, turned2, xn2, sh.ident[:]).then_inc(turned2_ready, 1)

                def step(i, first=False, ahead=True):
                    if ahead:
                        turn_first(i + 1)
                    pe.wait_ge(rw_ready, i + 1)
                    if not first:
                        pe.wait_ge(trec_ready, i)
                    for t in range(ST):
                        last = project_rows(pe, p_orec[:, t, :], rw, W["Wo"], t)
                    last.then_inc(o_ready, 1)
                    if ahead:
                        pe.wait_ge(xT1_ready, i + 2)
                        products(p_w, "Ww", xT1)
                        products(p_k, "Wk", xT1)
                        products(p_r, "Wr", xT1)
                    turn_second(i)
                    if ahead:
                        products(p_v, "Wv", xT1)
                    pe.wait_ge(xT2_ready, i + 1)
                    read = (ew_ready, tr_ready, kw_ready, ev_ready)
                    for j in range(PAIRS):
                        if ahead:
                            pe.wait_ge(read[j], i + 2)
                        for c in range(2):
                            last = project(pe, p_key[j][:, c, :], W["Wkey"], xT2, (2 * j + c) * P)
                        last.then_inc(key_ready, 1)
                    for t in range(ST):
                        last = project_rows(pe, p_orec[:, t, :], xT2, W["Wrec"], t)
                    last.then_inc(rec_ready, 1)
                    pe.wait_ge(ksq_ready, i * PAIRS + PAIRS)
                    for t in range(ST):
                        last = project_rows(pe, p_val[:, t, :], ksq, W["Wval"], t)
                    last.then_inc(val_ready, 1)

                turn_first(0)
                pe.wait_ge(xT1_ready, 1)
                pe.wait_ge(first_in, 16 * len(FIRST))
                for bank, name in ((p_w, "Ww"), (p_k, "Wk"), (p_r, "Wr"), (p_v, "Wv")):
                    products(bank, name, xT1)
                pe.wait_ge(rest_in, 16 * len(REST))
                step(0, first=True)
                with pe.Fori(1, B - 1) as i:
                    step(i)
                step(B - 1, ahead=False)

            @block.scalar
            def _(a):
                def time_mix(j):
                    a.wait_ge(turned1_ready, j + 1)
                    a.copy(xT1[:], turned1[:]).then_inc(xT1_ready, 1)
                    a.wait_ge(proj_ready, j * 4 + 1)
                    a.activation(ew[:], p_w[:], ACT.Exp).then_inc(ew_ready, 1)
                    a.wait_ge(kw_ready, j + 1)
                    a.activation(e[:], wk[:], ACT.Exp).then_inc(e_ready, 1)
                    a.wait_ge(proj_ready, j * 4 + 3)
                    a.activation(tr[:], p_r[:], ACT.Tanh, scale=0.5).then_inc(tr_ready, 1)

                def channel_mix(i):
                    a.wait_ge(turned2_ready, i + 1)
                    a.copy(xT2[:], turned2[:]).then_inc(xT2_ready, 1)
                    for j in range(PAIRS):
                        a.wait_ge(key_ready, i * PAIRS + j + 1)
                        pair = slice(2 * j, 2 * j + 2)
                        a.activation(kr[:, pair, :], p_key[j][:], ACT.Relu)
                        a.drain()
                        a.activation(ksq[:, pair, :], kr[:, pair, :], ACT.Square).then_inc(ksq_ready, 1)
                    a.wait_ge(rec_ready, i + 1)
                    a.activation(trec[:], p_orec[:], ACT.Tanh, scale=0.5).then_inc(trec_ready, 1)

                a.wait_ge(vectors_in, 16 * (len(VECTORS) + 1))
                a.activation(decay[:], W["time_decay"][:], ACT.Exp).then_inc(decay_ready, 1)
                time_mix(0)
                with a.Fori(0, B - 1) as i:
                    time_mix(i + 1)
                    channel_mix(i)
                channel_mix(B - 1)

            @block.vector
            def _(v):
                def moments(src):
                    for t in range(ST):
                        v.bn_stats(stats[:, t, :], src(t))
                    v.drain()
                    for t in range(ST):
                        v.bn_aggr(mv[:, t, :], stats[:, t, :])
                    v.drain()
                    v.tensor_scalar(mv[:, :, 1:2], mv[:, :, 1:2], LN_EPS, None, ALU.add).then_inc(var, 1)

                def normed_with_gain(out, src, gain, bias, count):
                    moments(src)
                    for t in range(ST):
                        v.scalar_tensor_tensor(out[:, t, :], src(t), mv[:, t, 0:1], gain[:], ALU.subtract, ALU.mult)
                    v.drain()
                    v.wait_ge(rst, count)
                    for t in range(ST):
                        v.scalar_tensor_tensor(out[:, t, :], out[:, t, :], rstd[:, t, 0:1], bias[:], ALU.mult, ALU.add)

                def embed(j):
                    blocks = lambda m: m[:, ds(j * ST, ST), :].rearrange("p t (n k) -> p (t n) k", k=BLK)
                    each = lambda m: m[:].unsqueeze(2).broadcast_to([P, NB, BLK])
                    v.tensor_reduce(amax[:], blocks(raw), AXX, ALU.max, apply_absolute_value=True)
                    v.drain()
                    v.tensor_scalar(scale[:], amax[:], 1.0 / QMAX, None, ALU.mult)
                    v.drain()
                    v.scalar_tensor_tensor(safe[:], scale[:], 0.0, scale[:], ALU.is_equal, ALU.add)
                    v.drain()
                    v.reciprocal(inv[:], safe[:])
                    v.drain()
                    v.tensor_tensor(q[:], blocks(raw), each(inv), ALU.mult)
                    v.drain()
                    v.tensor_scalar(q[:], q[:], ROUND, ROUND, ALU.add, ALU.subtract)
                    v.drain()
                    v.tensor_scalar(q[:], q[:], QMAX, -QMAX, ALU.min, ALU.max)
                    v.drain()
                    v.tensor_tensor(blocks(sh.h), q[:], each(scale), ALU.mult)
                    v.drain()

                def first_norms(j, count):
                    x = lambda t: x0[:, ds(j * ST + t, 1), :]
                    src = lambda t: sh.h[:, ds(j * ST + t, 1), :]
                    moments(src)
                    v.wait_ge(rst, count)
                    for t in range(ST):
                        v.tensor_scalar(x(t), src(t), mv[:, t, 0:1], rstd[:, t, 0:1], ALU.subtract, ALU.mult)
                    v.drain()
                    moments(x)
                    for t in range(ST):
                        v.scalar_tensor_tensor(xn1[:, t:t + 1, :], x(t), mv[:, t, 0:1], W["ln1_g"][:].unsqueeze(1),
                                               ALU.subtract, ALU.mult)
                    v.drain()
                    v.wait_ge(rst, count + 1)
                    for t in range(ST):
                        last = v.scalar_tensor_tensor(xn1[:, t, :], xn1[:, t, :], rstd[:, t, 0:1], W["ln1_b"][:],
                                                      ALU.mult, ALU.add)
                    v.drain().then_inc(xn1_ready, 1)

                def time_mix(j):
                    v.wait_ge(ew_ready, j + 1)
                    v.wait_ge(proj_ready, j * 4 + 2)
                    v.tensor_tensor(wk[:], p_k[:], ew[:], ALU.subtract).then_inc(kw_ready, 1)
                    v.wait_ge(e_ready, j + 1)
                    for c in range(DC):
                        v.tensor_tensor_scan(den[:, c, :], decays[:, c, :], e[:, c, :], 0.0, ALU.mult, ALU.add)
                    v.drain()
                    v.tensor_scalar(den[:], den[:], 1e-8, None, ALU.add)
                    v.drain()
                    v.reciprocal(den[:], den[:])
                    v.wait_ge(proj_ready, j * 4 + 4)
                    v.tensor_tensor(ev[:], p_v[:], e[:], ALU.mult).then_inc(ev_ready, 1)
                    v.drain()
                    for c in range(DC):
                        v.tensor_tensor_scan(num[:, c, :], decays[:, c, :], ev[:, c, :], 0.0, ALU.mult, ALU.add)
                    v.drain()
                    v.tensor_tensor(num[:], num[:], den[:], ALU.mult)
                    v.drain()
                    v.wait_ge(tr_ready, j + 1)
                    v.scalar_tensor_tensor(rw[:], tr[:], 1.0, num[:], ALU.add, ALU.mult).then_inc(rw_ready, 1)

                def step(i, count, ahead=True, norms=True):
                    v.wait_ge(o_ready, i + 1)
                    v.scalar_tensor_tensor(x1[:], p_orec[:], 0.5, x0[:, ds(i * ST, ST), :], ALU.mult, ALU.add)
                    v.drain()
                    normed_with_gain(xn2, lambda t: x1[:, t, :], W["ln2_g"], W["ln2_b"], count)
                    v.drain().then_inc(xn2_ready, 1)
                    if ahead:
                        time_mix(i + 1)
                    v.tensor_tensor(x1[:], x1[:], sh.h[:, ds(i * ST, ST), :], ALU.add)
                    if norms:
                        embed(i + 2)
                        first_norms(i + 2, count + 1)
                    v.wait_ge(trec_ready, i + 1)
                    v.wait_ge(val_ready, i + 1)
                    v.scalar_tensor_tensor(cm[:], trec[:], 1.0, p_val[:], ALU.add, ALU.mult)
                    v.drain()
                    v.scalar_tensor_tensor(sh.h[:, ds(i * ST, ST), :], cm[:], 0.5, x1[:], ALU.mult, ALU.add)
                    v.drain()

                v.wait_ge(rows_in[0], 16 * ST)
                embed(0)
                v.wait_ge(vectors_in, 16 * (len(VECTORS) + 1))
                first_norms(0, 1)
                v.wait_ge(decay_ready, 1)
                for c in range(DC):
                    v.tensor_copy(decays[:, c, :], decay[:, c:c + 1].broadcast_to([P, S]))
                v.drain()
                time_mix(0)
                v.wait_ge(rows_in[1], 16 * ST)
                embed(1)
                first_norms(1, 3)
                v.wait_ge(rows_in[2], 16 * ST * (B - 2))
                with v.Fori(0, B - 2) as i:
                    step(i, i * 3 + 5)
                step(B - 2, (B - 2) * 3 + 5, norms=False)
                step(B - 1, (B - 2) * 3 + 6, ahead=False, norms=False)


def store_out(nc, sh, out):
    with ExitStack() as ctx, Signals(nc) as signals:
        stored = signals("stored")
        with nc.Block() as block:
            @block.sync
            def _(sp):
                for k in range(2):
                    half = slice(k * NT // 2, (k + 1) * NT // 2)
                    sp.dma_start(out.rearrange("b (t p) d -> p (b t) d", p=P)[:, half, :], sh.h[:, half, :]).then_inc(stored, 16)
                sp.wait_ge(stored, 32)


E = 8
K = 2
TILE = 256
TB = TILE // P
KT = K * NT
SHARED_TILES = T // TILE
ROUTED_TILES = K * T // TILE + E
CAP = 640
SLOTS = (SHARED_TILES + ROUTED_TILES) * TILE
TRASH = SLOTS


def routing_state(nc, ctx, sh):
    sb = lambda n, shape, dt=F32: ctx.enter_context(nc.sbuf_tensor(n, shape, dt))
    sh.slot = sb("slot", [P, KT], I32)
    sh.back = sb("back", [P, KT], I32)
    sh.weight = sb("weight", [P, KT])
    sh.tile_expert = sb("tile_expert", [1, SHARED_TILES + ROUTED_TILES], I32)


def route(nc, sh, name, gate, kind, attn, bias=None):
    wt, attn_kind, attn_w = attn
    with ExitStack() as ctx, Signals(nc) as signals:
        sb = lambda n, shape, dt=F32: ctx.enter_context(nc.sbuf_tensor(f"{name}_{n}", shape, dt))
        ps = lambda n, shape, dt=F32: ctx.enter_context(nc.psum_tensor(f"{name}_{n}", shape, dt))
        sem = lambda n: signals(f"{name}_{n}")
        gw = sb("gw", [P, DC, E])
        bias_row = sb("bias", [P, E])
        stats, mv, rstd, xn, xT = ([sb(f"{n}{p}", shape) for p in range(2)] for n, shape in (
            ("stats", [P, ST, 6]), ("mv", [P, ST, 2]), ("rstd", [P, ST, 1]), ("xn", [P, ST, D]), ("xT", [P, DC, S])))
        logits = sb("logits", [P, NT, E])
        sel = sb("sel", [P, NT, E])
        val = sb("val", [P, NT, E])
        tmp = sb("tmp", [P, NT, E])
        best = sb("best", [P, NT])
        idx = sb("idx", [P, E])
        idx8 = sb("idx8", [P, E])
        oh = sb("oh", [P, E, KT])
        ohk = sb("ohk", [P, NT, E])
        w2 = sb("w2", [P, K, NT])
        total, incl, pos, big = (sb(n, [P, E, KT]) for n in ("total", "incl", "pos", "big"))
        reset = sb("reset", [P, E, KT])
        one8 = sb("one8", [P, E])
        base, tiles, ends = sb("base", [P, E]), sb("tiles", [P, E]), sb("ends", [P, E])
        rank, ebase, valid, trash, tf = (sb(n, [P, KT]) for n in ("rank", "ebase", "valid", "trash", "tf"))
        tidx = sb("tidx", [1, ROUTED_TILES])
        tcmp = sb("tcmp", [1, ROUTED_TILES, E])
        texp = sb("texp", [1, ROUTED_TILES])
        turned = [ps(f"turned{p}", [P, DC, S]) for p in range(2)]
        p_logit = ps("p_logit", [P, NT, E])
        p_rank, p_total = ps("p_rank", [P, E, KT]), ps("p_total", [P, E, KT])
        w_in, var, rst, consts = sem("w_in"), sem("var"), sem("rst"), sem("consts")
        attn_cleared, attn_in = sem("attn_cleared"), sem("attn_in")
        xn_ready, xn_free, turned_ready, xT_ready, logit_ready, oh_ready, count_ready, soft, softed = (
            sem(n) for n in ("xn_ready", "xn_free", "turned_ready", "xT_ready", "logit_ready", "oh_ready",
                             "count_ready", "soft", "softed"))
        with nc.Block() as block:
            @block.sync
            def _(sp):
                sp.dma_start(gw[:], gate.rearrange("(c p) e -> p c e", p=P),
                             allow_slow_non_contiguous=True).then_inc(w_in, 16)
                if bias is not None:
                    sp.dma_start(bias_row[:], row_ap(bias)).then_inc(w_in, 16)
                load_attention(sp, wt, attn_kind, attn_w, attn_cleared, attn_in)

            @block.gpsimd
            def _(g):
                clear_attention(g, wt, attn_kind, attn_cleared)
                g.iota(idx[:], [[1, E]], base=0, channel_multiplier=0, allow_small_or_imprecise_dtypes=True)
                g.iota(idx8[:], [[1, E]], base=E, channel_multiplier=0, allow_small_or_imprecise_dtypes=True)
                g.iota(tidx[:], [[1, ROUTED_TILES]], base=0, channel_multiplier=0, allow_small_or_imprecise_dtypes=True)
                g.iota(base[:], [[CAP, E]], base=0, channel_multiplier=0, allow_small_or_imprecise_dtypes=True)
                g.iota(trash[:], [[P, KT]], base=TRASH, channel_multiplier=1, allow_small_or_imprecise_dtypes=True)
                g.memset(one8[:], 1.0)
                g.memset(reset[:, :, 1:KT], 1.0)
                g.memset(reset[:, :, 0:1], 0.0)
                g.drain().then_inc(consts, 1)
                with g.Fori(0, B // 2) as k:
                    for p in range(2):
                        rstd_of(g, sh, mv[p], rstd[p], var, rst, k * 2 + p + 1)

            @block.tensor
            def _(pe):
                pe.wait_ge(w_in, 16 if bias is None else 32)
                with pe.Fori(0, B // 2) as k:
                    for p in range(2):
                        pe.wait_ge(xn_ready, k * 2 + p + 1)
                        turn(pe, turned[p], xn[p], sh.ident[:]).then_inc(turned_ready, 1)
                    for p in range(2):
                        pe.wait_ge(xT_ready, k * 2 + p + 1)
                        for t in range(ST):
                            out = p_logit[:, ds(k * 2 * ST + p * ST + t, 1), :].rearrange("p a e -> p (a e)")
                            last = project_rows(pe, out, xT[p], gw, t)
                        last.then_inc(logit_ready, 1)
                pe.wait_ge(oh_ready, 1)
                pe.matmul(p_rank[:], sh.above[:], oh[:], start=True, stop=True)
                pe.matmul(p_total[:], sh.ones[:], oh[:], start=True, stop=True).then_inc(count_ready, 1)

            @block.scalar
            def _(a):
                a.drain().then_inc(xn_free, 2)
                with a.Fori(0, B // 2) as k:
                    for p in range(2):
                        a.wait_ge(turned_ready, k * 2 + p + 1)
                        a.copy(xT[p][:], turned[p][:]).then_inc(xT_ready, 1)
                        a.copy(sh.xn_all[:, ds(k * 2 * ST + p * ST, ST), :], xn[p][:]).then_inc(xn_free, 1)
                a.wait_ge(soft, 1)
                a.activation(tmp[:], tmp[:], ACT.Exp).then_inc(softed, 1)

            @block.vector
            def _(v):
                with v.Fori(0, B // 2) as k:
                    rows = lambda p, t: sh.h[:, ds(k * 2 * ST + p * ST + t, 1), :]
                    for p in range(2):
                        for t in range(ST):
                            v.bn_stats(stats[p][:, t, :], rows(p, t))
                        v.drain()
                        for t in range(ST):
                            v.bn_aggr(mv[p][:, t, :], stats[p][:, t, :])
                        v.drain()
                        v.tensor_scalar(mv[p][:, :, 1:2], mv[p][:, :, 1:2], LN_EPS, None, ALU.add).then_inc(var, 1)
                    for p in range(2):
                        v.wait_ge(xn_free, k * 2 + p + 1)
                        v.wait_ge(rst, k * 2 + p + 1)
                        for t in range(ST):
                            last = v.tensor_scalar(xn[p][:, t:t + 1, :], rows(p, t), mv[p][:, t, 0:1], rstd[p][:, t, 0:1],
                                                   ALU.subtract, ALU.mult)
                        last.then_inc(xn_ready, 1)
                v.wait_ge(logit_ready, B)
                v.tensor_copy(logits[:], p_logit[:])
                v.drain()
                v.wait_ge(consts, 1)
                v.wait_ge(w_in, 16 if bias is None else 32)
                if kind == "sigmoid":
                    v.tensor_scalar(tmp[:], logits[:], -1.0, None, ALU.mult).then_inc(soft, 1)
                    v.wait_ge(softed, 1)
                    v.tensor_scalar(tmp[:], tmp[:], 1.0, None, ALU.add)
                    v.drain()
                    v.reciprocal(val[:], tmp[:])
                    v.drain()
                    v.tensor_tensor(sel[:], val[:], bc(bias_row[:], [P, NT, E]), ALU.add)
                elif kind == "softmax":
                    v.tensor_reduce(best[:], logits[:], AXX, ALU.max)
                    v.drain()
                    v.tensor_tensor(tmp[:], logits[:], best[:].unsqueeze(2).broadcast_to([P, NT, E]),
                                    ALU.subtract).then_inc(soft, 1)
                    v.wait_ge(softed, 1)
                    v.tensor_reduce(best[:], tmp[:], AXX, ALU.add)
                    v.drain()
                    v.reciprocal(best[:], best[:])
                    v.drain()
                    v.tensor_tensor(val[:], tmp[:], best[:].unsqueeze(2).broadcast_to([P, NT, E]), ALU.mult)
                    v.drain()
                    v.tensor_copy(sel[:], val[:])
                else:
                    v.tensor_copy(val[:], logits[:])
                    v.tensor_copy(sel[:], logits[:])
                for k in range(K):
                    v.drain()
                    v.tensor_reduce(best[:], sel[:], AXX, ALU.max)
                    v.drain()
                    v.tensor_tensor(ohk[:], sel[:], best[:].unsqueeze(2).broadcast_to([P, NT, E]), ALU.is_equal)
                    v.drain()
                    v.scalar_tensor_tensor(ohk[:], ohk[:], -float(E), bc(idx8[:], [P, NT, E]), ALU.mult, ALU.add)
                    v.drain()
                    v.tensor_reduce(best[:], ohk[:], AXX, ALU.min)
                    v.drain()
                    v.tensor_tensor(ohk[:], bc(idx[:], [P, NT, E]), best[:].unsqueeze(2).broadcast_to([P, NT, E]),
                                    ALU.is_equal)
                    v.drain()
                    v.tensor_copy(oh[:, :, k * NT:(k + 1) * NT].rearrange("p e t -> p t e"), ohk[:])
                    v.scalar_tensor_tensor(sel[:], ohk[:], -3e38, sel[:], ALU.mult, ALU.add)
                    v.tensor_tensor(ohk[:], ohk[:], val[:], ALU.mult)
                    v.drain()
                    v.tensor_reduce(w2[:, k, :], ohk[:], AXX, ALU.add)
                v.drain().then_inc(oh_ready, 1)
                if kind == "softmax2":
                    v.tensor_tensor(tmp[:, :, 0], w2[:, 1, :], w2[:, 0, :], ALU.subtract)
                    v.tensor_scalar(tmp[:, :, 1:E], logits[:, :, 1:E], 0.0, None, ALU.min)
                    v.drain().then_inc(soft, 1)
                    v.wait_ge(softed, 1)
                    v.tensor_scalar(best[:], tmp[:, :, 0], 1.0, None, ALU.add)
                    v.drain()
                    v.reciprocal(w2[:, 0, :], best[:])
                    v.drain()
                    v.tensor_tensor(w2[:, 1, :], w2[:, 0, :], tmp[:, :, 0], ALU.mult)
                    v.drain()
                v.wait_ge(count_ready, 1)
                v.tensor_copy(total[:], p_total[:])
                v.drain()
                flat = lambda x: x[:].rearrange("p e k -> p (e k)")
                v.tensor_tensor_scan(flat(incl), flat(reset), flat(total), 0.0, ALU.mult, ALU.add)
                v.drain()
                v.tensor_tensor(pos[:], incl[:], total[:], ALU.subtract)
                v.drain()
                v.tensor_tensor(pos[:], pos[:], p_rank[:], ALU.add)
                if kind != "softmax2":
                    v.tensor_scalar(tiles[:], incl[:, :, KT - 1], TILE / 2 - 0.5, 1.0 / TILE, ALU.add, ALU.mult)
                    v.drain()
                    v.tensor_scalar(tiles[:], tiles[:], ROUND, ROUND, ALU.add, ALU.subtract)
                    v.drain()
                    v.tensor_tensor_scan(ends[:], one8[:], tiles[:], 0.0, ALU.mult, ALU.add)
                    v.drain()
                    v.tensor_tensor(base[:], ends[:], tiles[:], ALU.subtract)
                    v.drain()
                    first = SHARED_TILES * TILE if kind == "sigmoid" else 0
                    v.tensor_scalar(base[:], base[:], float(TILE), float(first), ALU.mult, ALU.add)
                    v.tensor_tensor(tcmp[:], ends[0:1, :].unsqueeze(1).broadcast_to([1, ROUTED_TILES, E]),
                                    tidx[:].unsqueeze(2).broadcast_to([1, ROUTED_TILES, E]), ALU.is_le)
                    v.drain()
                    v.tensor_reduce(texp[:], tcmp[:], AXX, ALU.add)
                    v.drain()
                    v.tensor_scalar(texp[:], texp[:], float(E - 1), None, ALU.min)
                    v.drain()
                    if kind == "sigmoid":
                        v.memset(sh.tile_expert[:, 0:SHARED_TILES], E)
                        v.tensor_copy(sh.tile_expert[:, SHARED_TILES:], texp[:])
                    else:
                        v.tensor_copy(sh.tile_expert[:, 0:ROUTED_TILES], texp[:])
                by_choice = lambda x: x[:].rearrange("p e k -> p k e")
                v.drain()
                v.tensor_tensor(big[:], oh[:], pos[:], ALU.mult)
                v.drain()
                v.tensor_reduce(rank[:], by_choice(big), AXX, ALU.add)
                v.drain()
                v.tensor_tensor(big[:], oh[:], base[:].unsqueeze(2).broadcast_to([P, E, KT]), ALU.mult)
                v.drain()
                v.tensor_reduce(ebase[:], by_choice(big), AXX, ALU.add)
                v.drain()
                if kind == "softmax2":
                    v.tensor_scalar(valid[:], rank[:], float(CAP), None, ALU.is_lt)
                    v.tensor_tensor(tf[:], rank[:], ebase[:], ALU.add)
                    v.drain()
                    v.tensor_tensor(tf[:], tf[:], trash[:], ALU.subtract)
                    v.drain()
                    v.tensor_tensor(tf[:], tf[:], valid[:], ALU.mult)
                    v.drain()
                    v.tensor_tensor(tf[:], tf[:], trash[:], ALU.add)
                    v.drain()
                    v.tensor_copy(sh.slot[:], tf[:])
                    v.scalar_tensor_tensor(rank[:], rank[:], float(CAP - 1), ebase[:], ALU.min, ALU.add)
                    v.drain()
                    v.tensor_copy(sh.back[:], rank[:])
                    v.tensor_tensor(sh.weight[:], w2[:].rearrange("p k t -> p (k t)"), valid[:], ALU.mult)
                else:
                    v.tensor_tensor(tf[:], rank[:], ebase[:], ALU.add)
                    v.drain()
                    v.tensor_copy(sh.slot[:], tf[:])
                    v.tensor_copy(sh.back[:], tf[:])
                    v.tensor_copy(sh.weight[:], w2[:].rearrange("p k t -> p (k t)"))
                v.drain()


SCALED_GROUP = 4


def dispatch(g, sh, buf, sent, scaled=None, scaled_ready=None):
    for j in range(KT):
        if scaled is not None and j % SCALED_GROUP == 0:
            g.wait_ge(scaled_ready, j // SCALED_GROUP + 1)
        src = sh.xn_all[:, j % NT, :] if scaled is None else scaled[:, j, :]
        g.indirect_dma_start(out=buf, out_offset=bass.IndirectOffsetOnAxis(
            ap=sh.slot[:, j:j + 1].bitcast(U32), axis=0), in_=src, in_offset=None).then_inc(sent, 16)


def scale_rows(v, sh, scaled, scaled_ready):
    for j in range(KT):
        v.tensor_scalar(scaled[:, j, :], sh.xn_all[:, j % NT, :], sh.weight[:, j:j + 1], None, ALU.mult)
        if j % SCALED_GROUP == SCALED_GROUP - 1:
            v.drain().then_inc(scaled_ready, 1)


def expert_tiles(nc, sh, name, buf, obuf, wts, n_tiles, gated, b_out=None):
    WCOLS = wts.shape[2]
    W2 = WCOLS - DC * D
    with ExitStack() as ctx, Signals(nc) as signals:
        sb = lambda n, shape, dt=F32: ctx.enter_context(nc.sbuf_tensor(f"{name}_{n}", shape, dt))
        ps = lambda n, shape, dt=F32: ctx.enter_context(nc.psum_tensor(f"{name}_{n}", shape, dt))
        sem = lambda n: signals(f"{name}_{n}")
        wbuf = [sb(f"w{p}", [P, WCOLS]) for p in range(2)]
        w1 = [w[:, 0:DC * D].rearrange("p (c n) -> p c n", c=DC) for w in wbuf]
        w3 = [w[:, DC * D:2 * DC * D].rearrange("p (c n) -> p c n", c=DC) for w in wbuf]
        w2 = [w[:, W2:WCOLS].rearrange("p (c n) -> p c n", c=DC) for w in wbuf]
        bo = [sb(f"bo{p}", [P, D]) for p in range(2)] if not gated else None
        xin = [sb(f"xin{p}", [P, TB, D]) for p in range(2)]
        xT = [sb(f"xT{p}", [P, DC, TILE]) for p in range(2)]
        sg = sb("sg", [P, DC, TILE])
        hT = sb("hT", [P, DC, TILE])
        y = [sb(f"y{p}", [P, TB, D]) for p in range(2)]
        p_t = [ps(f"p_t{p}", [P, DC, TILE]) for p in range(2)]
        p_g = [ps(f"p_g{p}", [P, DC, TILE]) for p in range(2)]
        p_u = [ps(f"p_u{p}", [P, DC, TILE]) for p in range(2)] if gated else None
        p_o = [ps(f"p_o{p}", [P, TB, D]) for p in range(2)]
        scaled = sb("scaled", [P, KT, D]) if gated else None
        scaled_ready, sent = sem("scaled_ready"), sem("sent")
        x_in = [sem(f"x_in{p}") for p in range(2)]
        w_in, w2_in = ([sem(f"{n}{p}") for p in range(2)] for n in ("w_in", "w2_in"))
        stored = [sem(f"stored{p}") for p in range(2)]
        turned, xT_ready, g_ready, u_ready, sg_ready, h_ready, o_ready, y_ready, bank_free = (
            sem(n) for n in ("turned", "xT_ready", "g_ready", "u_ready", "sg_ready", "h_ready", "o_ready", "y_ready",
                             "bank_free"))
        rows = lambda m, i: m[ds(i * TILE, TILE), :].rearrange("(p t) d -> p t d", t=TB)
        W2_DMAS = 1 if gated else 2
        with nc.Block() as block:
            @block.sync
            def _(sp):
                def load(i, p, before_w2=None):
                    e = sp.value_load(sh.tile_expert[0:1, ds(i, 1)], min_val=0, max_val=wts.shape[0] - 1)
                    matrices = wts[ds(e, 1), :, :].rearrange("a p n -> (a p) n")
                    sp.dma_start(wbuf[p][:, 0:W2], matrices[:, 0:W2]).then_inc(w_in[p], 16)
                    if before_w2:
                        before_w2()
                    sp.dma_start(wbuf[p][:, W2:WCOLS], matrices[:, W2:WCOLS]).then_inc(w2_in[p], 16)
                    if not gated:
                        sp.dma_start(bo[p][:], b_out[ds(e, 1), :].rearrange("a n -> (a n)").partition_broadcast(P)
                                     ).then_inc(w2_in[p], 16)

                def load_x(i, p):
                    sp.dma_start(xin[p][:], rows(buf, i)).then_inc(x_in[p], 16)

                def load_sequence(i, p):
                    sp.dma_start(xin[p][:], sh.xn_all[:, ds(i * ST, ST), :]).then_inc(x_in[p], 16)

                def reload(k, p, rows_of):
                    sp.wait_ge(turned, k * 2 + (p - 1))
                    rows_of(k * 2 + p, p)
                    sp.wait_ge(u_ready if gated else h_ready, k * 2 + (p - 1))

                    def used():
                        sp.wait_ge(o_ready, k * 2 + (p - 1))
                        if not gated:
                            sp.wait_ge(y_ready, k * 2 + (p - 1))

                    load(k * 2 + p, p, used)

                for p in range(2):
                    load(p, p)
                if gated:
                    for p in range(2):
                        load_sequence(p, p)
                    with sp.Fori(1, SHARED_TILES // 2) as k:
                        for p in range(2):
                            reload(k, p, load_sequence)
                sp.wait_ge(sent, 16 * KT)
                if not gated:
                    for p in range(2):
                        load_x(p, p)
                with sp.Fori(SHARED_TILES // 2 if gated else 1, n_tiles // 2) as k:
                    for p in range(2):
                        reload(k, p, load_x)

            @block.gpsimd
            def _(g):
                dispatch(g, sh, buf, sent, scaled, scaled_ready)

            @block.tensor
            def _(pe):
                def turn_tile(i, k, p):
                    pe.wait_ge(x_in[p], k * 16 + 16)
                    turn(pe, p_t[p], xin[p], sh.ident[:]).then_inc(turned, 1)

                def tile(i, k, p, ahead):
                    pe.wait_ge(xT_ready, i + 1)
                    pe.wait_ge(w_in[p], k * 16 + 16)
                    for c in range(DC):
                        last = project(pe, p_g[p][:, c, :], w1[p], xT[p], c * P)
                    last.then_inc(g_ready, 1)
                    if gated:
                        for c in range(DC):
                            last = project(pe, p_u[p][:, c, :], w3[p], xT[p], c * P)
                        last.then_inc(u_ready, 1)
                    if ahead:
                        turn_tile(i + 1, k + p, 1 - p)
                    pe.wait_ge(h_ready, i + 1)
                    pe.wait_ge(w2_in[p], k * (16 * W2_DMAS) + 16 * W2_DMAS)
                    for t in range(TB):
                        last = project_rows(pe, p_o[p][:, t, :], hT, w2[p], t)
                    last.then_inc(o_ready, 1)

                turn_tile(0, 0, 0)
                with pe.Fori(0, n_tiles // 2 - 1) as k:
                    for p in range(2):
                        tile(k * 2 + p, k, p, True)
                for p in range(2):
                    tile(n_tiles - 2 + p, n_tiles // 2 - 1, p, p == 0)

            @block.scalar
            def _(a):
                def copy_turned(i, p):
                    a.wait_ge(turned, i + 1)
                    a.copy(xT[p][:], p_t[p][:]).then_inc(xT_ready, 1)

                def store(i, p):
                    a.wait_ge(y_ready, i + 1)
                    a.dma_start(rows(obuf, i), y[p][:]).then_inc(stored[p], 16)

                def tile(i, p, first, ahead):
                    a.wait_ge(g_ready, i + 1)
                    if gated:
                        a.activation(sg[:], p_g[p][:], ACT.Silu).then_inc(sg_ready, 1)
                    else:
                        for c in range(DC):
                            last = a.activation(hT[:, c, :], p_g[p][:, c, :], ACT.Gelu_apprx_tanh,
                                                bias=wbuf[p][:, W2 - DC + c:W2 - DC + c + 1])
                        last.then_inc(h_ready, 1)
                    if ahead:
                        copy_turned(i + 1, 1 - p)
                    if not first:
                        store(i - 1, 1 - p)

                a.preload_act_table(ACT.Silu if gated else ACT.Gelu_apprx_tanh)
                copy_turned(0, 0)
                tile(0, 0, True, True)
                tile(1, 1, False, True)
                with a.Fori(1, n_tiles // 2 - 1) as k:
                    for p in range(2):
                        tile(k * 2 + p, p, False, True)
                for p in range(2):
                    tile(n_tiles - 2 + p, p, False, p == 0)
                store(n_tiles - 1, 1)
                for p in range(2):
                    a.wait_ge(stored[p], 16 * (n_tiles // 2))
                a.preload_act_table(ACT.Exp)

            @block.vector
            def _(v):
                def tile(i, k, p, reused):
                    if gated:
                        v.wait_ge(sg_ready, i + 1)
                        v.wait_ge(u_ready, i + 1)
                        v.tensor_tensor(hT[:], sg[:], p_u[p][:], ALU.mult).then_inc(h_ready, 1)
                    v.wait_ge(o_ready, i + 1)
                    if reused:
                        v.wait_ge(stored[p], k * 16)
                    if gated:
                        v.tensor_copy(y[p][:], p_o[p][:]).then_inc(y_ready, 1)
                    else:
                        v.tensor_tensor(y[p][:], p_o[p][:], bc(bo[p][:], [P, TB, D]), ALU.add).then_inc(y_ready, 1)

                if gated:
                    scale_rows(v, sh, scaled, scaled_ready)
                for p in range(2):
                    tile(p, 0, p, False)
                with v.Fori(1, n_tiles // 2) as k:
                    for p in range(2):
                        tile(k * 2 + p, k, p, True)




H = 16
HD = D // H
LAT = 32
GROUP_ROWS = 32
NEG = -1e30
SAMPLES = 40


class TernaryWeights:
    NAMES = ("gate", "up", "down")

    def __init__(self, nc, ctx, sources):
        self.src = sources
        F = sources["gate"].shape[1]
        sb = lambda n, shape, dt=F32: ctx.enter_context(nc.sbuf_tensor("tw_" + n, shape, dt))
        shapes = {"gate": [P, DC, F], "up": [P, DC, F], "down": [P, F // P, D]}
        self.elements = D * F
        self.wf = {n: sb(n, s) for n, s in shapes.items()}
        self.wq = {n: sb(n + "q", s, BF16) for n, s in shapes.items()}
        self.asum, self.wmean, self.wscale = sb("asum", [P, 3]), sb("wmean", [P, 3]), sb("wscale", [P, 3])

    def signals(self, sem):
        self.w_in, self.asum_ready, self.wsum_ready = (
            sem("tw_" + n) for n in ("w_in", "asum_ready", "wsum_ready"))

    def load(self, sp):
        for n in self.NAMES:
            sp.dma_start(self.wf[n][:], kxn(self.src[n])).then_inc(self.w_in, 16)

    def add_up(self, v, i):
        if i == 0:
            v.wait_ge(self.w_in, 16 * len(self.NAMES))
        v.tensor_reduce(self.asum[:, i:i + 1], self.wf[self.NAMES[i]][:].rearrange("p c n -> p (c n)"), AXX, ALU.add,
                        apply_absolute_value=True).then_inc(self.asum_ready, 1)

    def add_partitions(self, pe, ones, bank):
        pe.wait_ge(self.asum_ready, len(self.NAMES))
        pe.matmul(bank, ones, self.asum[:], start=True, stop=True).then_inc(self.wsum_ready, 1)

    def means(self, v, bank):
        v.wait_ge(self.wsum_ready, 1)
        v.tensor_scalar(self.wmean[:], bank, 1.0 / self.elements, 1e-5, ALU.mult, ALU.max)
        v.drain()
        v.reciprocal(self.wscale[:], self.wmean[:])
        v.drain()

    def quantise(self, v, step):
        i, part = step // 3, step % 3
        flat = lambda m: m[self.NAMES[i]][:].rearrange("p c n -> p (c n)")
        if part == 0:
            v.tensor_scalar(flat(self.wf), flat(self.wf), self.wscale[:, i:i + 1], ROUND, ALU.mult, ALU.add)
        if part == 1:
            v.tensor_scalar(flat(self.wf), flat(self.wf), ROUND, 1.0, ALU.subtract, ALU.min)
        if part == 2:
            v.tensor_scalar(flat(self.wq), flat(self.wf), -1.0, None, ALU.max)
        v.drain()


class DecayMasks:
    N = 2

    def __init__(self, nc, ctx, signals, masks, decay_params, mix_weights):
        N = self.N
        sb = lambda n, shape, dt=F32: ctx.enter_context(nc.sbuf_tensor("dm_" + n, shape, dt))
        self.masks, self.decay_params, self.mix_weights = masks, decay_params, mix_weights
        self.dist, self.far = sb("dist", [P, ST, S]), sb("far", [P, ST, S])
        self.dp, self.lnd = sb("dp", [P, H * N]), sb("lnd", [P, H * N])
        self.mw, self.ex = sb("mw", [P, H, N]), sb("ex", [P, H, N])
        self.top = sb("top", [P, H])
        self.powers = [sb(f"powers{n}", [P, ST, S]) for n in range(2)]
        (self.came, self.iota_done, self.clipped, self.shifted, self.exped, self.logged, self.dist_ready,
         self.power_ready, self.power_used) = (
            signals("dm_" + n) for n in ("came", "iota_done", "clipped", "shifted", "exped", "logged", "dist_ready",
                                         "power_ready", "power_used"))

    def sync(self, sp):
        sp.dma_start(self.dp[:], row_ap(self.decay_params.rearrange("h n -> (h n)"))).then_inc(self.came, 16)
        sp.dma_start(self.mw[:].rearrange("p h n -> p (h n)"), row_ap(self.mix_weights.rearrange("h n -> (h n)"))
                     ).then_inc(self.came, 16)

    def gpsimd(self, g):
        g.iota(self.dist[:], [[P, ST], [-1, S]], base=0, channel_multiplier=1,
               allow_small_or_imprecise_dtypes=True).then_inc(self.iota_done, 1)

    def scalar(self, a):
        a.wait_ge(self.shifted, 1)
        a.activation(self.ex[:], self.mw[:], ACT.Exp).then_inc(self.exped, 1)
        a.wait_ge(self.clipped, 1)
        a.activation(self.lnd[:], self.dp[:], ACT.Ln).then_inc(self.logged, 1)
        a.wait_ge(self.logged, 1)
        a.wait_ge(self.dist_ready, 1)
        for j in range(H * self.N):
            if j >= 2:
                a.wait_ge(self.power_used, j - 1)
            a.activation(self.powers[j % 2][:], self.dist[:], ACT.Exp, scale=self.lnd[:, j:j + 1]
                         ).then_inc(self.power_ready, 1)

    def vector(self, v):
        N, dist, far, ex, mw, top, powers, masks = (
            self.N, self.dist, self.far, self.ex, self.mw, self.top, self.powers, self.masks)
        v.wait_ge(self.came, 32)
        v.tensor_scalar(self.dp[:], self.dp[:], 0.01, 0.9999, ALU.max, ALU.min).then_inc(self.clipped, 1)
        v.tensor_reduce(top[:], mw[:], AXX, ALU.max)
        v.drain()
        v.tensor_tensor(mw[:], mw[:], top[:].unsqueeze(2).broadcast_to([P, H, N]), ALU.subtract
                        ).then_inc(self.shifted, 1)
        v.wait_ge(self.iota_done, 1)
        v.tensor_scalar(far[:], dist[:], -1.0, None, ALU.mult)
        v.drain()
        v.tensor_tensor(dist[:], dist[:], far[:], ALU.max).then_inc(self.dist_ready, 1)
        v.wait_ge(self.exped, 1)
        v.tensor_reduce(top[:], ex[:], AXX, ALU.add)
        v.drain()
        v.reciprocal(top[:], top[:])
        v.drain()
        v.tensor_tensor(ex[:], ex[:], top[:].unsqueeze(2).broadcast_to([P, H, N]), ALU.mult)
        v.drain()
        for h in range(H):
            v.wait_ge(self.power_ready, N * h + 1)
            v.tensor_scalar(masks[:, h, :, :], powers[0][:], ex[:, h, 0:1], None, ALU.mult
                            ).then_inc(self.power_used, 1)
            v.wait_ge(self.power_ready, N * h + 2)
            v.wait_ge(self.power_used, N * h + 1)
            v.scalar_tensor_tensor(masks[:, h, :, :], powers[1][:], ex[:, h, 1:2], masks[:, h, :, :],
                                   ALU.mult, ALU.add).then_inc(self.power_used, 1)


def attention_weights(nc, ctx, name, kind):
    sb = lambda n, shape, dt=F32: ctx.enter_context(nc.sbuf_tensor(f"{name}_{n}", shape, dt))
    wt = Shared()
    wt.Wq, wt.Wk, wt.Wv, wt.Wo = (sb(n, [P, DC, D]) for n in ("Wq", "Wk", "Wv", "Wo"))
    wt.bq, wt.bk, wt.bo = sb("bq", [P, DC]), sb("bk", [P, DC]), sb("bo", [P, D])
    if kind == "latent":
        wt.bvf = sb("bvf", [P, DC])
        wt.bd_q, wt.bd_k, wt.bd_o = (sb(n, [P, 2, P]) for n in ("bd_q", "bd_k", "bd_o"))
        wt.bd_kv, wt.bd_qk = sb("bd_kv", [P, D]), sb("bd_qk", [P, P])
        wt.rot, wt.cos, wt.sin = sb("rot", [P, P]), sb("cos", [P, S]), sb("sin", [P, S])
        wt.bl_q, wt.bl_k, wt.bl_qk, wt.bl_o = (sb(n, [P, 1]) for n in ("bl_q", "bl_k", "bl_qk", "bl_o"))
        wt.bl_v = sb("bl_v", [P, LAT])
    else:
        wt.bv, wt.parity = sb("bv", [P, D]), sb("parity", [P, 2])
    if kind == "sparse":
        wt.idx_i, wt.bvc = sb("idx_i", [P, SAMPLES], I32), sb("bvc", [P, DC])
    return wt


def clear_attention(g, wt, kind, cleared):
    if kind == "latent":
        for t in (wt.bd_q, wt.bd_k, wt.bd_kv, wt.bd_o, wt.bd_qk):
            g.memset(t[:], 0.0)
    g.drain().then_inc(cleared, 1)


def load_attention(sp, wt, kind, w, cleared, came):
    def load(dst, src, **how):
        sp.dma_start(dst, src, **how).then_inc(came, 16)
        loads.append(dst)

    loads = []
    if kind == "latent":
        for i, t in enumerate((wt.Wq, wt.Wk, wt.Wv)):
            load(t[:], kxn(w["c_attn_w"])[:, :, i * D:(i + 1) * D])
        for i, t in enumerate((wt.bq, wt.bk, wt.bvf)):
            load(t[:], col_ap(w["c_attn_b"][i * D:(i + 1) * D]), allow_slow_non_contiguous=True)
        load(wt.Wo[:], kxn(w["cproj_w"]))
        load(wt.bo[:], row_ap(w["cproj_b"]))
        for t, n in ((wt.rot, "rot"), (wt.cos, "cos"), (wt.sin, "sin")):
            load(t[:], w[n])
        col = lambda x: x.rearrange("(l a) -> l a", a=1)
        for g in range(P // LAT):
            rows = slice(g * LAT, (g + 1) * LAT)
            for t, n in ((wt.bl_q, "q2l_b"), (wt.bl_k, "kv2l_b"), (wt.bl_qk, "wqk_b")):
                load(t[rows, :], col(w[n]))
        for g in range(P // HD):
            load(wt.bl_o[g * HD:(g + 1) * HD, :], col(w["l2o_b"]))
        load(wt.bl_v[:], row_ap(w["kv2l_b"]))
        sp.wait_ge(cleared, 1)
        for g in range(P // HD):
            f = slice(g * HD, (g + 1) * HD)
            lat = slice(g % 4 * LAT, (g % 4 + 1) * LAT)
            load(wt.bd_q[f, g // 4, lat], w["q2l_w"])
            load(wt.bd_k[f, g // 4, lat], w["kv2l_w"])
            load(wt.bd_kv[f, g * LAT:(g + 1) * LAT], w["kv2l_w"])
            load(wt.bd_o[lat, g // 4, f], w["l2o_w"])
        for g in range(P // LAT):
            lat = slice(g * LAT, (g + 1) * LAT)
            load(wt.bd_qk[lat, lat], w["wqk_w"])
    else:
        for t, n in ((wt.bq, "bq"), (wt.bk, "bk")):
            load(t[:], col_ap(w[n]), allow_slow_non_contiguous=True)
        for t, n in ((wt.Wq, "Wq"), (wt.Wk, "Wk"), (wt.Wv, "Wv"), (wt.Wo, "Wo")):
            load(t[:], kxn(w[n]))
        load(wt.bo[:], row_ap(w["bo"]))
        load(wt.bv[:], row_ap(w["bv"]))
        load(wt.parity[:], w["parity"])
    if kind == "sparse":
        load(wt.idx_i[:], row_ap(w["idx_k"]))
        load(wt.bvc[:], col_ap(w["bv"]), allow_slow_non_contiguous=True)
    sp.wait_ge(came, 16 * len(loads))


def attention(nc, sh, name, kind, wt, results, shared=False, masks=None, ternary=None):
    latent, sparse, decayed = kind == "latent", kind == "sparse", kind == "decay"
    V = LAT if latent else HD
    CC = H * V // P
    KEYS = [P * (t + 1) if latent else S for t in range(ST)]
    SCOL = [sum(KEYS[:t]) for t in range(ST)]
    SW = sum(KEYS)
    LATE = 0 if sparse else 1
    PICK_HEADS = (5, 6, 7, 8, 9)
    ACT_COPIES = [not sparse or h >= 7 for h in range(H)]
    with ExitStack() as ctx, Signals(nc) as signals:
        sb = lambda n, shape, dt=F32: ctx.enter_context(nc.sbuf_tensor(f"{name}_{n}", shape, dt))
        ps = lambda n, shape, dt=F32: ctx.enter_context(nc.psum_tensor(f"{name}_{n}", shape, dt))
        sem = lambda n: signals(f"{name}_{n}")
        stats, mv, rstd = sb("stats", [P, ST, 6]), sb("mv", [P, ST, 2]), sb("rstd", [P, ST, 1])
        xn = sb("xn", [P, ST, D])
        xT = sb("xT", [P, DC, S])
        Wq, Wk, Wv, Wo, bq, bk, bo = wt.Wq, wt.Wk, wt.Wv, wt.Wo, wt.bq, wt.bk, wt.bo
        gathered = [sb(f"gathered{p}", [P, K * ST, D]) for p in range(2)]
        from_shared = [sb(f"from_shared{p}", [P, ST, D]) for p in range(2)] if shared else None
        pr = [sb(f"pr{i}", [P, SW]) for i in range(2)]
        prT = [sb(f"prT{i}", [P, SW]) for i in range(2)]
        negmax = sb("negmax", [P, H, ST])
        rsum = [sb(f"rsum{p}", [P, ST, H]) for p in range(2)]
        rden = sb("rden", [P, ST, H])
        rwide = sb("rwide", [P, ST, H, V])
        ctx_raw = sb("ctx_raw", [P, CC, S])
        cT = sb("cT", [P, CC, S])
        A, Bk, Dk = (ps(n, [P, 2, 512]) for n in ("A", "B", "D"))
        C = ps("C", [P, 2, 512])
        halves = lambda bank: bank.rearrange("p (a s) -> p a s", a=2)
        chunks4 = lambda t: t[:].rearrange("p b (a s) -> p (b a) s", a=2)
        D0, D1, C1 = halves(Dk[:, 0, :]), halves(Dk[:, 1, :]), halves(C[:, 1, :])
        c_ps = chunks4(C)[:, 0:CC, :]
        z = {n: sem(n) for n in (
            "gathered0", "gathered1", "shared0", "shared1", "added", "var", "rst", "xn_ready", "turned", "xT_ready", "q_ps", "k_ps", "v_ps", "q_ready", "k_ready",
            "v_ready", "s_ps", "neg_ready", "exp_ready", "pT_ps", "pT_ready_a", "pT_ready_v", "o_ps", "rden_ready", "rwide_ready", "r_ps",
            "ctx_read", "ctx_ready", "out_ps", "out_read", "consts")}
        if ternary:
            ternary.signals(signals)
        copies = [z["pT_ready_a" if on_act else "pT_ready_v"] for on_act in ACT_COPIES]
        copied_before = [ACT_COPIES[:h].count(ACT_COPIES[h]) for h in range(H)]
        if latent:
            qf, kf, vf = (sb(n, [P, DC, S]) for n in ("qf", "kf", "vf"))
            ql, kl, qr, t1, t2 = (sb(n, [P, 4, S]) for n in ("ql", "kl", "qr", "t1", "t2"))
            kr, qq = ([sb(f"{n}{p}", [P, 4, S]) for p in range(2)] for n in ("kr", "qq"))
            vl = [sb(f"vl{p}", [P, ST, H, LAT]) for p in range(2)]
            bvf, bd_q, bd_k, bd_kv, bd_o, bd_qk = wt.bvf, wt.bd_q, wt.bd_k, wt.bd_kv, wt.bd_o, wt.bd_qk
            rot, cos, sin = wt.rot, wt.cos, wt.sin
            bl_q, bl_k, bl_qk, bl_o, bl_v = wt.bl_q, wt.bl_k, wt.bl_qk, wt.bl_o, wt.bl_v
            mask = sb("mask", [P, SW])
            yT = sb("yT", [P, DC, S])
            z.update({n: sem(n) for n in (
                "ql_ps", "kl_ps", "vl_ps", "rq_ps", "rk_ps", "qk_ps", "vf_ready", "ql_ready",
                "kl_ready", "vl_ready", "qcos_ready", "kcos_ready", "qsin_ready", "ksin_ready", "qr_ready", "kr_ready",
                "qq_ready", "y_ps", "y_ready")})
            keys, qrows = kr, [qq, qq]
        else:
            qe, qo, kT = ([sb(f"{n}{p}", [P, DC, S]) for p in range(2)] for n in ("qe", "qo", "kT"))
            ve, vo = ([sb(f"{n}{p}", [P, ST, H // 2, 2, HD]) for p in range(2)] for n in ("ve", "vo"))
            bv, parity = wt.bv, wt.parity
            bqp = sb("bqp", [P, 2, DC])
            z.update({n: sem(n) for n in ("bqp_ready", "qo_ready")})
            keys, qrows = kT, [qe, qo]
        if latent or decayed:
            sm = [sb(f"sm{i}", [P, SW]) for i in range(2)]
        if sparse:
            idx_i, idx_f, neg_i = wt.idx_i, sb("idx_f", [P, SAMPLES]), sb("neg_i", [P, SAMPLES])
            tok = sb("tok", [P, ST])
            pick = sb("pick", [P, ST, P])
            xsT, ksT = sb("xsT", [P, DC, P]), sb("ksT", [P, DC, SAMPLES])
            ksum = sb("ksum", [P, DC])
            qs = sb("qs", [P, DC, S])
            bqs = sb("bqs", [P, DC])
            kd = sb("kd", [P, DC, 8 * (SAMPLES + 1)])
            kd_keys = kd[:, :, 0:8 * SAMPLES].rearrange("p c (h u) -> p c h u", u=SAMPLES)
            kd_sums = kd[:, :, 8 * SAMPLES:]
            own = sb("own", [P, 8])
            headsel = sb("headsel", [H, D])
            smax = sb("smax", [P, ST, H])
            mwork, best8 = sb("mwork", [H, S]), sb("best8", [H, 8])
            mrow = [sb(f"mrow{p}", [H, S]) for p in range(2)]
            bvc = wt.bvc
            meanT = [sb(f"meanT{p}", [P, 2, DC]) for p in range(2)]
            mpart = sb("mpart", [P, DC, S])
            z.update({n: sem(n) for n in (
                "iotas", "pick_ready", "xs_ps", "xs_ready", "ks_ps", "ks_ready", "kd_ready", "ss_ps", "ss_read",
                "stand_ready", "m_ps", "rows_ready", "kept_ps")})
        def head_rows(h):
            if latent:
                return h // 4, (h % 4) * GROUP_ROWS, 0
            return h // 8, (h % 8) // 2 * GROUP_ROWS, h % 2

        def walk(engine, first, sequence, last):
            first()
            sequence(0, 0, False, True)
            with engine.Fori(0, B // 2 - 1) as k:
                sequence(k * 2 + 1, 1, True, True)
                sequence(k * 2 + 2, 0, True, True)
            sequence(B - 1, (B - 1) % 2, True, False)
            last()

        with nc.Block() as block:
            @block.sync
            def _(sp):
                if ternary:
                    sp.wait_ge(z["added"], 1)
                    ternary.load(sp)
                if shared:
                    for b in range(B):
                        if b >= 2:
                            sp.wait_ge(z["added"], b - 1)
                        sp.dma_start(from_shared[b % 2][:], results[b * S:(b + 1) * S, :].rearrange("(p t) d -> p t d", t=ST)
                                     ).then_inc(z[f"shared{b % 2}"], 16)

            @block.gpsimd
            def _(g):
                def gather(b):
                    for k in range(K):
                        for t in range(ST):
                            j = k * NT + b * ST + t
                            g.indirect_dma_start(
                                out=gathered[b % 2][:, k * ST + t, :], out_offset=None, in_=results,
                                in_offset=bass.IndirectOffsetOnAxis(ap=sh.back[:, j:j + 1].bitcast(U32), axis=0)
                            ).then_inc(z[f"gathered{b % 2}"], 16)

                gather(0)
                if latent:
                    g.memset(mask[:], 0.0)
                    g.drain()
                    for t in range(ST):
                        m = mask[:, SCOL[t]:SCOL[t] + KEYS[t]]
                        g.affine_select(out=m, in_=m, compare_op=ALU.is_ge, fill=NEG, base=t * P,
                                        pattern=[[-1, KEYS[t]]], channel_multiplier=1)
                    g.drain().then_inc(z["consts"], 1)
                if sparse:
                    g.iota(tok[:], [[P, ST]], base=0, channel_multiplier=1, allow_small_or_imprecise_dtypes=True)
                    g.memset(own[:], 1.0)
                    g.memset(headsel[:], 1.0)
                    g.drain()
                    g.affine_select(out=own[:], in_=own[:], compare_op=ALU.is_ge, fill=0.0, base=0,
                                    pattern=[[-HD, 8]], channel_multiplier=1)
                    g.affine_select(out=headsel[:], in_=headsel[:], compare_op=ALU.is_ge, fill=0.0, base=0,
                                    pattern=[[1, D]], channel_multiplier=-HD)
                    g.drain()
                    g.affine_select(out=own[:], in_=own[:], compare_op=ALU.is_ge, fill=0.0, base=HD - 1,
                                    pattern=[[HD, 8]], channel_multiplier=-1)
                    g.affine_select(out=headsel[:], in_=headsel[:], compare_op=ALU.is_ge, fill=0.0, base=HD - 1,
                                    pattern=[[-1, D]], channel_multiplier=HD)
                    g.drain().then_inc(z["iotas"], 1)
                gather(1)
                def widen(b):
                    g.wait_ge(z["rden_ready"], b + 1)
                    g.tensor_copy(rwide[:], rden[:].unsqueeze(3).broadcast_to([P, ST, H, V])).then_inc(z["rwide_ready"], 1)

                for b in range(B):
                    rstd_of(g, sh, mv, rstd, z["var"], z["rst"], b + 1)
                    if latent:
                        g.wait_ge(z["ql_ready"], b + 1)
                        g.tensor_tensor(t1[:], ql[:], bc(cos[:], [P, 4, S]), ALU.mult).then_inc(z["qcos_ready"], 1)
                        g.wait_ge(z["qcos_ready"], b + 1)
                        g.wait_ge(z["qsin_ready"], b + 1)
                        g.tensor_tensor(qr[:], t1[:], t2[:], ALU.add).then_inc(z["qr_ready"], 1)
                        g.wait_ge(z["kl_ready"], b + 1)
                        g.wait_ge(z["qr_ready"], b + 1)
                        g.tensor_tensor(t1[:], kl[:], bc(cos[:], [P, 4, S]), ALU.mult).then_inc(z["kcos_ready"], 1)
                    if b + 2 < B:
                        g.wait_ge(z["added"], b + 1)
                        gather(b + 2)
                    if b >= 1:
                        widen(b - 1)
                widen(B - 1)

            @block.tensor
            def _(pe):
                def scores(b, p, h):
                    c, r, odd = head_rows(h)
                    rows = slice(r, r + GROUP_ROWS)
                    for t in range(ST):
                        last = pe.matmul(A[:, h % 2, SCOL[t]:SCOL[t] + KEYS[t]], qrows[odd][p][rows, c, t * P:(t + 1) * P],
                                         keys[p][rows, c, 0:KEYS[t]], start=True, stop=True)
                    last.then_inc(z["s_ps"], 1)

                def first_scores(b, p):
                    pe.wait_ge(z["qq_ready" if latent else "q_ready"], b + 1)
                    if sparse:
                        pe.wait_ge(z["qo_ready"], b + 1)
                    pe.wait_ge(z["kr_ready" if latent else "k_ready"], b + 1)
                    pe.wait_ge(z["vl_ready" if latent else "v_ready"], b + 1)
                    scores(b, p, 0)

                def turn_probs(b, h):
                    pe.wait_ge(z["exp_ready"], b * H + h + 1)
                    for t in range(ST):
                        for kb in range(KEYS[t] // P):
                            at = t * P if kb == 0 else S + (t * P if not latent else 0)
                            last = pe.transpose(Bk[:, h % 2, at:at + P], pr[h % 2][:, SCOL[t] + kb * P:SCOL[t] + (kb + 1) * P],
                                                sh.ident[:])
                    last.then_inc(z["pT_ps"], 1)

                def values(b, p, h):
                    pe.wait_ge(copies[h], b * ACT_COPIES.count(ACT_COPIES[h]) + copied_before[h] + 1)
                    c, r, odd = head_rows(h)
                    out = c_ps[r:r + GROUP_ROWS, c, :]
                    for kb in range(ST):
                        v_ = vl[p][:, kb, h, :] if latent else (ve, vo)[odd][p][:, kb, h // 2, :, :].rearrange("p a d -> p (a d)")
                        q0 = S - P if latent and kb else 0
                        last = pe.matmul(out[:, q0:S], v_, prT[h % 2][:, kb * S:kb * S + S - q0],
                                         start=(kb == 0 and (latent or not odd)),
                                         stop=(kb == ST - 1 and (latent or odd == 1)))
                    if h == H - 1:
                        last.then_inc(z["o_ps"], 1)

                def prepare(b, p, step):
                    if step == 4:
                        pe.wait_ge(z["xn_ready"], b + 1)
                        turn(pe, D0, xn, sh.ident[:]).then_inc(z["turned"], 1)
                        if sparse:
                            for c in range(DC):
                                for t in range(ST):
                                    last = pe.matmul(D1[:, c, 0:P], xn[:, t, c * P:(c + 1) * P], pick[:, t, :],
                                                     start=(t == 0), stop=(t == ST - 1))
                            last.then_inc(z["xs_ps"], 1)
                    if step == 5:
                        pe.wait_ge(z["xT_ready"], b + 1)
                        for c in range(DC):
                            last = project(pe, (D1 if latent else C1)[:, c, :], Wq, xT, c * P)
                        last.then_inc(z["q_ps"], 1)
                    if step == (5 if latent else 6):
                        for c in range(DC):
                            last = project(pe, D0[:, c, :], Wk, xT, c * P)
                        last.then_inc(z["k_ps"], 1)
                    if latent:
                        whole = chunks4(Dk)
                        if step == 6:
                            pe.wait_ge(z["q_ready"], b + 1)
                            for c in range(DC):
                                last = project(pe, D1[:, c, :], Wv, xT, c * P)
                            last.then_inc(z["v_ps"], 1)
                        for at, src, stat, ready, done in (
                                (7, qf, bd_q, ("k_ready", "vf_ready"), "ql_ps"), (8, kf, bd_k, ("ql_ready",), "kl_ps"),
                                (10, ql, rot, ("vl_ready",), "rq_ps"), (11, kl, rot, ("qsin_ready",), "rk_ps"),
                                (12, qr, bd_qk, ("qr_ready", "ksin_ready"), "qk_ps")):
                            if step == at:
                                for n in ready:
                                    pe.wait_ge(z[n], b + 1)
                                for j in range(4):
                                    blocks = stat in (bd_q, bd_k)
                                    last = pe.matmul(whole[:, j, :], stat[:, j % 2, :] if blocks else stat[:],
                                                     src[:, j // 2 if blocks else j, :], start=True, stop=True)
                                last.then_inc(z[done], 1)
                        if step == 9:
                            pe.wait_ge(z["kl_ready"], b + 1)
                            for t in range(ST):
                                for c in range(DC):
                                    last = pe.matmul(Dk[:, t, c * D:(c + 1) * D], vf[:, c, t * P:(t + 1) * P], bd_kv[:],
                                                     start=True, stop=True)
                            last.then_inc(z["vl_ps"], 1)
                        return
                    if step == 7:
                        if sparse:
                            pe.wait_ge(z["xs_ready"], b + 1)
                        for t in range(ST):
                            last = project_rows(pe, D1[:, t, :], xT, Wv, t)
                        last.then_inc(z["v_ps"], 1)
                    if sparse and step == 8:
                        pe.wait_ge(z["q_ready"], b + 1)
                        pe.wait_ge(z["qo_ready"], b + 1)
                        for c in range(DC):
                            project(pe, C1[:, c, 0:P], Wk, xsT, c * P)
                        for c in range(DC):
                            last = project(pe, C1[:, c, P:2 * P], Wv, xsT, c * P)
                        last.then_inc(z["ks_ps"], 1)
                    if sparse and step in (11, 12):
                        t = step - 11
                        pe.wait_ge(z["kd_ready"], b + 1)
                        pe.wait_ge(z["v_ready"], b + 1)
                        if t:
                            pe.wait_ge(z["ss_read"], b * ST + 1)
                        else:
                            pe.wait_ge(z["k_ready"], b + 1)
                        for c in range(DC):
                            out = (Dk[:, 0, :], C[:, 1, :])[c] if t == 0 else (Dk[:, 1, :], Dk[:, 0, :])[c]
                            last = pe.matmul(out[:, 0:8 * (SAMPLES + 1)], qs[:, c, t * P:(t + 1) * P], kd[:, c, :],
                                             start=True, stop=True)
                        last.then_inc(z["ss_ps"], 1)
                    if sparse and step == 14:
                        pe.wait_ge(z["stand_ready"], b + 1)
                        for t in range(ST):
                            last = pe.transpose(D1[0:H, 0, t * P:(t + 1) * P], smax[:, t, :], sh.ident[:])
                        last.then_inc(z["m_ps"], 1)

                def tail(b, p, step):
                    if step == LATE:
                        pe.wait_ge(z["rwide_ready"], b + 1)
                        for t in range(ST):
                            for c in range(CC):
                                last = pe.transpose(chunks4(Dk)[:, c, t * P:(t + 1) * P],
                                                    rwide[:, t, :, :].rearrange("p h v -> p (h v)")[:, c * P:(c + 1) * P],
                                                    sh.ident[:])
                        last.then_inc(z["r_ps"], 1)
                    if sparse and step == LATE:
                        pe.wait_ge(z["rows_ready"], b + 1)
                        for c in range(DC):
                            last = pe.matmul(D1[:, c, :], headsel[:, c * P:(c + 1) * P], mrow[p][:], start=True, stop=True)
                        last.then_inc(z["kept_ps"], 1)
                    if latent and step == LATE + 2:
                        pe.wait_ge(z["ctx_ready"], b + 1)
                        for c in range(DC):
                            for j in range(2):
                                last = pe.matmul(D0[:, c, :], bd_o[:, j, :], cT[:, 2 * c + j, :], start=(j == 0),
                                                 stop=(j == 1))
                        last.then_inc(z["y_ps"], 1)
                    if step == LATE + 3:
                        pe.wait_ge(z["y_ready" if latent else "ctx_ready"], b + 1)
                        for t in range(ST):
                            last = project_rows(pe, (D1 if latent else C1)[:, t, :], yT if latent else cT, Wo, t)
                        last.then_inc(z["out_ps"], 1)

                def sequence(b, p, before, after):
                    for h in range(H):
                        turn_probs(b, h)
                        if h + 2 < H:
                            scores(b, p, h + 2)
                        elif after and h + 2 == H:
                            first_scores(b + 1, 1 - p)
                        elif after:
                            scores(b + 1, 1 - p, 1)
                        if h >= 1:
                            if h == 1 and before:
                                pe.wait_ge(z["ctx_read"], b)
                            values(b, p, h - 1)
                        elif before:
                            values(b - 1, 1 - p, H - 1)
                        if before:
                            tail(b - 1, 1 - p, h)
                        if after:
                            if h == 5 and before:
                                pe.wait_ge(z["out_read"], b)
                            prepare(b + 1, 1 - p, h)
                        if ternary and not before and h == 12:
                            ternary.add_partitions(pe, sh.ones[:], C1[:, 0, 0:3])

                def first():
                    if sparse:
                        pe.wait_ge(z["pick_ready"], 1)
                    for step in range(H):
                        prepare(0, 0, step)
                    first_scores(0, 0)
                    scores(0, 0, 1)

                def last():
                    values(B - 1, 1, H - 1)
                    for step in range(H):
                        tail(B - 1, 1, step)

                walk(pe, first, sequence, last)

            @block.scalar
            def _(a):
                def exps(b, p, h):
                    a.wait_ge(z["neg_ready"], b * H + h + 1)
                    for t in range(ST):
                        cols = slice(SCOL[t], SCOL[t] + KEYS[t])
                        src = sm[h % 2][:, cols] if latent or decayed else A[:, h % 2, cols]
                        a.activation(pr[h % 2][:, cols], src, ACT.Exp, bias=negmax[:, h, t:t + 1],
                                     accum_out=rsum[p][:, t, h:h + 1])
                    a.drain().then_inc(z["exp_ready"], 1)

                def copy_turned(b, h):
                    a.wait_ge(z["pT_ps"], b * H + h + 1)
                    a.copy(prT[h % 2][:], Bk[:, h % 2, 0:SW]).then_inc(z["pT_ready_a"], 1)

                def prepare(b, p, step):
                    if step == 4:
                        a.wait_ge(z["turned"], b + 1)
                        a.copy(xT[:], D0).then_inc(z["xT_ready"], 1)
                        if sparse:
                            a.wait_ge(z["xs_ps"], b + 1)
                            a.copy(xsT[:], D1[:, :, 0:P]).then_inc(z["xs_ready"], 1)
                    if latent:
                        for at, dst, src, bias, came, done in (
                                (5, qf, D1, bq, "q_ps", "q_ready"), (5, kf, D0, bk, "k_ps", "k_ready"),
                                (6, vf, D1, bvf, "v_ps", "vf_ready")):
                            if step == at:
                                a.wait_ge(z[came], b + 1)
                                for c in range(DC):
                                    last = a.activation(dst[:, c, :], src[:, c, :], ACT.Identity, bias=bias[:, c:c + 1])
                                last.then_inc(z[done], 1)
                        for at, dst, bias, came, done in (
                                (7, ql, bl_q, "ql_ps", "ql_ready"), (8, kl, bl_k, "kl_ps", "kl_ready"),
                                (12, qq[p], bl_qk, "qk_ps", "qq_ready")):
                            if step == at:
                                a.wait_ge(z[came], b + 1)
                                a.activation(dst[:], chunks4(Dk), ACT.Identity, bias=bias[:, 0:1]).then_inc(z[done], 1)
                        return
                    if step == 5:
                        a.wait_ge(z["q_ps"], b + 1)
                        for i, q in enumerate((qe[p],) if sparse else (qe[p], qo[p])):
                            for c in range(DC):
                                last = a.activation(q[:, c, :], C1[:, c, :], ACT.Identity, bias=bqp[:, i, c:c + 1],
                                                    scale=parity[:, i:i + 1])
                        if sparse:
                            for c in range(DC):
                                last = a.activation(qs[:, c, :], C1[:, c, :], ACT.Identity, bias=bqs[:, c:c + 1],
                                                    scale=float(HD) ** -0.5)
                        last.then_inc(z["q_ready"], 1)
                    if step == 6:
                        a.wait_ge(z["k_ps"], b + 1)
                        for c in range(DC):
                            last = a.activation(kT[p][:, c, :], D0[:, c, :], ACT.Identity, bias=bk[:, c:c + 1])
                        last.then_inc(z["k_ready"], 1)
                    if sparse and step == 8:
                        a.wait_ge(z["ks_ps"], b + 1)
                        for c in range(DC):
                            a.activation(ksT[:, c, :], C1[:, c, 0:SAMPLES], ACT.Identity, bias=bk[:, c:c + 1])
                            a.activation(meanT[p][:, 0, c:c + 1], C1[:, c, P + SAMPLES:P + SAMPLES + 1], ACT.Identity, bias=bvc[:, c:c + 1],
                                         scale=1.0 / S)
                        a.drain().then_inc(z["ks_ready"], 1)

                def tail(b, p, step):
                    if step == 0:
                        a.wait_ge(z["o_ps"], b + 1)
                        a.copy(ctx_raw[:], c_ps).then_inc(z["ctx_read"], 1)
                    if latent and step == LATE + 2:
                        a.wait_ge(z["y_ps"], b + 1)
                        a.activation(yT[:], D0, ACT.Identity, bias=bl_o[:, 0:1]).then_inc(z["y_ready"], 1)

                def sequence(b, p, before, after):
                    for h in range(H):
                        if h + 1 < H:
                            exps(b, p, h + 1)
                        elif after:
                            exps(b + 1, 1 - p, 0)
                        if ACT_COPIES[h]:
                            copy_turned(b, h)
                        if before:
                            tail(b - 1, 1 - p, h)
                        if after:
                            prepare(b + 1, 1 - p, h)

                def first():
                    if not latent:
                        a.wait_ge(z["bqp_ready"], 1)
                    for step in range(H):
                        prepare(0, 0, step)
                    exps(0, 0, 0)

                def last():
                    for step in range(H):
                        tail(B - 1, 1, step)

                walk(a, first, sequence, last)

            @block.vector
            def _(v):
                def row_max(b, h):
                    v.wait_ge(z["s_ps"], b * H + h + 1)
                    src = A[:, h % 2, 0:SW]
                    if latent:
                        v.scalar_tensor_tensor(sm[h % 2][:], src, float(LAT) ** -0.5, mask[:], ALU.mult, ALU.add)
                    if decayed:
                        v.tensor_tensor(sm[h % 2][:], src, masks[:, h, :, :].rearrange("p t k -> p (t k)"), ALU.mult)
                    if latent or decayed:
                        v.drain()
                        src = sm[h % 2][:]
                    if latent:
                        for t in range(ST):
                            v.tensor_reduce(negmax[:, h, t:t + 1], src[:, SCOL[t]:SCOL[t] + KEYS[t]], AXX, ALU.max, negate=True)
                        v.drain().then_inc(z["neg_ready"], 1)
                    else:
                        v.tensor_reduce(negmax[:, h, :], src.rearrange("p (t k) -> p t k", t=ST), AXX, ALU.max,
                                        negate=True).then_inc(z["neg_ready"], 1)

                def copy_turned(b, h):
                    v.wait_ge(z["pT_ps"], b * H + h + 1)
                    v.tensor_copy(prT[h % 2][:], Bk[:, h % 2, 0:SW]).then_inc(z["pT_ready_v"], 1)

                def sum_samples(b, t):
                    v.wait_ge(z["ss_ps"], b * ST + t + 1)
                    for c in range(DC):
                        bank = (Dk[:, 0, :], C[:, 1, :])[c] if t == 0 else (Dk[:, 1, :], Dk[:, 0, :])[c]
                        src = bank[:, 0:8 * SAMPLES].rearrange("p (h u) -> p h u", u=SAMPLES)
                        most = smax[:, t, 8 * c:8 * c + 8]
                        v.tensor_reduce(most, src, AXX, ALU.max)
                        v.drain()
                        v.scalar_tensor_tensor(most, bank[:, 8 * SAMPLES:8 * (SAMPLES + 1)], -1.0 / SAMPLES, most,
                                               ALU.mult, ALU.add)
                    v.drain().then_inc(z["ss_read"], 1)

                def combine(b, p, k):
                    rows = lambda t: sh.h[:, ds(b * ST + t, 1), :]
                    if k == 0 and shared:
                        v.wait_ge(z[f"shared{p}"], b * 8 + (16 - 8 * p))
                        v.tensor_tensor(sh.h[:, ds(b * ST, ST), :], sh.h[:, ds(b * ST, ST), :], from_shared[p][:], ALU.add)
                        v.drain()
                    if k == 0:
                        each = 16 * K * ST
                        v.wait_ge(z[f"gathered{p}"], b * (each // 2) + (each - each // 2 * p))
                    for t in range(ST):
                        v.scalar_tensor_tensor(rows(t), gathered[p][:, k * ST + t:k * ST + t + 1, :],
                                               sh.weight[:, ds(b * ST + k * NT + t, 1)], rows(t), ALU.mult, ALU.add)
                    if k == K - 1:
                        v.drain().then_inc(z["added"], 1)
                    else:
                        v.drain()

                def prepare(b, p, step):
                    if step < K:
                        combine(b, p, step)
                    if step == 2:
                        for t in range(ST):
                            v.bn_stats(stats[:, t, :], sh.h[:, ds(b * ST + t, 1), :])
                        v.drain()
                        for t in range(ST):
                            v.bn_aggr(mv[:, t, :], stats[:, t, :])
                        v.drain()
                        v.tensor_scalar(mv[:, :, 1:2], mv[:, :, 1:2], LN_EPS, None, ALU.add).then_inc(z["var"], 1)
                    if step == 3:
                        v.wait_ge(z["rst"], b + 1)
                        for t in range(ST):
                            v.tensor_scalar(xn[:, t, :], sh.h[:, ds(b * ST + t, 1), :], mv[:, t, 0:1], rstd[:, t, 0:1],
                                            ALU.subtract, ALU.mult)
                        v.drain().then_inc(z["xn_ready"], 1)
                    if step == 7:
                        v.tensor_tensor(sh.h[:, ds(b * ST, ST), :], sh.h[:, ds(b * ST, ST), :], bc(bo[:], [P, ST, D]), ALU.add)
                        v.drain()
                    if latent:
                        if step == 10:
                            v.wait_ge(z["vl_ps"], b + 1)
                            v.tensor_tensor(vl[p][:].rearrange("p t h l -> p (t h) l"),
                                            Dk[:].rearrange("p a (h l) -> p (a h) l", l=LAT),
                                            bc(bl_v[:], [P, ST * H, LAT]), ALU.add).then_inc(z["vl_ready"], 1)
                        if step == 11:
                            v.wait_ge(z["rq_ps"], b + 1)
                            v.tensor_tensor(t2[:], chunks4(Dk), bc(sin[:], [P, 4, S]), ALU.mult).then_inc(z["qsin_ready"], 1)
                        if step == 12:
                            v.wait_ge(z["rk_ps"], b + 1)
                            v.tensor_tensor(kr[p][:], chunks4(Dk), bc(sin[:], [P, 4, S]), ALU.mult).then_inc(z["ksin_ready"], 1)
                            v.drain()
                        if step == 13:
                            v.wait_ge(z["kcos_ready"], b + 1)
                            v.tensor_tensor(kr[p][:], kr[p][:], t1[:], ALU.add).then_inc(z["kr_ready"], 1)
                        return
                    if sparse and step == 6:
                        v.wait_ge(z["q_ready"], b + 1)
                        for c in range(DC):
                            last = v.tensor_scalar(qo[p][:, c, :], C1[:, c, :], parity[:, 1:2], bqp[:, 1, c:c + 1],
                                                   ALU.mult, ALU.add)
                        last.then_inc(z["qo_ready"], 1)
                    if step == 8:
                        v.wait_ge(z["v_ps"], b + 1)
                        for i, dst in enumerate((ve[p], vo[p])):
                            for t in range(ST):
                                v.tensor_tensor(dst[:, t, :, i, :], D1[:, t, :].rearrange("p (n a d) -> p n a d", a=2, d=HD)[:, :, i, :],
                                                bv[:].rearrange("p (n a d) -> p n a d", a=2, d=HD)[:, :, i, :], ALU.add)
                        v.drain().then_inc(z["v_ready"], 1)
                    if sparse:
                        if step == 10:
                            v.wait_ge(z["ks_ready"], b + 1)
                            v.tensor_reduce(ksum[:], ksT[:], AXX, ALU.add)
                            for c in range(DC):
                                v.tensor_tensor(kd_keys[:, c, :, :], bc(ksT[:, c, :], [P, 8, SAMPLES]),
                                                own[:].unsqueeze(2).broadcast_to([P, 8, SAMPLES]), ALU.mult)
                            v.drain()
                            for c in range(DC):
                                v.tensor_scalar(kd_sums[:, c, :], own[:], ksum[:, c:c + 1], None, ALU.mult)
                            v.tensor_scalar(meanT[p][:, 1, :], meanT[p][:, 0, :], -1.0, None, ALU.mult)
                            v.drain().then_inc(z["kd_ready"], 1)
                        if step == 12:
                            sum_samples(b, 0)
                        if step == 13:
                            sum_samples(b, 1)
                            v.drain().then_inc(z["stand_ready"], 1)
                        if step == 15:
                            v.wait_ge(z["m_ps"], b + 1)
                            v.tensor_copy(mwork[:], D1[0:H, 0, :])
                            v.drain()

                def pick_queries(p, h):
                    if h in PICK_HEADS:
                        v.max(best8[:], mwork[:])
                        v.drain()
                        v.match_replace(mwork[:], best8[:], mwork[:], NEG)
                        v.drain()
                    if h == PICK_HEADS[-1]:
                        v.tensor_scalar(mrow[p][:], mwork[:], NEG, None, ALU.is_equal)
                        v.drain().then_inc(z["rows_ready"], 1)

                def reciprocals(b, p):
                    v.wait_ge(z["exp_ready"], b * H + H)
                    v.reciprocal(rden[:], rsum[p][:]).then_inc(z["rden_ready"], 1)

                def tail(b, p, step):
                    if step == LATE + 1:
                        v.wait_ge(z["r_ps"], b + 1)
                        v.wait_ge(z["ctx_read"], b + 1)
                        v.tensor_tensor(cT[:], ctx_raw[:], chunks4(Dk)[:, 0:CC, :], ALU.mult)
                        if not sparse:
                            v.drain().then_inc(z["ctx_ready"], 1)
                    if sparse and step == LATE + 2:
                        v.wait_ge(z["kept_ps"], b + 1)
                        for c in range(DC):
                            v.tensor_scalar(mpart[:, c, :], D1[:, c, :], meanT[p][:, 1, c:c + 1], meanT[p][:, 0, c:c + 1],
                                            ALU.mult, ALU.add)
                        v.drain()
                        v.tensor_tensor(cT[:], cT[:], D1, ALU.mult)
                        v.drain()
                        v.tensor_tensor(cT[:], cT[:], mpart[:], ALU.add)
                        v.drain().then_inc(z["ctx_ready"], 1)
                    if step == LATE + 4:
                        v.wait_ge(z["out_ps"], b + 1)
                        v.tensor_tensor(sh.h[:, ds(b * ST, ST), :], sh.h[:, ds(b * ST, ST), :], D1 if latent else C1, ALU.add)
                        v.drain().then_inc(z["out_read"], 1)

                def sequence(b, p, before, after):
                    for h in range(H):
                        if h + 1 < H:
                            row_max(b, h + 1)
                        elif after:
                            row_max(b + 1, 0)
                        if h == H - 1 and not sparse:
                            reciprocals(b, p)
                        if not ACT_COPIES[h]:
                            copy_turned(b, h)
                        if sparse:
                            pick_queries(p, h)
                        if before:
                            tail(b - 1, 1 - p, h)
                        if after:
                            prepare(b + 1, 1 - p, h)
                        if h == H - 1 and sparse:
                            reciprocals(b, p)
                        if ternary and not before:
                            if h in (7, 9, 11):
                                ternary.add_up(v, (h - 7) // 2)
                            if h == 13:
                                ternary.means(v, C1[:, 0, 0:3])
                        if ternary and not after and 4 <= h < 13:
                            ternary.quantise(v, h - 4)

                def first():
                    if latent:
                        v.wait_ge(z["consts"], 1)
                    else:
                        for i in range(2):
                            v.tensor_scalar(bqp[:, i, :], bq[:], parity[:, i:i + 1], None, ALU.mult)
                        for t in (*ve, *vo):
                            v.memset(t[:], 0.0)
                        if sparse:
                            v.tensor_scalar(bqs[:], bq[:], float(HD) ** -0.5, None, ALU.mult)
                        v.drain().then_inc(z["bqp_ready"], 1)
                    if sparse:
                        v.wait_ge(z["iotas"], 1)
                        v.tensor_copy(idx_f[:], idx_i[:])
                        v.drain()
                        v.tensor_scalar(neg_i[:], idx_f[:], 0.0, float(S), ALU.is_lt, ALU.mult)
                        v.drain()
                        v.tensor_tensor(idx_f[:], idx_f[:], neg_i[:], ALU.add)
                        v.drain()
                        v.tensor_scalar(idx_f[:], idx_f[:], 0.0, float(S - 1), ALU.max, ALU.min)
                        v.drain()
                        v.memset(pick[:], 0.0)
                        v.drain()
                        v.memset(pick[:, :, SAMPLES:SAMPLES + 1], 1.0)
                        for t in range(ST):
                            v.tensor_scalar(pick[:, t, 0:SAMPLES], idx_f[:], tok[:, t:t + 1], None, ALU.is_equal)
                        v.drain().then_inc(z["pick_ready"], 1)
                    for step in range(H):
                        prepare(0, 0, step)
                    row_max(0, 0)

                def last():
                    for step in range(H):
                        tail(B - 1, 1, step)

                walk(v, first, sequence, last)


def capacity_experts(nc, sh, buf, obuf, c_fc, c_proj, masks, decay_params, mix_weights):
    F = c_fc.shape[2] // DC
    FC = F // P
    CB = CAP // P
    HALF = CAP // 2
    GB = 3
    GROUPS = 2 * FC
    with ExitStack() as ctx, Signals(nc) as signals:
        sb = lambda n, shape, dt=F32: ctx.enter_context(nc.sbuf_tensor("x2_" + n, shape, dt))
        ps = lambda n, shape, dt=F32: ctx.enter_context(nc.psum_tensor("x2_" + n, shape, dt))
        sem = lambda n: signals("x2_" + n)
        wf = [sb(f"wf{p}", [P, DC, F]) for p in range(2)]
        wp = [sb(f"wp{p}", [P, FC, D]) for p in range(2)]
        xin = [sb(f"xin{p}", [P, CB, D]) for p in range(2)]
        xT = [sb(f"xT{p}", [P, DC, CAP]) for p in range(2)]
        hT = sb("hT", [P, FC, CAP])
        r = [sb(f"r{i}", [P, HALF]) for i in range(GB)]
        y = [sb(f"y{p}", [P, CB, D]) for p in range(2)]
        p_t = [ps(f"p_t{c}", [P, 4, P]) for c in range(DC + 1)]
        p_g = [ps(f"p_g{i}", [P, 512]) for i in range(GB)]
        p_o = [ps(f"p_o{i}", [P, D]) for i in range(2)]
        x_in, wf_in, wp_in, stored = ([sem(f"{n}{p}") for p in range(2)] for n in ("x_in", "wf_in", "wp_in", "stored"))
        turned, xT_ready, g_ready, relu_ready, h_ready, o_ready, y_ready = (
            sem(n) for n in ("turned", "xT_ready", "g_ready", "relu_ready", "h_ready", "o_ready", "y_ready"))
        sent = sem("sent")
        decays = DecayMasks(nc, ctx, signals, masks, decay_params, mix_weights)
        rows = lambda m, e: m[ds(e * CAP, CAP), :].rearrange("(p t) d -> p t d", t=CB)
        with nc.Block() as block:
            @block.sync
            def _(sp):
                def load_x(e, p):
                    sp.dma_start(xin[p][:], rows(buf, e)).then_inc(x_in[p], 16)

                def load(e, p):
                    sp.dma_start(wf[p][:].rearrange("p c n -> p (c n)"), c_fc[ds(e, 1), :, :].rearrange("a p n -> (a p) n")
                                 ).then_inc(wf_in[p], 16)
                    sp.dma_start(wp[p][:].rearrange("p c n -> p (c n)"), c_proj[ds(e, 1), :, :].rearrange("a p n -> (a p) n")
                                 ).then_inc(wp_in[p], 16)

                decays.sync(sp)
                for p in range(2):
                    load(p, p)
                sp.wait_ge(sent, 16 * KT)
                for p in range(2):
                    load_x(p, p)
                with sp.Fori(1, E // 2) as k:
                    for p in range(2):
                        sp.wait_ge(turned, k * 2 + (p - 1))
                        load_x(k * 2 + p, p)
                        sp.wait_ge(o_ready, k * (2 * CB) + (p - 1) * CB)
                        load(k * 2 + p, p)

            @block.gpsimd
            def _(g):
                decays.gpsimd(g)
                dispatch(g, sh, buf, sent)

            @block.tensor
            def _(pe):
                def turn_rows(k, p):
                    pe.wait_ge(x_in[p], k * 16 + 16)
                    for c in range(DC):
                        for t in range(CB):
                            out = p_t[c][:, t, :] if t < 4 else p_t[DC][:, c, :]
                            last = pe.transpose(out, xin[p][:, t, c * P:(c + 1) * P], sh.ident[:])
                    last.then_inc(turned, 1)

                def expert(e, k, p, ahead):
                    pe.wait_ge(xT_ready, e + 1)
                    pe.wait_ge(wf_in[p], k * 16 + 16)
                    for n in range(GROUPS):
                        f, half = n // 2, n % 2
                        if n >= GB:
                            pe.wait_ge(relu_ready, e * GROUPS + n - GB + 1)
                        for c in range(DC):
                            last = pe.matmul(p_g[n % GB][:, 0:HALF], wf[p][:, c, f * P:(f + 1) * P],
                                             xT[p][:, c, half * HALF:(half + 1) * HALF], start=(c == 0), stop=(c == DC - 1))
                        last.then_inc(g_ready, 1)
                    if ahead:
                        turn_rows(k + p, 1 - p)
                    pe.wait_ge(h_ready, e * GROUPS + GROUPS)
                    pe.wait_ge(wp_in[p], k * 16 + 16)
                    for t in range(CB):
                        if t >= 2:
                            pe.wait_ge(y_ready, e * CB + t - 1)
                        for f in range(FC):
                            last = pe.matmul(p_o[t % 2][:], hT[:, f, t * P:(t + 1) * P], wp[p][:, f, :],
                                             start=(f == 0), stop=(f == FC - 1))
                        last.then_inc(o_ready, 1)

                turn_rows(0, 0)
                with pe.Fori(0, E // 2 - 1) as k:
                    for p in range(2):
                        expert(k * 2 + p, k, p, True)
                for p in range(2):
                    expert(E - 2 + p, E // 2 - 1, p, p == 0)

            @block.scalar
            def _(a):
                def copy_turned(e, p):
                    a.wait_ge(turned, e + 1)
                    for c in range(DC):
                        a.copy(xT[p][:, c, 0:4 * P], p_t[c][:].rearrange("p t n -> p (t n)"))
                    a.copy(xT[p][:, :, 4 * P:CAP], p_t[DC][:, 0:DC, :]).then_inc(xT_ready, 1)

                def store(e, p):
                    a.wait_ge(y_ready, e * CB + CB)
                    a.dma_start(rows(obuf, e), y[p][:]).then_inc(stored[p], 16)

                def expert(e, p, first, ahead):
                    for n in range(GROUPS):
                        a.wait_ge(g_ready, e * GROUPS + n + 1)
                        if n >= GB:
                            a.wait_ge(h_ready, e * GROUPS + n - GB + 1)
                        a.activation(r[n % GB][:], p_g[n % GB][:, 0:HALF], ACT.Relu).then_inc(relu_ready, 1)
                    if ahead:
                        copy_turned(e + 1, 1 - p)
                    if not first:
                        store(e - 1, 1 - p)

                decays.scalar(a)
                copy_turned(0, 0)
                expert(0, 0, True, True)
                expert(1, 1, False, True)
                with a.Fori(1, E // 2 - 1) as k:
                    for p in range(2):
                        expert(k * 2 + p, p, False, True)
                for p in range(2):
                    expert(E - 2 + p, p, False, p == 0)
                store(E - 1, 1)
                for p in range(2):
                    a.wait_ge(stored[p], 16 * (E // 2))

            @block.vector
            def _(v):
                def expert(e, k, p, reused):
                    for n in range(GROUPS):
                        f, half = n // 2, n % 2
                        v.wait_ge(relu_ready, e * GROUPS + n + 1)
                        v.tensor_tensor(hT[:, f, half * HALF:(half + 1) * HALF], r[n % GB][:], r[n % GB][:], ALU.mult
                                        ).then_inc(h_ready, 1)
                    if reused:
                        v.wait_ge(stored[p], k * 16)
                    for t in range(CB):
                        v.wait_ge(o_ready, e * CB + t + 1)
                        v.tensor_copy(y[p][:, t, :], p_o[t % 2][:]).then_inc(y_ready, 1)

                decays.vector(v)
                for p in range(2):
                    expert(p, 0, p, False)
                with v.Fori(1, E // 2) as k:
                    for p in range(2):
                        expert(k * 2 + p, k, p, True)


def quantised_ffn(nc, sh, ternary):
    F = ternary.src["gate"].shape[1]
    wq, wmean = ternary.wq, ternary.wmean
    FC = F // P
    QA = 127.0
    HALF = 512
    HALVES = F // HALF
    TURNS = 4
    with ExitStack() as ctx, Signals(nc) as signals:
        sb = lambda n, shape, dt=F32: ctx.enter_context(nc.sbuf_tensor("q_" + n, shape, dt))
        ps = lambda n, shape, dt=F32: ctx.enter_context(nc.psum_tensor("q_" + n, shape, dt))
        sem = lambda n: signals("q_" + n)
        stats, mv, rstd = sb("stats", [P, NT, 6]), sb("mv", [P, NT, 2]), sb("rstd", [P, NT, 1])
        minus_half = sb("minus_half", [P, NT, 1])
        xn = sb("xn", [P, NT, D])
        amax, rscale, gscale, uscale = (sb(n, [P, NT]) for n in ("amax", "rscale", "gscale", "uscale"))
        xq = sb("xq", [P, NT, D], BF16)
        xqT = sb("xqT", [P, NT, DC, P], BF16)
        sg = [sb(f"sg{p}", [P, F]) for p in range(2)]
        gs = [sb(f"gs{p}", [P, 1]) for p in range(2)]
        pmax, pscale, dscale = ([sb(f"{n}{p}", [P, 1]) for p in range(2)] for n in ("pmax", "pscale", "dscale"))
        pq = [sb(f"pq{p}", [P, F], BF16) for p in range(2)]
        pqT = [sb(f"pqT{p}", [P, FC, P], BF16) for p in range(2)]
        p_g, p_u = ([ps(f"{n}{i}", [P, HALF]) for i in range(HALVES)] for n in ("p_g", "p_u"))
        p_T = [ps(f"p_T{p}", [P, FC, P], BF16) for p in range(2)]
        p_d = [ps(f"p_d{p}", [P, 512]) for p in range(2)]
        var, rst, halves_set = sem("var"), sem("rst"), sem("halves_set")
        xq_ready, turned, xT_ready, g_ready, u_ready, sg_ready, bank_free, pq_ready, pT_ps, pT_ready, d_ready = (
            sem(n) for n in ("xq_ready", "turned", "xT_ready", "g_ready", "u_ready", "sg_ready",
                             "bank_free", "pq_ready", "pT_ps", "pT_ready", "d_ready"))
        scales_ready = sem("scales_ready")

        def blocks(engine, first, step):
            first()
            with engine.Fori(0, NT // 2 - 1) as k:
                for p in range(2):
                    step(k * 2 + p, p, True)
            for p in range(2):
                step(NT - 2 + p, p, p == 0)

        with nc.Block() as block:
            @block.gpsimd
            def _(g):
                g.memset(minus_half[:], -0.5).then_inc(halves_set, 1)
                g.wait_ge(halves_set, 1)
                g.wait_ge(var, 1)
                g.tensor_tensor(rstd[:], mv[:, :, 1:2], minus_half[:], ALU.pow).then_inc(rst, 1)

            @block.tensor
            def _(pe):
                pe.wait_ge(xq_ready, 1)
                for r in range(NT // TURNS):
                    if r >= 2:
                        pe.wait_ge(xT_ready, r - 1)
                    for i in range(TURNS):
                        for c in range(DC):
                            last = pe.transpose(p_T[r % 2][:, i * DC + c, :], xq[:, r * TURNS + i, c * P:(c + 1) * P],
                                                sh.identb[:])
                    last.then_inc(turned, 1)
                pe.wait_ge(xT_ready, NT // TURNS)

                def gate_and_up(n):
                    for i in range(HALVES):
                        pe.wait_ge(bank_free, n * HALVES + i + 1)
                        for dst, name, done in ((p_g, "gate", g_ready), (p_u, "up", u_ready)):
                            for c in range(DC):
                                last = pe.matmul(dst[i][:], xqT[:, ds(n, 1), c, :].rearrange("p a t -> p (a t)"),
                                                 wq[name][:, c, i * HALF:(i + 1) * HALF], start=(c == 0), stop=(c == DC - 1))
                            last.then_inc(done, 1)

                def step(n, p, ahead):
                    if ahead:
                        gate_and_up(n + 1)
                    pe.wait_ge(pq_ready, n + 1)
                    for f in range(FC):
                        last = pe.transpose(p_T[p][:, f, :], pq[p][:, f * P:(f + 1) * P], sh.identb[:])
                    last.then_inc(pT_ps, 1)
                    pe.wait_ge(pT_ready, n + 1)
                    for f in range(FC):
                        last = pe.matmul(p_d[p][:, 0:D], pqT[p][:, f, :], wq["down"][:, f, :], start=(f == 0),
                                         stop=(f == FC - 1))
                    last.then_inc(d_ready, 1)

                blocks(pe, lambda: gate_and_up(0), step)

            @block.scalar
            def _(a):
                a.preload_act_table(ACT.Silu)
                for r in range(NT // TURNS):
                    a.wait_ge(turned, r + 1)
                    a.copy(xqT[:, r * TURNS:(r + 1) * TURNS, :, :], p_T[r % 2][:].rearrange("p (i c) t -> p i c t", c=DC)
                           ).then_inc(xT_ready, 1)
                a.wait_ge(scales_ready, 1)

                def gated(n, p):
                    a.copy(gs[p][:], gscale[:, ds(n, 1)])
                    a.drain()
                    for i in range(HALVES):
                        a.wait_ge(g_ready, n * HALVES + i + 1)
                        a.activation(sg[p][:, i * HALF:(i + 1) * HALF], p_g[i][:], ACT.Silu, scale=gs[p][:, 0:1]
                                     ).then_inc(sg_ready, 1)

                def step(n, p, ahead):
                    if ahead:
                        gated(n + 1, 1 - p)
                    a.wait_ge(pT_ps, n + 1)
                    a.copy(pqT[p][:], p_T[p][:]).then_inc(pT_ready, 1)

                blocks(a, lambda: gated(0, 0), step)

            @block.vector
            def _(v):
                v.drain().then_inc(bank_free, HALVES)
                for t in range(NT):
                    v.bn_stats(stats[:, t, :], sh.h[:, t, :])
                v.drain()
                for t in range(NT):
                    v.bn_aggr(mv[:, t, :], stats[:, t, :])
                v.drain()
                v.tensor_scalar(mv[:, :, 1:2], mv[:, :, 1:2], LN_EPS, None, ALU.add).then_inc(var, 1)
                v.wait_ge(rst, 1)
                for t in range(NT):
                    v.tensor_scalar(xn[:, t, :], sh.h[:, t, :], mv[:, t, 0:1], rstd[:, t, 0:1], ALU.subtract, ALU.mult)
                v.drain()
                v.tensor_reduce(amax[:], xn[:], AXX, ALU.max, apply_absolute_value=True)
                v.drain()
                v.tensor_scalar(amax[:], amax[:], 1e-5, 1.0 / QA, ALU.max, ALU.mult)
                v.drain()
                v.reciprocal(rscale[:], amax[:])
                v.drain()
                for t in range(NT):
                    v.tensor_scalar(xn[:, t, :], xn[:, t, :], rscale[:, t:t + 1], ROUND, ALU.mult, ALU.add)
                v.drain()
                v.tensor_scalar(xq[:], xn[:], ROUND, QA, ALU.subtract, ALU.min).then_inc(xq_ready, 1)
                v.tensor_scalar(gscale[:], amax[:], wmean[:, 0:1], None, ALU.mult)
                v.tensor_scalar(uscale[:], amax[:], wmean[:, 1:2], None, ALU.mult)
                v.drain().then_inc(scales_ready, 1)

                def levels(n, p):
                    for i in range(HALVES):
                        half = sg[p][:, i * HALF:(i + 1) * HALF]
                        v.wait_ge(sg_ready, n * HALVES + i + 1)
                        v.wait_ge(u_ready, n * HALVES + i + 1)
                        v.scalar_tensor_tensor(half, p_u[i][:], uscale[:, ds(n, 1)], half, ALU.mult, ALU.mult
                                               ).then_inc(bank_free, 1)
                    v.drain()
                    v.tensor_reduce(pmax[p][:], sg[p][:], AXX, ALU.max, apply_absolute_value=True)
                    v.drain()
                    v.tensor_scalar(pmax[p][:], pmax[p][:], 1e-5, 1.0 / QA, ALU.max, ALU.mult)
                    v.drain()
                    v.reciprocal(pscale[p][:], pmax[p][:])
                    v.tensor_scalar(dscale[p][:], pmax[p][:], wmean[:, 2:3], None, ALU.mult)
                    v.drain()
                    v.tensor_scalar(sg[p][:], sg[p][:], pscale[p][:, 0:1], ROUND, ALU.mult, ALU.add)
                    v.drain()
                    v.tensor_scalar(pq[p][:], sg[p][:], ROUND, QA, ALU.subtract, ALU.min).then_inc(pq_ready, 1)

                def step(n, p, ahead):
                    if ahead:
                        levels(n + 1, 1 - p)
                    v.wait_ge(d_ready, n + 1)
                    v.scalar_tensor_tensor(sh.h[:, ds(n, 1), :], p_d[p][:, 0:D].unsqueeze(1), dscale[p][:, 0:1],
                                           sh.h[:, ds(n, 1), :], ALU.mult, ALU.add)

                blocks(v, lambda: levels(0, 0), step)
                v.drain()




def tower(nc, a, out):
    buf = nc.dram_tensor("slots", (SLOTS + K * T, D), F32).ap()
    obuf = nc.dram_tensor("slot_results", (SLOTS, D), F32).ap()
    with ExitStack() as ctx:
        sh = Shared()
        setup_constants(nc, ctx, sh)
        time_and_channel_mix(nc, sh, a["x"], a["L0_tok_weight"], {n: a["L0_attn_" + n] for n in (
            "Wr", "Ww", "Wk", "Wv", "Wo", "Wrec", "Wkey", "Wval", "time_decay", "ln1_g", "ln1_b", "ln2_g", "ln2_b")}, buf)
        routing_state(nc, ctx, sh)
        xn_all = lambda stack, i: stack.enter_context(nc.sbuf_tensor(f"xn_all{i}", [P, NT, D], F32))
        with ExitStack() as outer:
            w = {n: a["L1_attn_" + n] for n in (
                "c_attn_w", "c_attn_b", "q2l_w", "q2l_b", "kv2l_w", "kv2l_b", "l2o_w", "l2o_b", "wqk_w", "wqk_b",
                "cproj_w", "cproj_b", "rot", "cos", "sin")}
            wt = attention_weights(nc, outer, "a1", "latent")
            with ExitStack() as moe:
                sh.xn_all = xn_all(moe, 0)
                route(nc, sh, "r0", a["L0_ffn_gate_w"], "sigmoid", (wt, "latent", w), a["L0_ffn_expert_bias"])
                expert_tiles(nc, sh, "x0", buf, obuf, a["L0_ffn_experts"], SHARED_TILES + ROUTED_TILES, True)
            attention(nc, sh, "a1", "latent", wt, obuf, shared=True)
        with ExitStack() as outer:
            w = {n: a["L2_attn_" + n] for n in ("Wq", "bq", "Wk", "bk", "Wv", "bv", "Wo", "bo", "idx_k")}
            w["parity"] = a["parity"]
            wt = attention_weights(nc, outer, "a2", "sparse")
            with ExitStack() as moe:
                sh.xn_all = xn_all(moe, 1)
                route(nc, sh, "r1", a["L1_ffn_router_w"], "softmax", (wt, "sparse", w))
                expert_tiles(nc, sh, "x1", buf, obuf, a["L1_ffn_experts"], ROUTED_TILES, False, a["L1_ffn_b_out"])
            attention(nc, sh, "a2", "sparse", wt, obuf)
        with ExitStack() as outer:
            w = {n: a["L3_attn_" + n] for n in ("Wq", "bq", "Wk", "bk", "Wv", "bv", "Wo", "bo")}
            w["parity"] = a["parity"]
            wt = attention_weights(nc, outer, "a3", "decay")
            masks = outer.enter_context(nc.sbuf_tensor("masks", [P, H, ST, S], F32))
            with ExitStack() as moe:
                sh.xn_all = xn_all(moe, 2)
                route(nc, sh, "r2", a["L2_ffn_w_g"], "softmax2", (wt, "decay", w))
                capacity_experts(nc, sh, buf, obuf, a["L2_ffn_c_fc"], a["L2_ffn_c_proj"], masks,
                                 a["L3_attn_decay_params"], a["L3_attn_mix_weights"])
            ternary = TernaryWeights(nc, outer, {n: a["L3_ffn_w_" + n] for n in TernaryWeights.NAMES})
            attention(nc, sh, "a3", "decay", wt, obuf, masks=masks, ternary=ternary)
            quantised_ffn(nc, sh, ternary)
        store_out(nc, sh, out)


_TURNED = ["L0_attn_Wr", "L0_attn_Ww", "L0_attn_Wk", "L0_attn_Wv", "L0_attn_Wo", "L0_attn_Wkey", "L0_attn_Wval",
           "L0_attn_Wrec", "L0_ffn_gate_w", "L1_attn_c_attn_w", "L1_attn_q2l_w", "L1_attn_kv2l_w", "L1_attn_l2o_w",
           "L1_attn_wqk_w", "L1_attn_cproj_w", "L2_attn_Wq", "L2_attn_Wk", "L2_attn_Wv", "L2_attn_Wo", "L2_ffn_w_g",
           "L3_attn_Wq", "L3_attn_Wk", "L3_attn_Wv", "L3_attn_Wo", "L3_ffn_w_gate", "L3_ffn_w_up", "L3_ffn_w_down"]
_AS_IS = ["x", "L0_tok_weight", "L0_attn_ln1_g", "L0_attn_ln1_b", "L0_attn_ln2_g", "L0_attn_ln2_b",
          "L0_attn_time_decay", "L0_ffn_expert_bias", "L1_attn_c_attn_b", "L1_attn_q2l_b", "L1_attn_kv2l_b",
          "L1_attn_l2o_b", "L1_attn_wqk_b", "L1_attn_cproj_b", "L1_ffn_router_w", "L1_ffn_b_out",
          "L2_attn_bq", "L2_attn_bk", "L2_attn_bv", "L2_attn_bo", "L2_attn_idx_k", "L3_attn_bq", "L3_attn_bk",
          "L3_attn_bv", "L3_attn_bo", "L3_attn_decay_params", "L3_attn_mix_weights"]


def _chunked(*mats):
    parts = [m.reshape(m.shape[0], -1, 128, m.shape[2]).transpose(0, 2, 1, 3).reshape(m.shape[0], 128, -1)
             for m in mats]
    return np.ascontiguousarray(np.concatenate(parts, axis=2))


def kernel(**inputs):
    import concourse.bacc as bacc
    from concourse.bass_utils import run_bass_kernel_spmd as run

    nc = bacc.Bacc("TRN2", target_bir_lowering=False, num_devices=1)
    a = {n: np.asarray(v) for n, v in inputs.items()}
    turned = lambda m: np.swapaxes(m, -1, -2)
    arrays = {}
    for name in _AS_IS:
        arrays[name] = np.ascontiguousarray(a[name])
    for name in _TURNED:
        arrays[name] = np.ascontiguousarray(turned(a[name]))
    arrays["L0_ffn_experts"] = _chunked(*(turned(np.concatenate([a[f"L0_ffn_w{m}"], a[f"L0_ffn_sw{m}"][None]]))
                                          for m in (1, 3, 2)))
    b_in = a["L1_ffn_b_in"].reshape(E, DC, P).transpose(0, 2, 1)
    arrays["L1_ffn_experts"] = np.ascontiguousarray(np.concatenate(
        [_chunked(a["L1_ffn_w_in"]), b_in, _chunked(a["L1_ffn_w_out"])], axis=2))
    arrays["L2_ffn_c_fc"] = _chunked(a["L2_ffn_c_fc"])
    arrays["L2_ffn_c_proj"] = _chunked(a["L2_ffn_c_proj"])
    pair = np.arange(P) % LAT // 2
    angle = (np.arange(S, dtype=np.float32)[None, :]
             * (1.0 / 10000.0 ** (2.0 * pair / LAT)).astype(np.float32)[:, None]).astype(np.float32)
    arrays["L1_attn_cos"] = np.cos(angle).astype(np.float32)
    arrays["L1_attn_sin"] = np.sin(angle).astype(np.float32)
    swap = np.zeros((P, P), np.float32)
    even = np.arange(0, P, 2)
    swap[even + 1, even], swap[even, even + 1] = -1.0, 1.0
    arrays["L1_attn_rot"] = swap
    odd = (np.arange(P) // HD % 2).astype(bool)
    arrays["parity"] = np.where(np.stack([~odd, odd], axis=1), np.float32(HD ** -0.5), np.float32(0.0))
    handles = {n: nc.dram_tensor(n, v.shape, mybir.dt.from_np(v.dtype), kind="ExternalInput").ap()
               for n, v in arrays.items()}
    out = nc.dram_tensor("out", (B, S, D), F32, kind="ExternalOutput").ap()
    tower(nc, handles, out)
    result = run(nc, [arrays], core_ids=[0])
    return result.results[0]["out"]
```
